# Optimizing a Trainium2 kernel written in Bass

```python
import numpy as np
import jax
import jax.numpy as jnp

def _softmax(x, axis=-1):
    return jax.nn.softmax(x, axis=axis)

def _gelu(x):
    return jax.nn.gelu(x, approximate=True)

def _silu(x):
    return jax.nn.silu(x)

def _sigmoid(x):
    return jax.nn.sigmoid(x)

def _layernorm(x, axis=-1, eps=1e-05):
    m = jnp.mean(x, axis=axis, keepdims=True)
    v = jnp.var(x, axis=axis, keepdims=True)
    return (x - m) / jnp.sqrt(v + eps)

def _scatter_add(tgt, idx, src, axis=0):
    return tgt.at[idx].add(src)

def _segment_sum(src, seg, n):
    return jax.ops.segment_sum(src, seg, n)
kernel_name = 'mk_vit_tower_postln_d2_tok_img768_r4_7cf451'

def setup_inputs(seed: int=0):
    np.random.seed(seed)
    _w = jnp.asarray

    def _rec_inputs():
        import jax
        import jax.numpy as jnp
        _rk = jax.random.key(seed)
        x = -0.00016672 + 0.999947 * jax.random.normal(jax.random.fold_in(_rk, 1), (64, 3, 112, 112), jnp.float32)
        return x
    x = _rec_inputs()

    def _L0_tok_setup():
        import math
        import jax, jax.numpy as jnp
        import numpy as np
        IMG = (96, 96)
        PATCH = (16, 16)
        CH = 3
        LEN = 192
        B = 64
        NPATCH = IMG[0] // PATCH[0] * (IMG[1] // PATCH[1])

        def _pos_encoding(n_patch, length, dtype):
            i = jnp.arange(n_patch, dtype=dtype)[:, None]
            j = jnp.arange(length)
            expo = (2 * (j // 2)).astype(dtype) / length
            angle = i / jnp.power(jnp.asarray(10000.0, dtype), expo)
            angle = angle + jnp.where(j % 2 == 1, jnp.asarray(math.pi / 2, dtype), 0.0)
            return jnp.sin(angle)
        key = jax.random.key(seed)
        k1, k2, k3 = jax.random.split(key, 3)
        x = jax.random.normal(k1, (B, CH, IMG[0], IMG[1]), dtype=jnp.float32)
        fan_in = CH * PATCH[0] * PATCH[1]
        std = math.sqrt(2.0 / fan_in)
        W = jax.random.normal(k2, (LEN, CH, PATCH[0], PATCH[1]), dtype=jnp.float32) * std
        b = jax.random.normal(k3, (LEN,), dtype=jnp.float32) * 0.01
        return {'x': x, 'W': W, 'b': b}
    _L0_tok_all = _L0_tok_setup()
    _L0_tok_in = {k: v for k, v in _L0_tok_all.items() if k in ('W', 'b')}
    del _L0_tok_all

    def _L0_attn_setup():
        import jax, jax.numpy as jnp
        import numpy as np
        B, T, C = (4, 512, 192)
        H, D = (12, 64)
        R = 64
        ROPE_THETA = 10000.0

        def _rope_cos_sin(t, d, dtype):
            inv_freq = 1.0 / ROPE_THETA ** (jnp.arange(0, d, 2, dtype=jnp.float32) / d)
            ang = jnp.arange(t, dtype=jnp.float32)[:, None] * inv_freq[None, :]
            ang = jnp.concatenate([ang, ang], axis=-1)
            return (jnp.cos(ang).astype(dtype), jnp.sin(ang).astype(dtype))

        def _apply_rope(q, cos, sin):
            d2 = q.shape[-1] // 2
            rot = jnp.concatenate([-q[..., d2:], q[..., :d2]], axis=-1)
            return q * cos + rot * sin
        key = jax.random.key(seed)
        ks = jax.random.split(key, 8)
        s = lambda fan_in: 1.0 / np.sqrt(fan_in)
        return {'x': jax.random.normal(ks[0], (B, T, C), jnp.float32), 'Wq': jax.random.normal(ks[1], (C, H * D), jnp.float32) * s(C), 'Wdown': jax.random.normal(ks[2], (C, R), jnp.float32) * s(C), 'ln_g': jnp.ones((R,), jnp.float32), 'ln_b': jnp.zeros((R,), jnp.float32), 'Wup': jax.random.normal(ks[3], (R, 2 * H * D), jnp.float32) * s(R), 'Wo': jax.random.normal(ks[4], (H * D, C), jnp.float32) * s(H * D), 'bo': jnp.zeros((C,), jnp.float32)}
    _L0_attn_all = _L0_attn_setup()
    _L0_attn_in = {k: v for k, v in _L0_attn_all.items() if k in ('Wq', 'Wdown', 'ln_g', 'ln_b', 'Wup', 'Wo', 'bo')}
    del _L0_attn_all

    def _L0_ffn_setup():
        import jax, jax.numpy as jnp
        import numpy as np
        E = 128
        I = 464
        IS = 928
        K = 6
        G = 1
        TG = 1
        SCALE = 2.5
        CAP = 192

        def moe_forward(hidden_states, Wg, e_bias, W_gate_up, W_down, Wsg, Wsu, Wsd):
            B, S, H = hidden_states.shape
            x = hidden_states.reshape(-1, H)
            T = x.shape[0]
            logits = x.astype(jnp.float32) @ Wg.T
            sig = jax.nn.sigmoid(logits)
            choice = sig + e_bias[None, :]
            grp = choice.reshape(T, G, E // G)
            group_scores = jax.lax.top_k(grp, 2)[0].sum(-1)
            gidx = jax.lax.top_k(group_scores, TG)[1]
            gmask = jnp.zeros((T, G), jnp.float32).at[jnp.arange(T)[:, None], gidx].set(1.0)
            smask = jnp.repeat(gmask, E // G, axis=1)
            scores_for_choice = jnp.where(smask > 0, choice, 0.0)
            topk_idx = jax.lax.top_k(scores_for_choice, K)[1]
            topk_w = jnp.take_along_axis(sig, topk_idx, axis=1)
            topk_w = topk_w / (topk_w.sum(-1, keepdims=True) + 1e-20)
            topk_w = topk_w * SCALE
            P = T * K
            flat_e = topk_idx.reshape(-1)
            order = jnp.argsort(flat_e)
            se = flat_e[order]
            counts = jax.ops.segment_sum(jnp.ones(P, jnp.int32), flat_e, num_segments=E)
            starts = jnp.cumsum(counts) - counts
            pos = jnp.arange(P) - starts[se]
            buf_idx = jnp.where(pos < CAP, se * CAP + pos, E * CAP)
            tok_of_pair = (order // K).astype(jnp.int32)
            w_of_pair = topk_w.reshape(-1)[order]
            token_buf = jnp.zeros((E * CAP,), jnp.int32).at[buf_idx].set(tok_of_pair, mode='drop')
            w_buf = jnp.zeros((E * CAP,), x.dtype).at[buf_idx].set(w_of_pair.astype(x.dtype), mode='drop')
            xb = x[token_buf].reshape(E, CAP, H)
            gu = jnp.einsum('ech,ehf->ecf', xb, W_gate_up)
            g, u = jnp.split(gu, 2, axis=-1)
            inter = jax.nn.silu(g) * u
            yb = jnp.einsum('eci,eih->ech', inter, W_down)
            yb = yb * w_buf.reshape(E, CAP, 1)
            routed = jnp.zeros((T, H), x.dtype).at[token_buf].add(yb.reshape(E * CAP, H))
            shared = jax.nn.silu(x @ Wsg) * (x @ Wsu) @ Wsd
            return (routed + shared).reshape(B, S, H)
        key = jax.random.key(seed)
        ks = jax.random.split(key, 8)
        B, S, H = (1, 512, 192)
        sc = 0.02
        return {'hidden_states': jax.random.normal(ks[0], (B, S, H), jnp.float32), 'Wg': jax.random.normal(ks[1], (E, H), jnp.float32) * sc, 'e_bias': jnp.zeros((E,), jnp.float32), 'W_gate_up': jax.random.normal(ks[2], (E, H, 2 * I), jnp.float32) * sc, 'W_down': jax.random.normal(ks[3], (E, I, H), jnp.float32) * sc, 'Wsg': jax.random.normal(ks[4], (H, IS), jnp.float32) * sc, 'Wsu': jax.random.normal(ks[5], (H, IS), jnp.float32) * sc, 'Wsd': jax.random.normal(ks[6], (IS, H), jnp.float32) * sc}
    _L0_ffn_all = _L0_ffn_setup()
    _L0_ffn_in = {k: v for k, v in _L0_ffn_all.items() if k in ('Wg', 'e_bias', 'W_gate_up', 'W_down', 'Wsg', 'Wsu', 'Wsd')}
    del _L0_ffn_all

    def _L1_attn_setup():
        import jax, jax.numpy as jnp
        import numpy as np
        H = 12
        BETA = 0.5
        LN_EPS = 1e-12

        def layer_norm(x, g, b):
            mu = x.mean(-1, keepdims=True)
            var = ((x - mu) ** 2).mean(-1, keepdims=True)
            return (x - mu) * jax.lax.rsqrt(var + LN_EPS) * g + b
        key = jax.random.key(seed)
        B, S, D, F, L = (16, 128, 192, 768, 4)
        ks = jax.random.split(key, 9)
        w = lambda k, shape: jax.random.normal(k, shape, jnp.float32) * 0.02
        return {'hidden_states': jax.random.normal(ks[0], (B, S, D), jnp.float32), 'Wq': w(ks[1], (L, D, D)), 'bq': jnp.zeros((L, D), jnp.float32), 'Wk': w(ks[2], (L, D, D)), 'bk': jnp.zeros((L, D), jnp.float32), 'Wv': w(ks[3], (L, D, D)), 'bv': jnp.zeros((L, D), jnp.float32), 'Wc': w(ks[4], (L, D, D)), 'bc': jnp.zeros((L, D), jnp.float32), 'Wo': w(ks[5], (L, D, D)), 'bo': jnp.zeros((L, D), jnp.float32), 'g1': jnp.ones((L, D), jnp.float32), 'b1': jnp.zeros((L, D), jnp.float32), 'Wi': w(ks[6], (L, D, F)), 'bi': jnp.zeros((L, F), jnp.float32), 'Wo2': w(ks[7], (L, F, D)), 'bo2': jnp.zeros((L, D), jnp.float32), 'g2': jnp.ones((L, D), jnp.float32), 'b2': jnp.zeros((L, D), jnp.float32)}
    _L1_attn_all = _L1_attn_setup()
    _L1_attn_in = {k: v for k, v in _L1_attn_all.items() if k in ('Wq', 'bq', 'Wk', 'bk', 'Wv', 'bv', 'Wc', 'bc', 'Wo', 'bo', 'g1', 'b1', 'Wi', 'bi', 'Wo2', 'bo2', 'g2', 'b2')}
    del _L1_attn_all

    def _L1_ffn_setup():
        import jax, jax.numpy as jnp
        import numpy as np
        TOP_K = 2

        def _moe(x, Wg, bg, W1, b1, W2, b2):
            B, S, D = x.shape
            E = Wg.shape[1]
            logits = x @ Wg + bg
            top_vals, top_idx = jax.lax.top_k(logits, TOP_K)
            gates_k = jax.nn.softmax(top_vals, axis=-1)
            one_hot = jax.nn.one_hot(top_idx, E, dtype=x.dtype)
            gates = jnp.sum(one_hot * gates_k[..., None], axis=-2)
            flat_x = x.reshape(-1, D)
            flat_g = gates.reshape(-1, E).T

            def body(acc, p):
                W1e, b1e, W2e, b2e, ge = p
                h = jax.nn.relu(flat_x @ W1e + b1e)
                acc = acc + (h @ W2e + b2e) * ge[:, None]
                return (acc, None)
            out, _ = jax.lax.scan(body, jnp.zeros_like(flat_x), (W1, b1, W2, b2, flat_g))
            return out.reshape(B, S, D)
        key = jax.random.key(seed)
        k = jax.random.split(key, 5)
        B, S, D, E, H = (8, 512, 192, 8, 768)
        init = lambda kk, shape: jax.random.normal(kk, shape, jnp.float32) * 0.02
        return {'x': jax.random.normal(k[0], (B, S, D), jnp.float32), 'Wg': init(k[1], (D, E)), 'bg': jnp.zeros((E,), jnp.float32), 'W1': init(k[2], (E, D, H)), 'b1': jnp.zeros((E, H), jnp.float32), 'W2': init(k[3], (E, H, D)), 'b2': jnp.zeros((E, D), jnp.float32)}
    _L1_ffn_all = _L1_ffn_setup()
    _L1_ffn_in = {k: v for k, v in _L1_ffn_all.items() if k in ('Wg', 'bg', 'W1', 'b1', 'W2', 'b2')}
    del _L1_ffn_all
    return {'x': x, 'L0_tok_W': _L0_tok_in['W'], 'L0_tok_b': _L0_tok_in['b'], 'L0_attn_Wq': _L0_attn_in['Wq'], 'L0_attn_Wdown': _L0_attn_in['Wdown'], 'L0_attn_ln_g': _L0_attn_in['ln_g'], 'L0_attn_ln_b': _L0_attn_in['ln_b'], 'L0_attn_Wup': _L0_attn_in['Wup'], 'L0_attn_Wo': _L0_attn_in['Wo'], 'L0_attn_bo': _L0_attn_in['bo'], 'L0_ffn_Wg': _L0_ffn_in['Wg'], 'L0_ffn_e_bias': _L0_ffn_in['e_bias'], 'L0_ffn_W_gate_up': _L0_ffn_in['W_gate_up'], 'L0_ffn_W_down': _L0_ffn_in['W_down'], 'L0_ffn_Wsg': _L0_ffn_in['Wsg'], 'L0_ffn_Wsu': _L0_ffn_in['Wsu'], 'L0_ffn_Wsd': _L0_ffn_in['Wsd'], 'L1_attn_Wq': _L1_attn_in['Wq'], 'L1_attn_bq': _L1_attn_in['bq'], 'L1_attn_Wk': _L1_attn_in['Wk'], 'L1_attn_bk': _L1_attn_in['bk'], 'L1_attn_Wv': _L1_attn_in['Wv'], 'L1_attn_bv': _L1_attn_in['bv'], 'L1_attn_Wc': _L1_attn_in['Wc'], 'L1_attn_bc': _L1_attn_in['bc'], 'L1_attn_Wo': _L1_attn_in['Wo'], 'L1_attn_bo': _L1_attn_in['bo'], 'L1_attn_g1': _L1_attn_in['g1'], 'L1_attn_b1': _L1_attn_in['b1'], 'L1_attn_Wi': _L1_attn_in['Wi'], 'L1_attn_bi': _L1_attn_in['bi'], 'L1_attn_Wo2': _L1_attn_in['Wo2'], 'L1_attn_bo2': _L1_attn_in['bo2'], 'L1_attn_g2': _L1_attn_in['g2'], 'L1_attn_b2': _L1_attn_in['b2'], 'L1_ffn_Wg': _L1_ffn_in['Wg'], 'L1_ffn_bg': _L1_ffn_in['bg'], 'L1_ffn_W1': _L1_ffn_in['W1'], 'L1_ffn_b1': _L1_ffn_in['b1'], 'L1_ffn_W2': _L1_ffn_in['W2'], 'L1_ffn_b2': _L1_ffn_in['b2']}

def reference(x, L0_tok_W, L0_tok_b, L0_attn_Wq, L0_attn_Wdown, L0_attn_ln_g, L0_attn_ln_b, L0_attn_Wup, L0_attn_Wo, L0_attn_bo, L0_ffn_Wg, L0_ffn_e_bias, L0_ffn_W_gate_up, L0_ffn_W_down, L0_ffn_Wsg, L0_ffn_Wsu, L0_ffn_Wsd, L1_attn_Wq, L1_attn_bq, L1_attn_Wk, L1_attn_bk, L1_attn_Wv, L1_attn_bv, L1_attn_Wc, L1_attn_bc, L1_attn_Wo, L1_attn_bo, L1_attn_g1, L1_attn_b1, L1_attn_Wi, L1_attn_bi, L1_attn_Wo2, L1_attn_bo2, L1_attn_g2, L1_attn_b2, L1_ffn_Wg, L1_ffn_bg, L1_ffn_W1, L1_ffn_b1, L1_ffn_W2, L1_ffn_b2):
    import jax
    import jax.numpy as jnp

    def _L0_tok_ref(x, W, b):
        import math
        import jax, jax.numpy as jnp
        import numpy as np
        IMG = (96, 96)
        PATCH = (16, 16)
        CH = 3
        LEN = 192
        B = 64
        NPATCH = IMG[0] // PATCH[0] * (IMG[1] // PATCH[1])

        def _pos_encoding(n_patch, length, dtype):
            i = jnp.arange(n_patch, dtype=dtype)[:, None]
            j = jnp.arange(length)
            expo = (2 * (j // 2)).astype(dtype) / length
            angle = i / jnp.power(jnp.asarray(10000.0, dtype), expo)
            angle = angle + jnp.where(j % 2 == 1, jnp.asarray(math.pi / 2, dtype), 0.0)
            return jnp.sin(angle)
        y = jax.lax.conv_general_dilated(x, W, window_strides=PATCH, padding='VALID', dimension_numbers=('NCHW', 'OIHW', 'NCHW'))
        y = y + b[None, :, None, None]
        Bn, L, Hp, Wp = y.shape
        y = y.reshape(Bn, L, Hp * Wp).transpose(0, 2, 1)
        pos = _pos_encoding(Hp * Wp, L, y.dtype)
        return y + pos[None, :, :]

    def _L0_attn_ref(x, Wq, Wdown, ln_g, ln_b, Wup, Wo, bo):
        import jax, jax.numpy as jnp
        import numpy as np
        B, T, C = (4, 512, 192)
        H, D = (12, 64)
        R = 64
        ROPE_THETA = 10000.0

        def _rope_cos_sin(t, d, dtype):
            inv_freq = 1.0 / ROPE_THETA ** (jnp.arange(0, d, 2, dtype=jnp.float32) / d)
            ang = jnp.arange(t, dtype=jnp.float32)[:, None] * inv_freq[None, :]
            ang = jnp.concatenate([ang, ang], axis=-1)
            return (jnp.cos(ang).astype(dtype), jnp.sin(ang).astype(dtype))

        def _apply_rope(q, cos, sin):
            d2 = q.shape[-1] // 2
            rot = jnp.concatenate([-q[..., d2:], q[..., :d2]], axis=-1)
            return q * cos + rot * sin
        b, t, c = x.shape
        q = (x @ Wq).reshape(b, t, H, D).transpose(0, 2, 1, 3)
        ckv = x @ Wdown
        mu = jnp.mean(ckv, axis=-1, keepdims=True)
        var = jnp.var(ckv, axis=-1, keepdims=True)
        ckv = (ckv - mu) * jax.lax.rsqrt(var + 1e-05) * ln_g + ln_b
        kv = (ckv @ Wup).reshape(b, t, 2, H, D)
        k = kv[:, :, 0].transpose(0, 2, 1, 3)
        v = kv[:, :, 1].transpose(0, 2, 1, 3)
        cos, sin = _rope_cos_sin(t, D, x.dtype)
        q = _apply_rope(q, cos, sin)
        k = _apply_rope(k, cos, sin)
        wei = jnp.einsum('bhqd,bhkd->bhqk', q, k) * D ** (-0.5)
        causal = jnp.tril(jnp.ones((t, t), bool))
        wei = jnp.where(causal, wei, -jnp.inf)
        wei = jax.nn.softmax(wei, axis=-1)
        out = jnp.einsum('bhqk,bhkd->bhqd', wei, v)
        out = out.transpose(0, 2, 1, 3).reshape(b, t, H * D)
        return out @ Wo + bo

    def _L0_ffn_ref(hidden_states, Wg, e_bias, W_gate_up, W_down, Wsg, Wsu, Wsd):
        import jax, jax.numpy as jnp
        import numpy as np
        E = 128
        I = 464
        IS = 928
        K = 6
        G = 1
        TG = 1
        SCALE = 2.5
        CAP = 192

        def moe_forward(hidden_states, Wg, e_bias, W_gate_up, W_down, Wsg, Wsu, Wsd):
            B, S, H = hidden_states.shape
            x = hidden_states.reshape(-1, H)
            T = x.shape[0]
            logits = x.astype(jnp.float32) @ Wg.T
            sig = jax.nn.sigmoid(logits)
            choice = sig + e_bias[None, :]
            grp = choice.reshape(T, G, E // G)
            group_scores = jax.lax.top_k(grp, 2)[0].sum(-1)
            gidx = jax.lax.top_k(group_scores, TG)[1]
            gmask = jnp.zeros((T, G), jnp.float32).at[jnp.arange(T)[:, None], gidx].set(1.0)
            smask = jnp.repeat(gmask, E // G, axis=1)
            scores_for_choice = jnp.where(smask > 0, choice, 0.0)
            topk_idx = jax.lax.top_k(scores_for_choice, K)[1]
            topk_w = jnp.take_along_axis(sig, topk_idx, axis=1)
            topk_w = topk_w / (topk_w.sum(-1, keepdims=True) + 1e-20)
            topk_w = topk_w * SCALE
            P = T * K
            flat_e = topk_idx.reshape(-1)
            order = jnp.argsort(flat_e)
            se = flat_e[order]
            counts = jax.ops.segment_sum(jnp.ones(P, jnp.int32), flat_e, num_segments=E)
            starts = jnp.cumsum(counts) - counts
            pos = jnp.arange(P) - starts[se]
            buf_idx = jnp.where(pos < CAP, se * CAP + pos, E * CAP)
            tok_of_pair = (order // K).astype(jnp.int32)
            w_of_pair = topk_w.reshape(-1)[order]
            token_buf = jnp.zeros((E * CAP,), jnp.int32).at[buf_idx].set(tok_of_pair, mode='drop')
            w_buf = jnp.zeros((E * CAP,), x.dtype).at[buf_idx].set(w_of_pair.astype(x.dtype), mode='drop')
            xb = x[token_buf].reshape(E, CAP, H)
            gu = jnp.einsum('ech,ehf->ecf', xb, W_gate_up)
            g, u = jnp.split(gu, 2, axis=-1)
            inter = jax.nn.silu(g) * u
            yb = jnp.einsum('eci,eih->ech', inter, W_down)
            yb = yb * w_buf.reshape(E, CAP, 1)
            routed = jnp.zeros((T, H), x.dtype).at[token_buf].add(yb.reshape(E * CAP, H))
            shared = jax.nn.silu(x @ Wsg) * (x @ Wsu) @ Wsd
            return (routed + shared).reshape(B, S, H)
        return moe_forward(hidden_states, Wg, e_bias, W_gate_up, W_down, Wsg, Wsu, Wsd)

    def _L1_attn_ref(hidden_states, Wq, bq, Wk, bk, Wv, bv, Wc, bc, Wo, bo, g1, b1, Wi, bi, Wo2, bo2, g2, b2):
        import jax, jax.numpy as jnp
        import numpy as np
        H = 12
        BETA = 0.5
        LN_EPS = 1e-12

        def layer_norm(x, g, b):
            mu = x.mean(-1, keepdims=True)
            var = ((x - mu) ** 2).mean(-1, keepdims=True)
            return (x - mu) * jax.lax.rsqrt(var + LN_EPS) * g + b
        B, S, D = hidden_states.shape
        Dh = D // H
        L = Wq.shape[0]
        eye = jnp.eye(S, dtype=hidden_states.dtype)
        scale = 1.0 / np.sqrt(Dh).astype(np.float32)

        def heads(t):
            return t.reshape(B, S, H, Dh).transpose(0, 2, 1, 3)
        x = hidden_states
        for i in range(L):
            q = heads(x @ Wq[i] + bq[i])
            k = heads(x @ Wk[i] + bk[i])
            v = heads(x @ Wv[i] + bv[i])
            c = heads(x @ Wc[i] + bc[i])
            cn = jnp.linalg.norm(c, axis=-1, keepdims=True)
            denom = cn * jnp.swapaxes(cn, -1, -2)
            s1 = 1.0 - jnp.einsum('bhld,bhrd->bhlr', c, c) / denom + eye
            p1 = jax.nn.softmax(s1, axis=-1)
            s2 = jnp.einsum('bhld,bhrd->bhlr', q, k) * scale
            p2 = jax.nn.softmax(s2, axis=-1)
            p = BETA * p1 + (1.0 - BETA) * p2
            ctx = jnp.einsum('bhlr,bhrd->bhld', p, v)
            ctx = ctx.transpose(0, 2, 1, 3).reshape(B, S, D)
            attn_out = layer_norm(ctx @ Wo[i] + bo[i] + x, g1[i], b1[i])
            h = jax.nn.gelu(attn_out @ Wi[i] + bi[i], approximate=False)
            x = layer_norm(h @ Wo2[i] + bo2[i] + attn_out, g2[i], b2[i])
        return x

    def _L1_ffn_ref(x, Wg, bg, W1, b1, W2, b2):
        import jax, jax.numpy as jnp
        import numpy as np
        TOP_K = 2

        def _moe(x, Wg, bg, W1, b1, W2, b2):
            B, S, D = x.shape
            E = Wg.shape[1]
            logits = x @ Wg + bg
            top_vals, top_idx = jax.lax.top_k(logits, TOP_K)
            gates_k = jax.nn.softmax(top_vals, axis=-1)
            one_hot = jax.nn.one_hot(top_idx, E, dtype=x.dtype)
            gates = jnp.sum(one_hot * gates_k[..., None], axis=-2)
            flat_x = x.reshape(-1, D)
            flat_g = gates.reshape(-1, E).T

            def body(acc, p):
                W1e, b1e, W2e, b2e, ge = p
                h = jax.nn.relu(flat_x @ W1e + b1e)
                acc = acc + (h @ W2e + b2e) * ge[:, None]
                return (acc, None)
            out, _ = jax.lax.scan(body, jnp.zeros_like(flat_x), (W1, b1, W2, b2, flat_g))
            return out.reshape(B, S, D)
        return _moe(x, Wg, bg, W1, b1, W2, b2)
    h = _L0_tok_ref(x, L0_tok_W, L0_tok_b)
    h = _layernorm(h + _L0_attn_ref(h, L0_attn_Wq, L0_attn_Wdown, L0_attn_ln_g, L0_attn_ln_b, L0_attn_Wup, L0_attn_Wo, L0_attn_bo), axis=-1)
    h = _layernorm(h + _L0_ffn_ref(h, L0_ffn_Wg, L0_ffn_e_bias, L0_ffn_W_gate_up, L0_ffn_W_down, L0_ffn_Wsg, L0_ffn_Wsu, L0_ffn_Wsd), axis=-1)
    h = _layernorm(h + _L1_attn_ref(h, L1_attn_Wq, L1_attn_bq, L1_attn_Wk, L1_attn_bk, L1_attn_Wv, L1_attn_bv, L1_attn_Wc, L1_attn_bc, L1_attn_Wo, L1_attn_bo, L1_attn_g1, L1_attn_b1, L1_attn_Wi, L1_attn_bi, L1_attn_Wo2, L1_attn_bo2, L1_attn_g2, L1_attn_b2), axis=-1)
    h = _layernorm(h + _L1_ffn_ref(h, L1_ffn_Wg, L1_ffn_bg, L1_ffn_W1, L1_ffn_b1, L1_ffn_W2, L1_ffn_b2), axis=-1)
    return h

_drawn_inputs = setup_inputs


def setup_inputs(seed=0):
    import zlib

    import numpy as np

    out = dict(_drawn_inputs(seed))
    spreads = {'L0_attn_ln_g': (1.0, 0.2),
     'L0_attn_ln_b': (0.0, 0.1),
     'L0_attn_bo': (0.0, 0.1),
     'L0_ffn_e_bias': (0.0, 0.393),
     'L1_attn_bq': (0.0, 2.0),
     'L1_attn_bk': (0.0, 2.0),
     'L1_attn_bv': (0.0, 0.1),
     'L1_attn_bc': (0.0, 2.0),
     'L1_attn_bo': (0.0, 0.1),
     'L1_attn_g1': (1.0, 0.2),
     'L1_attn_b1': (0.0, 0.1),
     'L1_attn_bi': (0.0, 0.1),
     'L1_attn_bo2': (0.0, 0.1),
     'L1_attn_g2': (1.0, 0.2),
     'L1_attn_b2': (0.0, 0.1),
     'L1_ffn_bg': (0.0, 0.1),
     'L1_ffn_b1': (0.0, 0.3),
     'L1_ffn_b2': (0.0, 0.1)}
    factors = {'L0_tok_b': 5.346,
     'L0_ffn_Wg': 5.114,
     'L0_ffn_W_gate_up': 4.894,
     'L0_ffn_W_down': 4.678,
     'L1_attn_Wq': 8.0,
     'L1_attn_Wk': 8.0,
     'L1_attn_Wc': 64.0}
    for name, (base, spread) in spreads.items():
        noise = np.random.default_rng([zlib.crc32(name.encode()), seed]).standard_normal(out[name].shape)
        drawn = base * np.exp(spread * noise) if base else spread * noise
        out[name] = jnp.asarray(drawn.astype(out[name].dtype))
    for name, factor in factors.items():
        out[name] = (out[name] * factor).astype(out[name].dtype)
    return out
```

```python
from contextlib import ExitStack

import numpy as np
import concourse.bass as bass
from concourse import mybir

F32 = mybir.dt.float32
I32 = mybir.dt.uint32
ALU = mybir.AluOpType
ACT = mybir.ActivationFunctionType
AX = mybir.AxisListType

IMAGES, PATCHES, WIDTH = 64, 49, 192
TOKENS = IMAGES * PATCHES
PAIR = 2 * PATCHES
TURNS = IMAGES // 2
HALF = WIDTH // 2
GROUP = 4
GROUPS = TURNS // GROUP
GCOLS = GROUP * PAIR
SLOT = 64
PADDED = SLOT + PATCHES
HEADS = 12
NI = HEADS // 2
HD0 = 64
EXPERTS, TOPK, CAP, INTER = 128, 6, 192, 464
FC = 116
NF = INTER // FC
SHARED = 928
CAPH = CAP // 2
ROWS = CAPH * 2 * EXPERTS
LAYERS, FFN, NFF = 4, 768, 6
BIG = 1.0e30


def signals(ctx, nc, tag, names, dma="", setup=""):
    found = {n: nc.alloc_semaphore(f"{tag}_{n}") for n in f"{names} {dma} {setup}".split()}
    for n in names.split():
        nc.gpsimd.sem_inc(found[n], 1)
    for n in dma.split():
        nc.gpsimd.sem_inc(found[n], 16)
    nc.all_engine_barrier()
    ctx.callback(nc.all_engine_barrier)
    ctx.callback(nc.clear_and_free_semaphores, list(found.values()))
    return dict(**found)


def buffers(ctx, nc, tag, **shapes):
    return dict(**{n: ctx.enter_context(nc.sbuf_tensor(f"{tag}_{n}", list(s), F32)) for n, s in shapes.items()})


def banks(ctx, nc, tag, **widths):
    return dict(**{n: ctx.enter_context(nc.psum_tensor(f"{tag}_{n}", [128, w], F32)) for n, w in widths.items()})


def heads_of(ap):
    return ap.rearrange("p (a c) -> p a c", a=2)[:, :, 0:NI * PATCHES].rearrange("p a (i r) -> p a i r", i=NI)


def packed(ap):
    return ap.rearrange("p j (m r) -> p j m r", m=2)


def slots(ap, j):
    return ap.rearrange("p (j m q) -> p j m q", j=j, m=2)[:, :, :, 0:PATCHES]


def block_embed_and_latent_attention(nc, d, keep):
    with ExitStack() as ctx:
        b = buffers(
            ctx, nc, "la", xp=(128, 6, PAIR), wtok=(128, 6, WIDTH), posb=(PAIR, WIDTH), tokb=(PAIR, WIDTH), bo=(PAIR, WIDTH),
            wdown=(HALF, 2, 64), wq=(HALF, 2, 768), wqr=(HALF, 2, 768), wk=(64, 768), wkr=(64, 768), wv=(64, 768),
            wo=(128, 6, WIDTH), lng=(64, 1), lnb=(64, 1), cos=(128, PAIR), sin=(128, PAIR), mask=(128, PATCHES),
            hs=(PAIR, WIDTH), hb=(PAIR, WIDTH), hT=(HALF, 2, PAIR), st=(PAIR, 6), mv=(PAIR, 2), ve=(PAIR, 1), rstd=(PAIR, 1),
            ckn=(PAIR, 64), ckT=(64, PADDED + 15), r1=(128, 6, PAIR), r2=(128, 6, PAIR), qT=(128, 6, 128), kT=(128, 6, PAIR),
            V=(128, 2, NI, HD0), E=(128, 2, NI, PATCHES), mx=(128, 2, NI), P=(128, NI, 2, SLOT), z=(128, 2, NI), rz=(128, 2, NI),
            PT=(128, 2, NI, SLOT), C=(128, NI, 2, HD0), CT=(128, 6, PAIR), y=(PAIR, WIDTH), st2=(PAIR, 6), mv2=(PAIR, 2),
            ve2=(PAIR, 1), rstd2=(PAIR, 1), xn=(PAIR, WIDTH))
        p = banks(ctx, nc, "la", p0=512, p1=512, p23=1024, p45=1024, p67=1024)
        s = signals(
            ctx, nc, "la", "conv h hb hT_ps hT ckv q_ps st mv ve rstd ckn ck_ps ckT rq1 rq2 qT k_ps v_ps "
            "V rk1 rk2 kT s_ps masked mx shifted P z rz pt_ps PT0 PT1 ctx_ps C0 C1 ct_ps CT0 CT1 wo_ps y st2 mv2 ve2 rstd2 xn "
            "x_ps xT X", dma="xp stored", setup="imm weights ready_pos pads")
        loads = [(b["wtok"], d["wtok"]), (b["posb"], d["pos"]), (b["tokb"], d["tok_b"]), (b["bo"], d["bo0"]), (b["wdown"], d["wdown"]), (b["wq"], d["wq0"]),
                 (b["wqr"], d["wq0r"]), (b["wk"], d["wk0"]), (b["wkr"], d["wk0r"]), (b["wv"], d["wv0"]), (b["wo"], d["wo0"]), (b["lng"], d["ln_g"]), (b["lnb"], d["ln_b"]),
                 (b["cos"], d["cos"]), (b["sin"], d["sin"]), (b["mask"], d["mask"]), (keep["ident"], d["ident"]), (keep["half"], d["half"])]
        block = ctx.enter_context(nc.Block())

        @block.sync
        def _(sp):
            for to, src in loads:
                sp.dma_start(to[:], src).then_inc(s["weights"], 16)
            sp.dma_start(b["xp"][:], d["xp"][0]).then_inc(s["xp"], 16)
            with sp.Fori(2, TURNS + 1) as n:
                t = n - 2
                sp.wait_ge(s["imm"], 1)
                sp.wait_ge(s["conv"], n)
                sp.dma_start(b["xp"][:], d["xp"][t + 1]).then_inc(s["xp"], 16)
                sp.wait_ge(s["xn"], n)
                sp.dma_start(d["x_rows"][t], b["xn"][:]).then_inc(s["stored"], 16)
            sp.wait_ge(s["xn"], TURNS + 1)
            sp.dma_start(d["x_rows"][TURNS - 1], b["xn"][:]).then_inc(s["stored"], 16)
            sp.wait_ge(s["stored"], 16 * (TURNS + 1))

        @block.tensor
        def _(pe):
            pe.wait_ge(s["weights"], 16 * len(loads))
            pe.wait_ge(s["pads"], 4)
            with pe.Fori(2, TURNS + 2) as n:
                m, t = n - 1, n - 2
                pe.wait_ge(s["xp"], n * 16)
                pe.wait_ge(s["y"], m)
                for j in range(6):
                    mm = pe.matmul(p["p0"][0:PAIR, 0:WIDTH], b["xp"][:, j, :], b["wtok"][:, j, :], start=j == 0, stop=j == 5)
                mm.then_inc(s["conv"], 1)
                pe.wait_ge(s["h"], n)
                pe.wait_ge(s["xT"], m)
                for c in range(2):
                    mm = pe.transpose(p["p1"][0:HALF, c * PAIR:(c + 1) * PAIR], b["hs"][:, c * HALF:(c + 1) * HALF], keep["ident"][0:PAIR, 0:PAIR])
                mm.then_inc(s["hT_ps"], 1)
                pe.wait_ge(s["hT"], n)
                for c in range(2):
                    mm = pe.matmul(p["p0"][0:PAIR, 0:64], b["hT"][:, c, :], b["wdown"][:, c, :], start=c == 0, stop=c == 1)
                mm.then_inc(s["ckv"], 1)
                pe.wait_ge(s["PT0"], m)
                pe.wait_ge(s["PT1"], m)
                pe.wait_ge(s["C1"], m)
                for w, ps in ((b["wq"], p["p23"]), (b["wqr"], p["p45"])):
                    for j in range(6):
                        at = (j // 3) * 512 + (j % 3) * PAIR
                        for c in range(2):
                            mm = pe.matmul(ps[:, at:at + PAIR], w[:, c, j * 128:(j + 1) * 128], b["hT"][:, c, :], start=c == 0, stop=c == 1)
                mm.then_inc(s["q_ps"], 1)
                pe.wait_ge(s["imm"], 1)
                pe.wait_ge(s["ckn"], n)
                pe.transpose(p["p1"][0:64, 0:PAIR], b["ckn"][:], keep["ident"][0:PAIR, 0:PAIR]).then_inc(s["ck_ps"], 1)
                pe.wait_ge(s["imm"], 1)
                pe.wait_ge(s["ckT"], n)
                pe.wait_ge(s["V"], m)
                for im, ps in enumerate((p["p0"], p["p1"])):
                    for a in range(2):
                        mm = pe.matmul(ps[64 * a:64 * a + 64, 0:NI * HD0], b["ckT"][:, PATCHES * im:PATCHES * im + SLOT],
                                       b["wv"][:, a * 384:(a + 1) * 384], start=True, stop=True)
                mm.then_inc(s["v_ps"], 1)
                pe.wait_ge(s["rq2"], n)
                for w, ps in ((b["wk"], p["p23"]), (b["wkr"], p["p45"])):
                    for j in range(6):
                        at = (j // 3) * 512 + (j % 3) * PAIR
                        mm = pe.matmul(ps[:, at:at + PAIR], w[:, j * 128:(j + 1) * 128], b["ckT"][:, 0:PAIR], start=True, stop=True)
                mm.then_inc(s["k_ps"], 1)
                pe.wait_ge(s["imm"], 1)
                pe.wait_ge(s["qT"], n)
                pe.wait_ge(s["kT"], n)
                pe.wait_ge(s["CT1"], m)
                pe.wait_ge(s["CT0"], m)
                for i in range(NI):
                    for im in range(2):
                        for a in range(2):
                            rows = slice(64 * a, 64 * a + 64)
                            mm = pe.matmul(p["p67"][64 * im:64 * im + 64, 512 * a + i * PATCHES:512 * a + (i + 1) * PATCHES],
                                           b["qT"][rows, i, PATCHES * im:PATCHES * im + SLOT], b["kT"][rows, i, PATCHES * im:PATCHES * (im + 1)],
                                           start=True, stop=True)
                mm.then_inc(s["s_ps"], 1)
                pe.wait_ge(s["imm"], 1)
                pe.wait_ge(s["P"], n)
                for im in range(2):
                    rows = slice(64 * im, 64 * im + 64)
                    for i in range(NI):
                        mm = pe.transpose(p["p23"][:, 512 * im + i * SLOT:512 * im + (i + 1) * SLOT], b["P"][rows, i, :, :].rearrange("p a r -> p (a r)"),
                                          keep["ident"][rows, rows])
                mm.then_inc(s["pt_ps"], 1)
                pe.wait_ge(s["imm"], 1)
                pe.wait_ge(s["PT0"], n)
                pe.wait_ge(s["PT1"], n)
                pe.wait_ge(s["V"], n)
                for i in range(NI):
                    for im in range(2):
                        for a in range(2):
                            rows = slice(64 * a, 64 * a + PATCHES)
                            mm = pe.matmul(p["p45"][64 * im:64 * im + 64, 512 * a + i * HD0:512 * a + (i + 1) * HD0],
                                           b["PT"][rows, im, i, :], b["V"][rows, im, i, :], start=True, stop=True)
                mm.then_inc(s["ctx_ps"], 1)
                pe.wait_ge(s["C0"], n)
                pe.wait_ge(s["C1"], n)
                for j in range(6):
                    at = (j // 3) * 512 + (j % 3) * 128
                    mm = pe.transpose(p["p67"][:, at:at + 128], b["C"][:, j, :, :].rearrange("p a d -> p (a d)"), keep["ident"][:, :])
                mm.then_inc(s["ct_ps"], 1)
                pe.wait_ge(s["CT0"], n)
                pe.wait_ge(s["CT1"], n)
                for j in range(6):
                    mm = pe.matmul(p["p0"][0:PAIR, 0:WIDTH], b["CT"][:, j, :], b["wo"][:, j, :], start=j == 0, stop=j == 5)
                mm.then_inc(s["wo_ps"], 1)
                pe.wait_ge(s["xn"], n)
                for c in range(2):
                    mm = pe.transpose(p["p1"][0:HALF, c * PAIR:(c + 1) * PAIR], b["xn"][:, c * HALF:(c + 1) * HALF], keep["ident"][0:PAIR, 0:PAIR])
                mm.then_inc(s["x_ps"], 1)

        @block.vector
        def _(dve):
            dve.memset(b["ckT"][:, PAIR:], 0.0).then_inc(s["pads"], 1)
            dve.memset(b["qT"][:, :, PAIR:], 0.0).then_inc(s["pads"], 1)
            dve.memset(b["P"][:, :, :, PATCHES:], 0.0).then_inc(s["pads"], 1)
            dve.memset(keep["XT"][96:97, :, :], 1.0).then_inc(s["pads"], 1)
            dve.wait_ge(s["weights"], 16 * len(loads))
            dve.tensor_tensor(b["posb"][:], b["posb"][:], b["tokb"][:], ALU.add).then_inc(s["ready_pos"], 1)
            dve.wait_ge(s["ready_pos"], 1)

            def turned(ap):
                return ap.rearrange("p (u c) -> p u c", u=2)[:, :, 0:3 * PAIR].rearrange("p u (j r) -> p u j r", j=3)

            def six(ap):
                return ap.rearrange("p (u j) r -> p u j r", u=2)

            cos = b["cos"][:].rearrange("p (u j r) -> p u j r", u=1, j=1).to_broadcast([128, 2, 3, PAIR])
            sin = b["sin"][:].rearrange("p (u j r) -> p u j r", u=1, j=1).to_broadcast([128, 2, 3, PAIR])
            mask = b["mask"][:].rearrange("p (u j r) -> p u j r", u=1, j=1).to_broadcast([128, 2, NI, PATCHES])
            with dve.Fori(2, TURNS + 2) as n:
                m, t = n - 1, n - 2
                dve.wait_ge(s["conv"], n)
                dve.wait_ge(s["hb"], m)
                dve.tensor_tensor(b["hs"][:], p["p0"][0:PAIR, 0:WIDTH], b["posb"][:], ALU.add).then_inc(s["h"], 1)
                dve.wait_ge(s["ckv"], n)
                dve.bn_stats(b["st"][:], p["p0"][0:PAIR, 0:64]).then_inc(s["st"], 1)
                dve.wait_ge(s["imm"], 1)
                dve.wait_ge(s["st"], n)
                dve.bn_aggr(b["mv"][:], b["st"][:]).then_inc(s["mv"], 1)
                dve.wait_ge(s["mv"], n)
                dve.tensor_scalar(b["ve"][:], b["mv"][:, 1:2], 1e-5, None, ALU.add).then_inc(s["ve"], 1)
                dve.wait_ge(s["rstd"], n)
                dve.tensor_scalar(b["ckn"][:], p["p0"][0:PAIR, 0:64], b["mv"][:, 0:1], b["rstd"][:], ALU.subtract, ALU.mult).then_inc(s["ckn"], 1)
                dve.wait_ge(s["q_ps"], n)
                dve.tensor_tensor(six(b["r1"][:]), turned(p["p23"][:]), cos, ALU.mult).then_inc(s["rq1"], 1)
                dve.tensor_tensor(six(b["r2"][:]), turned(p["p45"][:]), sin, ALU.mult).then_inc(s["rq2"], 1)
                dve.wait_ge(s["ck_ps"], n)
                dve.tensor_scalar(b["ckT"][:, 0:PAIR], p["p1"][0:64, 0:PAIR], b["lng"][:], b["lnb"][:], ALU.mult, ALU.add).then_inc(s["ckT"], 1)
                dve.wait_ge(s["rq1"], n)
                dve.wait_ge(s["rq2"], n)
                dve.tensor_tensor(b["qT"][:, :, 0:PAIR], b["r1"][:], b["r2"][:], ALU.add).then_inc(s["qT"], 1)
                dve.wait_ge(s["k_ps"], n)
                dve.wait_ge(s["qT"], n)
                dve.tensor_tensor(six(b["r1"][:]), turned(p["p23"][:]), cos, ALU.mult).then_inc(s["rk1"], 1)
                dve.tensor_tensor(six(b["r2"][:]), turned(p["p45"][:]), sin, ALU.mult).then_inc(s["rk2"], 1)
                dve.wait_ge(s["rk1"], n)
                dve.wait_ge(s["rk2"], n)
                dve.tensor_tensor(b["kT"][:], b["r1"][:], b["r2"][:], ALU.add).then_inc(s["kT"], 1)
                dve.wait_ge(s["s_ps"], n)
                dve.tensor_tensor(b["E"][:], heads_of(p["p67"][:]), mask, ALU.add).then_inc(s["masked"], 1)
                dve.wait_ge(s["masked"], n)
                dve.tensor_reduce(b["mx"][:], b["E"][:], AX.X, ALU.max).then_inc(s["mx"], 1)
                dve.wait_ge(s["mx"], n)
                dve.tensor_tensor(b["E"][:], b["E"][:], b["mx"][:].unsqueeze(3).to_broadcast([128, 2, NI, PATCHES]), ALU.subtract).then_inc(s["shifted"], 1)
                dve.wait_ge(s["P"], n)
                dve.tensor_reduce(b["z"][:], b["P"][:, :, :, 0:PATCHES].rearrange("p i a r -> p a i r"), AX.X, ALU.add).then_inc(s["z"], 1)
                dve.wait_ge(s["z"], n)
                dve.reciprocal(b["rz"][:], b["z"][:]).then_inc(s["rz"], 1)
                dve.wait_ge(s["pt_ps"], n)
                dve.tensor_copy(b["PT"][:, 1, :, :], p["p23"][:, 512:512 + NI * SLOT].rearrange("p (i r) -> p i r", i=NI)).then_inc(s["PT1"], 1)
                dve.wait_ge(s["ctx_ps"], n)
                dve.wait_ge(s["rz"], n)
                for a, sem in ((0, s["C0"]), (1, s["C1"])):
                    dve.tensor_tensor(b["C"][:, :, a, :], p["p45"][:, 512 * a:512 * a + NI * HD0].rearrange("p (i d) -> p i d", i=NI),
                                      b["rz"][:, a, :].unsqueeze(2).to_broadcast([128, NI, HD0]), ALU.mult).then_inc(sem, 1)
                dve.wait_ge(s["ct_ps"], n)
                dve.tensor_copy(packed(b["CT"][:, 3:6, :]), slots(p["p67"][:, 512:512 + 384], 3)).then_inc(s["CT1"], 1)
                dve.wait_ge(s["wo_ps"], n)
                dve.wait_ge(s["hb"], n)
                dve.tensor_tensor(b["y"][:], p["p0"][0:PAIR, 0:WIDTH], b["hb"][:], ALU.add).then_inc(s["y"], 1)
                dve.wait_ge(s["y"], n)
                dve.bn_stats(b["st2"][:], b["y"][:]).then_inc(s["st2"], 1)
                dve.wait_ge(s["imm"], 1)
                dve.wait_ge(s["st2"], n)
                dve.bn_aggr(b["mv2"][:], b["st2"][:]).then_inc(s["mv2"], 1)
                dve.wait_ge(s["mv2"], n)
                dve.tensor_scalar(b["ve2"][:], b["mv2"][:, 1:2], 1e-5, None, ALU.add).then_inc(s["ve2"], 1)
                dve.wait_ge(s["rstd2"], n)
                dve.wait_ge(s["X"], m)
                dve.wait_ge(s["stored"], m * 16)
                dve.tensor_scalar(b["xn"][:], b["y"][:], b["mv2"][:, 0:1], b["rstd2"][:], ALU.subtract, ALU.mult).then_inc(s["xn"], 1)

        @block.scalar
        def _(act):
            act.preload_act_table(ACT.Exp)
            with act.Fori(2, TURNS + 2) as n:
                m, t = n - 1, n - 2
                act.wait_ge(s["hT_ps"], n)
                act.activation(b["hT"][:], p["p1"][0:HALF, 0:2 * PAIR].rearrange("p (c r) -> p c r", c=2), ACT.Copy).then_inc(s["hT"], 1)
                act.wait_ge(s["v_ps"], n)
                for im, ps in enumerate((p["p0"], p["p1"])):
                    ins = act.activation(b["V"][:, im, :, :], ps[:, 0:NI * HD0].rearrange("p (i d) -> p i d", i=NI), ACT.Copy)
                ins.then_inc(s["V"], 1)
                act.wait_ge(s["shifted"], n)
                act.activation(b["P"][:, :, :, 0:PATCHES].rearrange("p i a r -> p a i r"), b["E"][:], ACT.Exp, scale=HD0 ** -0.5).then_inc(s["P"], 1)
                act.wait_ge(s["pt_ps"], n)
                act.activation(b["PT"][:, 0, :, :], p["p23"][:, 0:NI * SLOT].rearrange("p (i r) -> p i r", i=NI), ACT.Copy).then_inc(s["PT0"], 1)
                act.wait_ge(s["ct_ps"], n)
                act.activation(packed(b["CT"][:, 0:3, :]), slots(p["p67"][:, 0:384], 3), ACT.Copy).then_inc(s["CT0"], 1)
                act.wait_ge(s["x_ps"], n)
                act.activation(keep["XT"][0:HALF, :, bass.ds(t * PAIR, PAIR)], p["p1"][0:HALF, 0:2 * PAIR].rearrange("p (c r) -> p c r", c=2),
                               ACT.Copy).then_inc(s["xT"], 1)
                act.activation(keep["X"][:, t, :], b["xn"][:], ACT.Copy).then_inc(s["X"], 1)

        @block.gpsimd
        def _(pool):
            pool.sem_inc(s["imm"], 1)
            pool.wait_ge(s["weights"], 16 * len(loads))
            with pool.Fori(2, TURNS + 2) as n:
                m, t = n - 1, n - 2
                pool.wait_ge(s["h"], n)
                pool.wait_ge(s["y"], m)
                pool.tensor_tensor(b["hb"][:], b["hs"][:], b["bo"][:], ALU.add).then_inc(s["hb"], 1)
                pool.wait_ge(s["ve"], n)
                pool.tensor_tensor(b["rstd"][:], b["ve"][:], keep["half"][:], ALU.pow).then_inc(s["rstd"], 1)
                pool.wait_ge(s["ve2"], n)
                pool.tensor_tensor(b["rstd2"][:], b["ve2"][:], keep["half"][:], ALU.pow).then_inc(s["rstd2"], 1)


def block_router_and_shared_expert(nc, d, keep):
    with ExitStack() as ctx:
        NS = SHARED // FC
        b = buffers(
            ctx, nc, "rt", wg=(HALF, 2, EXPERTS), ebias=(PAIR, EXPERTS), before=(PAIR, PAIR), ones=(PAIR, PAIR), slot0=(PAIR, EXPERTS),
            wsg=(HALF, 2, SHARED), wsu=(HALF, 2, SHARED), wsd=(FC, NS, WIDTH), xs=(HALF, 2, PAIR), sig=(PAIR, EXPERTS),
            choice=(PAIR, EXPERTS + 2), m8=(PAIR, 8), left=(PAIR, EXPERTS + 2), mask=(PAIR, EXPERTS), pos=(PAIR, EXPERTS),
            run=(PAIR, EXPERTS), wm=(PAIR, EXPERTS), sm=(PAIR, 1), sm1=(PAIR, 1), rs=(PAIR, 1), rs25=(PAIR, 1), sel=(PAIR, EXPERTS),
            far=(PAIR, EXPERTS), row=(PAIR, EXPERTS), row2=(PAIR, EXPERTS), code=(PAIR, EXPERTS), wsel=(PAIR, EXPERTS), s8=(PAIR, 8),
            hit=(PAIR, TOPK, EXPERTS), w6=(PAIR, TOPK), none=(PAIR, 8), sg=(FC, NS, PAIR), inter=(FC, NS, PAIR))
        into = ctx.enter_context(nc.sbuf_tensor("rt_into", [PAIR, 8], I32))
        tokens = ctx.enter_context(nc.sbuf_tensor("rt_tokens", [PAIR, TURNS], I32))
        token = ctx.enter_context(nc.sbuf_tensor("rt_token", [PAIR, 1], I32))
        zeros = ctx.enter_context(nc.sbuf_tensor("rt_zeros", [CAPH, 2 * EXPERTS], I32))
        p = banks(ctx, nc, "rt", p0=512, p1=512, p23=1024, p45=1024, p6=512, p7=512)
        s = signals(
            ctx, nc, "rt", "xs logits sig choice top8 top6 left mask pos_ps pos run wm sm rs rs25 sel far row "
            "row2 code wsel s8 w6 none into rows token landed kept g_ps u_ps sg inter out_ps Y", setup="imm weights start zeros cleared scattered")
        loads = [(b["wg"], d["wg"]), (b["ebias"], d["e_bias"]), (b["before"], d["before"]), (b["ones"], d["ones"]), (b["slot0"], d["slot0"]), (b["wsg"], d["wsg"]),
                 (b["wsu"], d["wsu"]), (b["wsd"], d["wsd"]), (tokens, d["token"])]
        block = ctx.enter_context(nc.Block())

        @block.sync
        def _(sp):
            for to, src in loads:
                sp.dma_start(to[:], src).then_inc(s["weights"], 16)
            sp.wait_ge(s["zeros"], 1)
            sp.dma_start(d["slot_token"], zeros[:]).then_inc(s["cleared"], 16)
            sp.wait_ge(s["cleared"], 16)

        @block.scalar
        def _(act):
            with act.Fori(2, TURNS + 2) as n:
                m, t = n - 1, n - 2
                act.wait_ge(s["out_ps"], m)
                act.activation(b["xs"][:], keep["XT"][0:HALF, :, bass.ds(t * PAIR, PAIR)], ACT.Copy).then_inc(s["xs"], 1)
                act.wait_ge(s["logits"], n)
                act.wait_ge(s["wsel"], m)
                act.activation(b["sig"][:], p["p0"][0:PAIR, 0:EXPERTS], ACT.Sigmoid).then_inc(s["sig"], 1)
                act.wait_ge(s["g_ps"], n)
                act.wait_ge(s["inter"], m)
                act.activation(b["sg"][:].rearrange("p (u j) r -> p u j r", u=2),
                               p["p23"][0:FC, :].rearrange("p (u c) -> p u c", u=2)[:, :, 0:4 * PAIR].rearrange("p u (j r) -> p u j r", j=4),
                               ACT.Silu).then_inc(s["sg"], 1)

        @block.tensor
        def _(pe):
            pe.wait_ge(s["weights"], 16 * len(loads))
            with pe.Fori(2, TURNS + 2) as n:
                m, t = n - 1, n - 2
                pe.wait_ge(s["xs"], n)
                pe.wait_ge(s["sig"], m)
                for c in range(2):
                    mm = pe.matmul(p["p0"][0:PAIR, 0:EXPERTS], b["xs"][:, c, :], b["wg"][:, c, :], start=c == 0, stop=c == 1)
                mm.then_inc(s["logits"], 1)
                for w, ps, free, sem in ((b["wsg"], p["p23"], s["sg"], s["g_ps"]), (b["wsu"], p["p45"], s["inter"], s["u_ps"])):
                    pe.wait_ge(free, m)
                    for j in range(NS):
                        at = (j // 4) * 512 + (j % 4) * PAIR
                        for c in range(2):
                            mm = pe.matmul(ps[0:FC, at:at + PAIR], w[:, c, j * FC:(j + 1) * FC], b["xs"][:, c, :], start=c == 0, stop=c == 1)
                    mm.then_inc(sem, 1)
                pe.wait_ge(s["mask"], n)
                pe.wait_ge(s["run"], m)
                pe.matmul(p["p1"][0:PAIR, 0:EXPERTS], b["before"][:], b["mask"][:], start=True, stop=True)
                pe.matmul(p["p1"][0:PAIR, EXPERTS:2 * EXPERTS], b["ones"][:], b["mask"][:], start=True, stop=True).then_inc(s["pos_ps"], 1)
                pe.wait_ge(s["inter"], n)
                pe.wait_ge(s["Y"], m)
                for j in range(NS):
                    mm = pe.matmul(p["p6"][0:PAIR, 0:WIDTH], b["inter"][:, j, :], b["wsd"][:, j, :], start=j == 0, stop=j == NS - 1)
                mm.then_inc(s["out_ps"], 1)

        @block.vector
        def _(dve):
            dve.memset(zeros[:], 0).then_inc(s["zeros"], 1)
            dve.memset(b["choice"][:, EXPERTS:], -BIG).then_inc(s["start"], 1)
            dve.memset(b["run"][:], 0.0).then_inc(s["start"], 1)
            dve.wait_ge(s["start"], 2)
            dve.wait_ge(s["weights"], 16 * len(loads))
            with dve.Fori(2, TURNS + 2) as n:
                m, t = n - 1, n - 2
                dve.wait_ge(s["sig"], n)
                dve.tensor_tensor(b["choice"][:, 0:EXPERTS], b["sig"][:], b["ebias"][:], ALU.add).then_inc(s["choice"], 1)
                dve.wait_ge(s["imm"], 1)
                dve.wait_ge(s["choice"], n)
                dve.max(b["m8"][:], b["choice"][:]).then_inc(s["top8"], 1)
                dve.wait_ge(s["top8"], n)
                dve.memset(b["m8"][:, TOPK:8], -BIG).then_inc(s["top6"], 1)
                dve.wait_ge(s["imm"], 1)
                dve.wait_ge(s["top6"], n)
                dve.match_replace(b["left"][:], b["m8"][:], b["choice"][:], -2 * BIG).then_inc(s["left"], 1)
                dve.wait_ge(s["left"], n)
                dve.wait_ge(s["pos_ps"], m)
                dve.tensor_tensor(b["mask"][:], b["left"][:, 0:EXPERTS], b["choice"][:, 0:EXPERTS], ALU.not_equal).then_inc(s["mask"], 1)
                dve.wait_ge(s["mask"], n)
                dve.tensor_tensor_reduce(b["wm"][:], b["sig"][:], b["mask"][:], 1.0, 0.0, ALU.mult, ALU.add, b["sm"][:]).then_inc(s["wm"], 1)
                dve.wait_ge(s["wm"], n)
                dve.tensor_scalar(b["sm1"][:], b["sm"][:], 1e-20, None, ALU.add).then_inc(s["sm"], 1)
                dve.wait_ge(s["sm"], n)
                dve.reciprocal(b["rs"][:], b["sm1"][:]).then_inc(s["rs"], 1)
                dve.wait_ge(s["rs"], n)
                dve.tensor_scalar(b["rs25"][:], b["rs"][:], 2.5, None, ALU.mult).then_inc(s["rs25"], 1)
                dve.wait_ge(s["pos_ps"], n)
                dve.tensor_tensor(b["pos"][:], p["p1"][0:PAIR, 0:EXPERTS], b["run"][:], ALU.add).then_inc(s["pos"], 1)
                dve.wait_ge(s["pos"], n)
                dve.tensor_tensor(b["run"][:], p["p1"][0:PAIR, EXPERTS:2 * EXPERTS], b["run"][:], ALU.add).then_inc(s["run"], 1)
                dve.scalar_tensor_tensor(b["sel"][:], b["pos"][:], float(CAP), b["mask"][:], ALU.is_lt, ALU.mult).then_inc(s["sel"], 1)
                dve.tensor_scalar(b["far"][:], b["pos"][:], float(CAPH), -float(CAPH * 2 * EXPERTS - 1), ALU.is_ge, ALU.mult).then_inc(s["far"], 1)
                dve.scalar_tensor_tensor(b["row"][:], b["pos"][:], 2.0 * EXPERTS, b["slot0"][:], ALU.mult, ALU.add).then_inc(s["row"], 1)
                dve.wait_ge(s["far"], n)
                dve.wait_ge(s["row"], n)
                dve.tensor_tensor(b["row2"][:], b["row"][:], b["far"][:], ALU.add).then_inc(s["row2"], 1)
                dve.wait_ge(s["row2"], n)
                dve.wait_ge(s["sel"], n)
                dve.scalar_tensor_tensor(b["code"][:], b["row2"][:], 1.0, b["sel"][:], ALU.add, ALU.mult).then_inc(s["code"], 1)
                dve.wait_ge(s["rs25"], n)
                dve.scalar_tensor_tensor(b["wsel"][:], b["wm"][:], b["rs25"][:], b["sel"][:], ALU.mult, ALU.mult).then_inc(s["wsel"], 1)
                dve.wait_ge(s["imm"], 1)
                dve.wait_ge(s["code"], n)
                dve.max(b["s8"][:], b["code"][:]).then_inc(s["s8"], 1)
                dve.wait_ge(s["s8"], n)
                dve.wait_ge(s["wsel"], n)
                dve.wait_ge(s["kept"], m)
                for k in range(TOPK):
                    ins = dve.scalar_tensor_tensor(b["hit"][:, k, :], b["code"][:], b["s8"][:, k:k + 1], b["wsel"][:], ALU.is_equal, ALU.mult,
                                                   accum_out=b["w6"][:, k:k + 1])
                ins.then_inc(s["w6"], 1)
                dve.tensor_scalar(b["none"][:], b["s8"][:], 0.0, 1.0e6, ALU.is_equal, ALU.mult).then_inc(s["none"], 1)
                dve.wait_ge(s["none"], n)
                dve.wait_ge(s["landed"], m)
                dve.scalar_tensor_tensor(into[:], b["s8"][:], -1.0, b["none"][:], ALU.add, ALU.add).then_inc(s["into"], 1)
                dve.tensor_scalar(keep["rows"][:, t, :], b["s8"][:], -1.0, 0.0, ALU.add, ALU.max).then_inc(s["rows"], 1)
                dve.wait_ge(s["sg"], n)
                dve.wait_ge(s["u_ps"], n)
                dve.wait_ge(s["out_ps"], m)
                dve.tensor_tensor(b["inter"][:].rearrange("p (u j) r -> p u j r", u=2),
                                  p["p45"][0:FC, :].rearrange("p (u c) -> p u c", u=2)[:, :, 0:4 * PAIR].rearrange("p u (j r) -> p u j r", j=4),
                                  b["sg"][:].rearrange("p (u j) r -> p u j r", u=2), ALU.mult).then_inc(s["inter"], 1)
                dve.wait_ge(s["out_ps"], n)
                dve.tensor_tensor(keep["Y"][:, t, :], p["p6"][0:PAIR, 0:WIDTH], keep["X"][:, t, :], ALU.add).then_inc(s["Y"], 1)

        @block.gpsimd
        def _(pool):
            pool.sem_inc(s["imm"], 1)
            pool.wait_ge(s["weights"], 16 * len(loads))
            pool.wait_ge(s["cleared"], 16)
            with pool.Fori(2, TURNS + 2) as n:
                m, t = n - 1, n - 2
                pool.tensor_copy(token[:], tokens[:, bass.ds(t, 1)]).then_inc(s["token"], 1)
                pool.wait_ge(s["imm"], 1)
                pool.wait_ge(s["w6"], n)
                pool.tensor_copy(keep["w6"][:, t, :], b["w6"][:]).then_inc(s["kept"], 1)
                pool.wait_ge(s["imm"], 1)
                pool.wait_ge(s["into"], n)
                pool.wait_ge(s["token"], n)
                for k in range(TOPK):
                    pool.indirect_dma_start(d["slot_token_rows"], bass.IndirectOffsetOnAxis(ap=into[:, k:k + 1], axis=0), token[:], None,
                                            bounds_check=ROWS - 1, oob_is_err=False).then_inc(s["scattered"], 16)
                pool.wait_ge(s["scattered"], 16 * TOPK * m)
                pool.sem_inc(s["landed"], 1)
            pool.wait_ge(s["scattered"], 16 * TOPK * TURNS)


def block_routed_experts(nc, d, keep):
    with ExitStack() as ctx:
        b = buffers(ctx, nc, "ex", wgu=(HALF, 2, 2, 2 * INTER), wdn=(FC, 2, NF, WIDTH), xe=(CAPH, 2, WIDTH), xT=(HALF, 2, CAP),
                    sg=(FC, NF, CAP), inter=(FC, NF, CAP), ys=(CAPH, 2, WIDTH))
        ids = ctx.enter_context(nc.sbuf_tensor("ex_ids", [CAPH, 2 * EXPERTS + 2], I32))
        idc = ctx.enter_context(nc.sbuf_tensor("ex_idc", [CAPH, 2], I32))
        p = banks(ctx, nc, "ex", pT=512, gu=2048, y=512)
        s = signals(ctx, nc, "ex", "idc x_ps xT gu0 gu1 gu2 gu3 sg0 sg1 sg2 sg3 in0 in1 in2 in3 y_ps ys", dma="stored", setup="pad ids w0 w1 xe")
        gu, sg, inter, w = (s["gu0"], s["gu1"], s["gu2"], s["gu3"]), (s["sg0"], s["sg1"], s["sg2"], s["sg3"]), (s["in0"], s["in1"], s["in2"], s["in3"]), (s["w0"], s["w1"])
        block = ctx.enter_context(nc.Block())

        def load(sp, e, u):
            sp.dma_start(b["wgu"][:, u], d["wgu"][e]).then_inc(w[u], 16)
            sp.dma_start(b["wdn"][:, u], d["wdn"][e]).then_inc(w[u], 16)

        @block.sync
        def _(sp):
            sp.wait_ge(s["pad"], 1)
            sp.dma_start(ids[:, 0:2 * EXPERTS], d["slot_token"]).then_inc(s["ids"], 16)
            for u in range(2):
                load(sp, u, u)
            def store(e):
                sp.wait_ge(s["pad"], 1)
                sp.wait_ge(s["ys"], e + 2)
                sp.dma_start(d["slot_out"][:, bass.ds(2 * e, 2), :], b["ys"][:]).then_inc(s["stored"], 16)

            with sp.Fori(0, EXPERTS // 2 - 1) as i:
                for u in range(2):
                    store(2 * i + u)
                    load(sp, 2 * i + u + 2, u)
            for u in range(2):
                store(EXPERTS - 2 + u)
            sp.wait_ge(s["stored"], 16 * (EXPERTS + 1))

        @block.gpsimd
        def _(pool):
            pool.memset(ids[:, 2 * EXPERTS:], 0).then_inc(s["pad"], 1)
            pool.wait_ge(s["ids"], 16)
            with pool.Fori(2, EXPERTS + 3) as n:
                e = n - 2
                pool.wait_ge(s["pad"], 1)
                pool.wait_ge(s["x_ps"], n - 1)
                pool.tensor_copy(idc[:], ids[:, bass.ds(2 * e, 2)]).then_inc(s["idc"], 1)
                pool.wait_ge(s["pad"], 1)
                pool.wait_ge(s["idc"], n)
                for h in range(2):
                    pool.indirect_dma_start(b["xe"][:, h, :], None, d["x_flat"], bass.IndirectOffsetOnAxis(ap=idc[:, h:h + 1], axis=0),
                                            bounds_check=TOKENS - 1, oob_is_err=False).then_inc(s["xe"], 16)
            pool.wait_ge(s["xe"], 32 * (EXPERTS + 1))

        @block.tensor
        def _(pe):
            def turn_rows(e):
                pe.wait_ge(s["xe"], 32 * (e + 1))
                pe.wait_ge(s["xT"], e + 1)
                for h in range(2):
                    for c in range(2):
                        mm = pe.transpose(p["pT"][0:HALF, c * CAP + h * CAPH:c * CAP + (h + 1) * CAPH], b["xe"][:, h, c * HALF:(c + 1) * HALF],
                                          keep["ident"][0:CAPH, 0:CAPH])
                mm.then_inc(s["x_ps"], 1)

            turn_rows(0)
            with pe.Fori(0, EXPERTS // 2) as i:
                for u in range(2):
                    e = 2 * i + u
                    pe.wait_ge(w[u], 32 * (i + 1))
                    pe.wait_ge(s["xT"], e + 2)
                    for f in range(NF):
                        pe.wait_ge(inter[f], e + 1)
                        for half in range(2):
                            for c in range(2):
                                mm = pe.matmul(p["gu"][0:FC, 512 * f + half * CAP:512 * f + (half + 1) * CAP],
                                               b["wgu"][:, u, c, half * INTER + f * FC:half * INTER + (f + 1) * FC], b["xT"][:, c, :],
                                               start=c == 0, stop=c == 1)
                        mm.then_inc(gu[f], 1)
                    turn_rows(e + 1)
                    pe.wait_ge(s["ys"], e + 1)
                    for f in range(NF):
                        pe.wait_ge(inter[f], e + 2)
                    for h in range(2):
                        for f in range(NF):
                            mm = pe.matmul(p["y"][0:CAPH, h * WIDTH:(h + 1) * WIDTH], b["inter"][:, f, h * CAPH:(h + 1) * CAPH], b["wdn"][:, u, f, :],
                                           start=f == 0, stop=f == NF - 1)
                    mm.then_inc(s["y_ps"], 1)

        @block.scalar
        def _(act):
            with act.Fori(2, EXPERTS + 2) as n:
                for f in range(NF):
                    act.wait_ge(gu[f], n)
                    act.wait_ge(inter[f], n - 1)
                    act.activation(b["sg"][:, f, :], p["gu"][0:FC, 512 * f:512 * f + CAP], ACT.Silu).then_inc(sg[f], 1)
                act.wait_ge(s["y_ps"], n)
                act.wait_ge(s["stored"], 16 * (n - 1))
                act.activation(b["ys"][:].rearrange("p h w -> p (h w)"), p["y"][0:CAPH, 0:2 * WIDTH], ACT.Copy).then_inc(s["ys"], 1)

        @block.vector
        def _(dve):
            def turned(n):
                dve.wait_ge(s["x_ps"], n)
                dve.tensor_copy(b["xT"][:].rearrange("p c r -> p (c r)"), p["pT"][0:HALF, 0:2 * CAP]).then_inc(s["xT"], 1)

            turned(2)
            with dve.Fori(2, EXPERTS + 2) as n:
                dve.wait_ge(s["y_ps"], n - 1)
                for f in range(NF):
                    dve.wait_ge(sg[f], n)
                    dve.tensor_tensor(b["inter"][:, f, :], p["gu"][0:FC, 512 * f + CAP:512 * f + 2 * CAP], b["sg"][:, f, :], ALU.mult).then_inc(inter[f], 1)
                turned(n + 1)


def block_combine(nc, d, keep):
    with ExitStack() as ctx:
        b = buffers(ctx, nc, "cb", G=(PAIR, TOPK, WIDTH), w6=(PAIR, TOPK), a=(PAIR, TOPK, WIDTH), st=(PAIR, 6), mv=(PAIR, 2), ve=(PAIR, 1),
                    rstd=(PAIR, 1), xn=(PAIR, WIDTH))
        rows = ctx.enter_context(nc.sbuf_tensor("cb_rows", [PAIR, 8], I32))
        p = banks(ctx, nc, "cb", p1=512)
        s = signals(ctx, nc, "cb", "rows w6 a0 a1 a2 a3 a4 a5 st mv ve rstd xn x_ps xT X", setup="imm g0 g1 g2 g3 g4 g5")
        got, added = (s["g0"], s["g1"], s["g2"], s["g3"], s["g4"], s["g5"]), (s["a0"], s["a1"], s["a2"], s["a3"], s["a4"], s["a5"])
        block = ctx.enter_context(nc.Block())

        @block.gpsimd
        def _(pool):
            pool.sem_inc(s["imm"], 1)
            with pool.Fori(2, TURNS + 2) as n:
                m, t = n - 1, n - 2
                pool.wait_ge(s["imm"], 1)
                pool.wait_ge(s["a5"], m)
                pool.tensor_copy(rows[:], keep["rows"][:, t, :]).then_inc(s["rows"], 1)
                for k in range(TOPK):
                    pool.wait_ge(s["imm"], 1)
                    pool.wait_ge(s["rows"], n)
                    pool.indirect_dma_start(b["G"][:, k, :], None, d["slot_out_rows"], bass.IndirectOffsetOnAxis(ap=rows[:, k:k + 1], axis=0),
                                            bounds_check=ROWS - 1, oob_is_err=False).then_inc(got[k], 16)
                pool.wait_ge(s["ve"], n)
                pool.tensor_tensor(b["rstd"][:], b["ve"][:], keep["half"][:], ALU.pow).then_inc(s["rstd"], 1)

        @block.scalar
        def _(act):
            with act.Fori(2, TURNS + 2) as n:
                m, t = n - 1, n - 2
                act.wait_ge(s["a5"], m)
                act.activation(b["w6"][:], keep["w6"][:, t, :], ACT.Copy).then_inc(s["w6"], 1)
                act.wait_ge(s["x_ps"], n)
                act.activation(keep["XT"][0:HALF, :, bass.ds(t * PAIR, PAIR)], p["p1"][0:HALF, 0:2 * PAIR].rearrange("p (c r) -> p c r", c=2),
                               ACT.Copy).then_inc(s["xT"], 1)
                act.activation(keep["X"][:, t, :], b["xn"][:], ACT.Copy).then_inc(s["X"], 1)

        @block.tensor
        def _(pe):
            with pe.Fori(2, TURNS + 2) as n:
                pe.wait_ge(s["imm"], 1)
                pe.wait_ge(s["xn"], n)
                pe.wait_ge(s["xT"], n - 1)
                for c in range(2):
                    mm = pe.transpose(p["p1"][0:HALF, c * PAIR:(c + 1) * PAIR], b["xn"][:, c * HALF:(c + 1) * HALF], keep["ident"][0:PAIR, 0:PAIR])
                mm.then_inc(s["x_ps"], 1)

        @block.vector
        def _(dve):
            with dve.Fori(2, TURNS + 2) as n:
                m, t = n - 1, n - 2
                dve.wait_ge(s["w6"], n)
                for k in range(TOPK):
                    dve.wait_ge(got[k], 16 * m)
                    if k:
                        dve.wait_ge(added[k - 1], n)
                    before = b["a"][:, k - 1, :] if k else keep["Y"][:, t, :]
                    dve.scalar_tensor_tensor(b["a"][:, k, :], b["G"][:, k, :], b["w6"][:, k:k + 1], before, ALU.mult, ALU.add).then_inc(added[k], 1)
                dve.wait_ge(s["a5"], n)
                dve.bn_stats(b["st"][:], b["a"][:, 5, :]).then_inc(s["st"], 1)
                dve.wait_ge(s["imm"], 1)
                dve.wait_ge(s["st"], n)
                dve.bn_aggr(b["mv"][:], b["st"][:]).then_inc(s["mv"], 1)
                dve.wait_ge(s["mv"], n)
                dve.tensor_scalar(b["ve"][:], b["mv"][:, 1:2], 1e-5, None, ALU.add).then_inc(s["ve"], 1)
                dve.wait_ge(s["rstd"], n)
                dve.wait_ge(s["X"], m)
                dve.tensor_scalar(b["xn"][:], b["a"][:, 5, :], b["mv"][:, 0:1], b["rstd"][:], ALU.subtract, ALU.mult).then_inc(s["xn"], 1)


def norm(dve, b, s, n, prev, y, eps, to, free=()):
    dve.wait_ge(s["y"], n)
    dve.bn_stats(b["st"][:], y).then_inc(s["st"], 1)
    dve.wait_ge(s["imm"], 1)
    dve.wait_ge(s["st"], n)
    dve.bn_aggr(b["mv"][:], b["st"][:]).then_inc(s["mv"], 1)
    dve.wait_ge(s["mv"], n)
    dve.tensor_scalar(b["ve"][:], b["mv"][:, 1:2], eps, None, ALU.add).then_inc(s["ve"], 1)
    dve.wait_ge(s["rstd"], n)
    for sem in free:
        dve.wait_ge(sem, prev)
    return dve.tensor_scalar(to, y, b["mv"][:, 0:1], b["rstd"][:], ALU.subtract, ALU.mult)


def pool_rstd(pool, b, s, n, keep):
    pool.wait_ge(s["ve"], n)
    pool.tensor_tensor(b["rstd"][:], b["ve"][:], keep["half"][:], ALU.pow).then_inc(s["rstd"], 1)


def block_bert(nc, d, keep):
    with ExitStack() as ctx:
        b = buffers(
            ctx, nc, "ba", wq=(HALF + 1, 2, WIDTH), wk=(HALF + 1, 2, WIDTH), wc=(HALF + 1, 2, WIDTH), wv=(HALF + 1, 2, WIDTH),
            wo=(HALF, 2, WIDTH), rows=(PAIR, 6, WIDTH), own=(HALF, NI), block16=(HALF, HALF), eye=(128, PATCHES),
            xs=(HALF + 1, 2, 128), hb=(PAIR, WIDTH), qT=(HALF, 2, 128), kd=(HALF, 2, NI, PAIR), c=(HALF, 2, PAIR), c2=(HALF, 2, PAIR),
            n2=(HALF, 2 * PAIR), rn=(HALF, 2 * PAIR), cT=(HALF, 2, 128), cd=(HALF, 2, NI, PAIR), V=(128, 2, NI, 16),
            E1=(128, 2, NI, PATCHES), E2=(128, 2, NI, PATCHES), mx=(128, 2, NI), z=(128, 2, 2, NI), rz=(128, 2, 2, NI),
            rh=(128, 2, 2, NI), P=(128, NI, 2, SLOT), PT=(128, 2, NI, SLOT), C=(128, 2, HALF), CT=(HALF, 2, PAIR), y=(PAIR, WIDTH),
            st=(PAIR, 6), mv=(PAIR, 2), ve=(PAIR, 1), rstd=(PAIR, 1), yn=(PAIR, WIDTH), yg=(PAIR, WIDTH), xn=(PAIR, WIDTH))
        f = buffers(
            ctx, nc, "bf", wi=(HALF + 1, 2, FFN), wo2=(128, NFF, WIDTH), h=(128, NFF, GCOLS), hb=(PAIR, GROUP, WIDTH),
            y=(PAIR, GROUP, WIDTH), st=(PAIR, 6), mv=(PAIR, 2), ve=(PAIR, 1), rstd=(PAIR, 1), yn=(PAIR, WIDTH), yg=(PAIR, WIDTH),
            xn=(PAIR, WIDTH))
        p = banks(ctx, nc, "ba", p0=512, p1=512, p2=512, p3=512, p45=1024, p67=1024)
        s = signals(
            ctx, nc, "ba", "xs hb q_ps k_ps c_ps v_ps qT kd c c2 n2_ps n2 rn cT cd V s1_ps s2_ps mx "
            "shifted E2 E1 E1x z1 z2 rz rh P1 P2 P pt_ps PT0 PT1 ctx_ps C ct_ps CT wo_ps y st mv ve rstd yn yg xn x_ps xT X",
            setup="imm consts pads saved attn_w")
        g = signals(ctx, nc, "bf", "h0 h1 h2 h3 h4 h5 a0 a1 a2 a3 a4 a5 hb out_ps y st mv ve rstd yn yg xn x_ps xT X", setup="ffn_w")
        g["imm"] = s["imm"]
        h_ps, h_sb = (g["h0"], g["h1"], g["h2"], g["h3"], g["h4"], g["h5"]), (g["a0"], g["a1"], g["a2"], g["a3"], g["a4"], g["a5"])
        h_bank = [p["p0"][:], p["p1"][:], p["p2"][:], p["p3"][:], p["p45"][:, 0:512], p["p45"][:, 512:1024]]
        consts = [(b["own"], d["own"]), (b["block16"], d["block16"]), (b["eye"], d["eye"])]
        AW, FW = 6, 2
        block = ctx.enter_context(nc.Block())

        @block.sync
        def _(sp):
            for to, src in consts:
                sp.dma_start(to[:], src).then_inc(s["consts"], 16)

            def load_attention(l):
                for to, src in ((b["wq"], d["bwq"]), (b["wk"], d["bwk"]), (b["wc"], d["bwc"]), (b["wv"], d["bwv"]), (b["wo"], d["bwo"]), (b["rows"], d["brows"])):
                    sp.dma_start(to[:], src[l]).then_inc(s["attn_w"], 16)

            def load_ffn(l):
                for to, src in ((f["wi"], d["bwi"]), (f["wo2"], d["bwo2"])):
                    sp.dma_start(to[:], src[l]).then_inc(g["ffn_w"], 16)

            load_attention(0)
            load_ffn(0)
            with sp.Fori(1, LAYERS) as l:
                sp.wait_ge(s["imm"], 1)
                sp.wait_ge(g["xn"], l * TURNS + 1)
                load_attention(l)
                sp.wait_ge(g["out_ps"], l * TURNS + 1)
                load_ffn(l)

        @block.tensor
        def _(pe):
            pe.wait_ge(s["consts"], 16 * len(consts))
            pe.wait_ge(s["pads"], 5)

            def attention(n, m):
                pe.wait_ge(s["xs"], n)
                for w, ps, free, sem in ((b["wc"], p["p2"], s["n2"], s["c_ps"]), (b["wq"], p["p0"], s["CT"], s["q_ps"]), (b["wk"], p["p1"], s["y"], s["k_ps"])):
                    pe.wait_ge(free, m)
                    for a in range(2):
                        for c in range(2):
                            K = HALF + c
                            mm = pe.matmul(ps[0:HALF, a * PAIR:(a + 1) * PAIR], w[0:K, c, a * HALF:(a + 1) * HALF], b["xs"][0:K, c, 0:PAIR],
                                           start=c == 0, stop=c == 1)
                    mm.then_inc(sem, 1)
                pe.wait_ge(s["xT"], m)
                for im in range(2):
                    for a in range(2):
                        for c in range(2):
                            K = HALF + c
                            mm = pe.matmul(p["p3"][64 * a:64 * a + 64, im * HALF:(im + 1) * HALF], b["xs"][0:K, c, PATCHES * im:PATCHES * im + SLOT],
                                           b["wv"][0:K, c, a * HALF:(a + 1) * HALF], start=c == 0, stop=c == 1)
                mm.then_inc(s["v_ps"], 1)
                pe.wait_ge(s["c2"], n)
                pe.wait_ge(s["c"], n)
                pe.matmul(p["p2"][0:HALF, 0:2 * PAIR], b["block16"][:], b["c2"][:].rearrange("p c r -> p (c r)"), start=True, stop=True).then_inc(s["n2_ps"], 1)
                pe.wait_ge(s["C"], m)
                for left, right, ready, ps, sem in ((b["qT"], b["kd"], (s["qT"], s["kd"]), p["p67"], s["s2_ps"]), (b["cT"], b["cd"], (s["cT"], s["cd"]), p["p45"], s["s1_ps"])):
                    for r in ready:
                        pe.wait_ge(r, n)
                    if ps is p["p45"]:
                        pe.wait_ge(s["PT0"], m)
                        pe.wait_ge(s["PT1"], m)
                    for im in range(2):
                        for a in range(2):
                            mm = pe.matmul(ps[64 * im:64 * im + 64, 512 * a:512 * a + NI * PATCHES], left[:, a, PATCHES * im:PATCHES * im + SLOT],
                                           right[:, a, :, PATCHES * im:PATCHES * (im + 1)], start=True, stop=True)
                    mm.then_inc(sem, 1)
                pe.wait_ge(s["imm"], 1)
                pe.wait_ge(s["P"], n)
                for im in range(2):
                    rows = slice(64 * im, 64 * im + 64)
                    for i in range(NI):
                        mm = pe.transpose(p["p45"][:, 512 * im + i * SLOT:512 * im + (i + 1) * SLOT], b["P"][rows, i, :, :].rearrange("p a r -> p (a r)"),
                                          keep["ident"][rows, rows])
                mm.then_inc(s["pt_ps"], 1)
                pe.wait_ge(s["imm"], 1)
                pe.wait_ge(s["PT0"], n)
                pe.wait_ge(s["PT1"], n)
                pe.wait_ge(s["V"], n)
                for i in range(NI):
                    for im in range(2):
                        for a in range(2):
                            rows = slice(64 * a, 64 * a + PATCHES)
                            mm = pe.matmul(p["p67"][64 * im:64 * im + 64, 512 * a + i * 16:512 * a + (i + 1) * 16],
                                           b["PT"][rows, im, i, :], b["V"][rows, im, i, :], start=True, stop=True)
                mm.then_inc(s["ctx_ps"], 1)
                pe.wait_ge(s["C"], n)
                pe.wait_ge(s["qT"], n)
                for a in range(2):
                    mm = pe.transpose(p["p0"][0:HALF, a * 128:(a + 1) * 128], b["C"][:, a, :], keep["ident"][:, :])
                mm.then_inc(s["ct_ps"], 1)
                pe.wait_ge(s["CT"], n)
                for c in range(2):
                    mm = pe.matmul(p["p1"][0:PAIR, 0:WIDTH], b["CT"][:, c, :], b["wo"][:, c, :], start=c == 0, stop=c == 1)
                mm.then_inc(s["wo_ps"], 1)
                pe.wait_ge(s["imm"], 1)
                pe.wait_ge(s["xn"], n)
                for c in range(2):
                    mm = pe.transpose(p["p3"][0:HALF, c * PAIR:(c + 1) * PAIR], b["xn"][:, c * HALF:(c + 1) * HALF], keep["ident"][0:PAIR, 0:PAIR])
                mm.then_inc(s["x_ps"], 1)

            def mlp(q, n, m, n0):
                cols = bass.ds((q - 1) * GCOLS, GCOLS)
                for j in range(NFF):
                    pe.wait_ge(h_sb[j], m)
                    if j == NFF - 1:
                        pe.wait_ge(g["xT"], n0 - 1)
                    for c in range(2):
                        K = HALF + c
                        mm = pe.matmul(h_bank[j][:, 0:GCOLS], f["wi"][0:K, c, j * 128:(j + 1) * 128], keep["XT"][0:K, c, cols], start=c == 0, stop=c == 1)
                    mm.then_inc(h_ps[j], 1)
                for j in range(NFF):
                    pe.wait_ge(h_sb[j], n)

                def down(r):
                    pe.wait_ge(g["y"], n0 + max(r - 2, -1))
                    for j in range(NFF):
                        mm = pe.matmul(p["p67"][0:PAIR, 512 * (r % 2):512 * (r % 2) + WIDTH], f["h"][:, j, r * PAIR:(r + 1) * PAIR], f["wo2"][:, j, :],
                                       start=j == 0, stop=j == NFF - 1)
                    mm.then_inc(g["out_ps"], 1)

                def turn_back(r):
                    pe.wait_ge(s["imm"], 1)
                    pe.wait_ge(g["xn"], n0 + r)
                    pe.wait_ge(g["xT"], n0 + r - 1)
                    for c in range(2):
                        mm = pe.transpose(h_bank[5][0:HALF, c * PAIR:(c + 1) * PAIR], f["xn"][:, c * HALF:(c + 1) * HALF], keep["ident"][0:PAIR, 0:PAIR])
                    mm.then_inc(g["x_ps"], 1)

                down(0)
                down(1)
                for r in range(GROUP):
                    if r + 2 < GROUP:
                        down(r + 2)
                    turn_back(r)

            with pe.Fori(1, LAYERS + 1) as l:
                with pe.Fori(1, TURNS + 1) as q:
                    n = TURNS * (l - 1) + q + 1
                    pe.wait_ge(s["attn_w"], 16 * AW * l)
                    pe.wait_ge(g["xT"], TURNS * (l - 1) + 1)
                    attention(n, n - 1)
                with pe.Fori(1, GROUPS + 1) as q:
                    pe.wait_ge(g["ffn_w"], 16 * FW * l)
                    pe.wait_ge(s["xT"], TURNS * l + 1)
                    n = GROUPS * (l - 1) + q + 1
                    mlp(q, n, n - 1, GROUP * (n - 2) + 2)

        @block.vector
        def _(dve):
            dve.memset(b["xs"][:, :, PAIR:], 0.0).then_inc(s["pads"], 1)
            dve.memset(b["qT"][:, :, PAIR:], 0.0).then_inc(s["pads"], 1)
            dve.memset(b["cT"][:, :, PAIR:], 0.0).then_inc(s["pads"], 1)
            dve.memset(b["P"][:, :, :, PATCHES:], 0.0).then_inc(s["pads"], 1)
            dve.memset(b["PT"][:], 0.0).then_inc(s["pads"], 1)
            dve.tensor_copy(keep["Y"][:], keep["X"][:]).then_inc(s["saved"], 1)
            dve.wait_ge(s["consts"], 16 * len(consts))
            dve.wait_ge(s["pads"], 5)

            def attention(n, m):
                dve.wait_ge(s["k_ps"], n)
                dve.wait_ge(s["s2_ps"], m)
                for a in range(2):
                    ins = dve.tensor_tensor(b["kd"][:, a], p["p1"][0:HALF, a * PAIR:(a + 1) * PAIR].unsqueeze(1).to_broadcast([HALF, NI, PAIR]),
                                            b["own"][:].unsqueeze(2).to_broadcast([HALF, NI, PAIR]), ALU.mult)
                ins.then_inc(s["kd"], 1)
                dve.wait_ge(s["s2_ps"], n)
                dve.tensor_reduce(b["mx"][:], heads_of(p["p67"][:]), AX.X, ALU.max).then_inc(s["mx"], 1)
                dve.wait_ge(s["mx"], n)
                dve.tensor_tensor(b["E2"][:], heads_of(p["p67"][:]), b["mx"][:].unsqueeze(3).to_broadcast([128, 2, NI, PATCHES]), ALU.subtract).then_inc(s["shifted"], 1)
                dve.wait_ge(s["E2"], n)
                dve.tensor_reduce(b["z"][:, 1], b["E2"][:], AX.X, ALU.add).then_inc(s["z2"], 1)
                dve.wait_ge(s["E1x"], n)
                dve.tensor_reduce(b["z"][:, 0], b["E1"][:], AX.X, ALU.add).then_inc(s["z1"], 1)
                dve.wait_ge(s["z1"], n)
                dve.wait_ge(s["z2"], n)
                dve.reciprocal(b["rz"][:], b["z"][:]).then_inc(s["rz"], 1)
                dve.wait_ge(s["rz"], n)
                dve.tensor_scalar(b["rh"][:], b["rz"][:], 0.5, None, ALU.mult).then_inc(s["rh"], 1)
                dve.wait_ge(s["rh"], n)
                dve.tensor_tensor(b["E2"][:], b["E2"][:], b["rh"][:, 1].unsqueeze(3).to_broadcast([128, 2, NI, PATCHES]), ALU.mult).then_inc(s["P2"], 1)
                dve.wait_ge(s["P1"], n)
                dve.wait_ge(s["P2"], n)
                dve.tensor_tensor(b["P"][:, :, :, 0:PATCHES].rearrange("p i a r -> p a i r"), b["E1"][:], b["E2"][:], ALU.add).then_inc(s["P"], 1)
                dve.wait_ge(s["pt_ps"], n)
                dve.tensor_copy(b["PT"][:, 1], p["p45"][:, 512:512 + NI * SLOT].rearrange("p (i r) -> p i r", i=NI)).then_inc(s["PT1"], 1)
                dve.wait_ge(s["ctx_ps"], n)
                dve.tensor_copy(b["C"][:], p["p67"][:].rearrange("p (a c) -> p a c", a=2)[:, :, 0:HALF]).then_inc(s["C"], 1)
                dve.wait_ge(s["ct_ps"], n)
                dve.tensor_copy(packed(b["CT"][:]), slots(p["p0"][0:HALF, 0:256], 2)).then_inc(s["CT"], 1)
                dve.wait_ge(s["wo_ps"], n)
                dve.wait_ge(s["hb"], n)
                dve.tensor_tensor(b["y"][:], p["p1"][0:PAIR, 0:WIDTH], b["hb"][:], ALU.add).then_inc(s["y"], 1)
                norm(dve, b, s, n, m, b["y"][:], 1e-12, b["yn"][:], (s["yg"],)).then_inc(s["yn"], 1)

            def mlp(n0):
                def add(r):
                    dve.wait_ge(g["out_ps"], n0 + r)
                    dve.tensor_tensor(f["y"][:, r], p["p67"][0:PAIR, 512 * (r % 2):512 * (r % 2) + WIDTH], f["hb"][:, r], ALU.add).then_inc(g["y"], 1)

                add(0)
                add(1)
                for r in range(GROUP):
                    norm(dve, f, g, n0 + r, n0 + r - 1, f["y"][:, r], 1e-12, f["yn"][:], (g["yg"],)).then_inc(g["yn"], 1)
                    if r + 2 < GROUP:
                        add(r + 2)

            with dve.Fori(1, LAYERS + 1) as l:
                with dve.Fori(1, TURNS + 1) as q:
                    n = TURNS * (l - 1) + q + 1
                    attention(n, n - 1)
                with dve.Fori(1, GROUPS + 1) as q:
                    n = GROUPS * (l - 1) + q + 1
                    dve.wait_ge(g["hb"], n)
                    mlp(GROUP * (n - 2) + 2)

        @block.scalar
        def _(act):
            act.wait_ge(s["pads"], 5)
            act.wait_ge(s["saved"], 1)

            def attention(q, n, m):
                act.wait_ge(s["v_ps"], m)
                act.activation(b["xs"][:, :, 0:PAIR], keep["XT"][:, :, bass.ds((q - 1) * PAIR, PAIR)], ACT.Copy).then_inc(s["xs"], 1)
                act.wait_ge(s["c_ps"], n)
                act.wait_ge(s["n2_ps"], m)
                act.wait_ge(s["cT"], m)
                act.activation(b["c2"][:].rearrange("p a r -> p (a r)"), p["p2"][0:HALF, 0:2 * PAIR], ACT.Square).then_inc(s["c2"], 1)
                act.activation(b["c"][:].rearrange("p a r -> p (a r)"), p["p2"][0:HALF, 0:2 * PAIR], ACT.Copy).then_inc(s["c"], 1)
                act.wait_ge(s["q_ps"], n)
                act.wait_ge(s["s2_ps"], m)
                act.activation(b["qT"][:, :, 0:PAIR], p["p0"][0:HALF, 0:2 * PAIR].rearrange("p (a r) -> p a r", a=2), ACT.Copy, scale=0.25).then_inc(s["qT"], 1)
                act.wait_ge(s["n2_ps"], n)
                act.activation(b["n2"][:], p["p2"][0:HALF, 0:2 * PAIR], ACT.Ln).then_inc(s["n2"], 1)
                act.wait_ge(s["n2"], n)
                act.activation(b["rn"][:], b["n2"][:], ACT.Exp, scale=-0.5).then_inc(s["rn"], 1)
                act.wait_ge(s["v_ps"], n)
                act.wait_ge(s["ctx_ps"], m)
                act.activation(b["V"][:].rearrange("p m i d -> p (m i d)"), p["p3"][:, 0:WIDTH], ACT.Copy).then_inc(s["V"], 1)
                act.wait_ge(s["shifted"], n)
                act.activation(b["E2"][:], b["E2"][:], ACT.Exp).then_inc(s["E2"], 1)
                act.wait_ge(s["s1_ps"], n)
                act.wait_ge(s["P"], m)
                act.activation(b["E1"][:], heads_of(p["p45"][:]), ACT.Exp, bias=1.0, scale=-1.0).then_inc(s["E1"], 1)
                act.wait_ge(s["pt_ps"], n)
                act.activation(b["PT"][:, 0], p["p45"][:, 0:NI * SLOT].rearrange("p (i r) -> p i r", i=NI), ACT.Copy).then_inc(s["PT0"], 1)
                act.wait_ge(s["imm"], 1)
                act.wait_ge(s["x_ps"], n)
                act.activation(keep["XT"][0:HALF, :, bass.ds((q - 1) * PAIR, PAIR)], p["p3"][0:HALF, 0:2 * PAIR].rearrange("p (c r) -> p c r", c=2),
                               ACT.Copy).then_inc(s["xT"], 1)
                act.activation(keep["X"][:, bass.ds(q - 1, 1), :], b["xn"][:].unsqueeze(1), ACT.Copy).then_inc(s["X"], 1)

            def mlp(q, n, n0):
                act.wait_ge(g["out_ps"], n0 - 1)
                for j in range(NFF):
                    act.wait_ge(h_ps[j], n)
                    act.activation(f["h"][:, j, :], h_bank[j][:, 0:GCOLS], ACT.Gelu).then_inc(h_sb[j], 1)
                for r in range(GROUP):
                    turn = GROUP * (q - 1) + r
                    act.wait_ge(g["x_ps"], n0 + r)
                    act.activation(keep["XT"][0:HALF, :, bass.ds(turn * PAIR, PAIR)], h_bank[5][0:HALF, 0:2 * PAIR].rearrange("p (c r) -> p c r", c=2),
                                   ACT.Copy).then_inc(g["xT"], 1)
                    act.activation(keep["X"][:, bass.ds(turn, 1), :], f["xn"][:].unsqueeze(1), ACT.Copy).then_inc(g["X"], 1)

            with act.Fori(1, LAYERS + 1) as l:
                act.preload_act_table_set("natural_log_exp_and_others")
                with act.Fori(1, TURNS + 1) as q:
                    act.wait_ge(g["xT"], TURNS * (l - 1) + 1)
                    n = TURNS * (l - 1) + q + 1
                    attention(q, n, n - 1)
                with act.Fori(1, GROUPS + 1) as q:
                    n = GROUPS * (l - 1) + q + 1
                    mlp(q, n, GROUP * (n - 2) + 2)

        @block.gpsimd
        def _(pool):
            pool.sem_inc(s["imm"], 1)
            pool.wait_ge(s["consts"], 16 * len(consts))
            pool.wait_ge(s["pads"], 5)

            def affine(bb, ss, n, m, k):
                pool.wait_ge(ss["yn"], n)
                pool.tensor_tensor(bb["yg"][:], bb["yn"][:], b["rows"][:, k, :], ALU.mult).then_inc(ss["yg"], 1)
                pool.wait_ge(ss["yg"], n)
                pool.wait_ge(ss["x_ps"], m)
                pool.wait_ge(ss["X"], m)
                pool.tensor_tensor(bb["xn"][:], bb["yg"][:], b["rows"][:, k + 1, :], ALU.add).then_inc(ss["xn"], 1)

            def attention(q, n, m):
                pool.wait_ge(s["y"], m)
                pool.tensor_tensor(b["hb"][:], keep["X"][:, bass.ds(q - 1, 1), :].rearrange("p o w -> p (o w)"), b["rows"][:, 0, :], ALU.add).then_inc(s["hb"], 1)
                pool.wait_ge(s["rn"], n)
                pool.wait_ge(s["c"], n)
                pool.wait_ge(s["s1_ps"], m)
                pool.tensor_tensor(b["cT"][:, :, 0:PAIR], b["c"][:], b["rn"][:].rearrange("p (a r) -> p a r", a=2), ALU.mult).then_inc(s["cT"], 1)
                pool.wait_ge(s["cT"], n)
                for a in range(2):
                    ins = pool.tensor_tensor(b["cd"][:, a], b["cT"][:, a, 0:PAIR].unsqueeze(1).to_broadcast([HALF, NI, PAIR]),
                                             b["own"][:].unsqueeze(2).to_broadcast([HALF, NI, PAIR]), ALU.mult)
                ins.then_inc(s["cd"], 1)
                pool.wait_ge(s["E1"], n)
                E1 = b["E1"][:].rearrange("p a i r -> p (a i) r")
                pool.tensor_tensor(E1, E1, b["eye"][:].unsqueeze(1).to_broadcast([128, HEADS, PATCHES]), ALU.mult).then_inc(s["E1x"], 1)
                pool.wait_ge(s["rh"], n)
                pool.tensor_tensor(E1, E1, b["rh"][:, 0].rearrange("p a i -> p (a i)").unsqueeze(2).to_broadcast([128, HEADS, PATCHES]),
                                   ALU.mult).then_inc(s["P1"], 1)
                pool_rstd(pool, b, s, n, keep)
                affine(b, s, n, m, 1)

            def mlp(q, n0):
                pool.wait_ge(g["y"], n0 - 1)
                pool.tensor_tensor(f["hb"][:], keep["X"][:, bass.ds(GROUP * (q - 1), GROUP), :], b["rows"][:, 3, :].unsqueeze(1).to_broadcast([PAIR, GROUP, WIDTH]),
                                   ALU.add).then_inc(g["hb"], 1)
                for r in range(GROUP):
                    pool_rstd(pool, f, g, n0 + r, keep)
                    affine(f, g, n0 + r, n0 + r - 1, 4)

            with pool.Fori(1, LAYERS + 1) as l:
                with pool.Fori(1, TURNS + 1) as q:
                    pool.wait_ge(s["attn_w"], 16 * AW * l)
                    pool.wait_ge(g["X"], TURNS * (l - 1) + 1)
                    n = TURNS * (l - 1) + q + 1
                    attention(q, n, n - 1)
                with pool.Fori(1, GROUPS + 1) as q:
                    pool.wait_ge(s["X"], TURNS * l + 1)
                    mlp(q, GROUP * (GROUPS * (l - 1) + q - 1) + 2)


def block_residual_norm(nc, d, keep):
    with ExitStack() as ctx:
        b = buffers(ctx, nc, "rn", y=(PAIR, WIDTH), st=(PAIR, 6), mv=(PAIR, 2), ve=(PAIR, 1), rstd=(PAIR, 1), xn=(PAIR, WIDTH))
        p = banks(ctx, nc, "rn", p1=512)
        s = signals(ctx, nc, "rn", "y st mv ve rstd xn x_ps xT X", setup="imm")
        block = ctx.enter_context(nc.Block())

        @block.vector
        def _(dve):
            with dve.Fori(2, TURNS + 2) as n:
                m, t = n - 1, n - 2
                dve.wait_ge(s["xn"], m)
                dve.tensor_tensor(b["y"][:], keep["X"][:, bass.ds(t, 1), :].rearrange("p o w -> p (o w)"),
                                  keep["Y"][:, bass.ds(t, 1), :].rearrange("p o w -> p (o w)"), ALU.add).then_inc(s["y"], 1)
                norm(dve, b, s, n, m, b["y"][:], 1e-5, b["xn"][:], (s["X"], s["x_ps"])).then_inc(s["xn"], 1)

        @block.gpsimd
        def _(pool):
            pool.sem_inc(s["imm"], 1)
            with pool.Fori(2, TURNS + 2) as n:
                pool_rstd(pool, b, s, n, keep)

        @block.tensor
        def _(pe):
            with pe.Fori(2, TURNS + 2) as n:
                pe.wait_ge(s["imm"], 1)
                pe.wait_ge(s["xn"], n)
                pe.wait_ge(s["xT"], n - 1)
                for c in range(2):
                    mm = pe.transpose(p["p1"][0:HALF, c * PAIR:(c + 1) * PAIR], b["xn"][:, c * HALF:(c + 1) * HALF], keep["ident"][0:PAIR, 0:PAIR])
                mm.then_inc(s["x_ps"], 1)

        @block.scalar
        def _(act):
            with act.Fori(2, TURNS + 2) as n:
                act.wait_ge(s["x_ps"], n)
                act.activation(keep["XT"][0:HALF, :, bass.ds((n - 2) * PAIR, PAIR)], p["p1"][0:HALF, 0:2 * PAIR].rearrange("p (c r) -> p c r", c=2),
                               ACT.Copy).then_inc(s["xT"], 1)
                act.activation(keep["Y"][:, bass.ds(n - 2, 1), :], b["xn"][:].unsqueeze(1), ACT.Copy).then_inc(s["X"], 1)


def block_mixture(nc, d, keep):
    NE = 8
    with ExitStack() as ctx:
        b = buffers(ctx, nc, "mx", wg=(HALF + 1, 2, NE), xs=(HALF + 1, 2, PAIR), lg=(PAIR, 10), m8=(PAIR, 8), neg=(PAIR, 1), left=(PAIR, 10),
                    mask=(PAIR, NE), ex=(PAIR, NE), em=(PAIR, NE), sm=(PAIR, 1), rs=(PAIR, 1), gates=(PAIR, NE, TURNS),
                    w1=(HALF + 1, 2, 2, FFN), w2=(128, 2, NFF, WIDTH), b2=(PAIR, 2, WIDTH), h=(128, NFF, GCOLS), ob=(PAIR, GROUP, WIDTH),
                    y=(PAIR, WIDTH), st=(PAIR, 6), mv=(PAIR, 2), ve=(PAIR, 1), rstd=(PAIR, 1), xn=(PAIR, WIDTH))
        p = banks(ctx, nc, "mx", hp=3072, o0=512, o1=512)
        s = signals(ctx, nc, "mx", "xs lg_ps lg top8 top2 left mask neg ex em rs gates h0 h1 h2 h3 h4 h5 a0 a1 a2 a3 a4 a5 "
                                   "out_ps ob Y y st mv ve rstd xn", dma="stored", setup="imm wg w0 w1 pad")
        h_ps, h_sb, w = (s["h0"], s["h1"], s["h2"], s["h3"], s["h4"], s["h5"]), (s["a0"], s["a1"], s["a2"], s["a3"], s["a4"], s["a5"]), (s["w0"], s["w1"])
        h_bank = [p["hp"][:, 512 * j:512 * j + GCOLS] for j in range(NFF)]
        outs = (p["o0"], p["o1"])
        out_rows = d["out"].rearrange("(t p) w -> t p w", p=PAIR)
        block = ctx.enter_context(nc.Block())

        def load(sp, e, u):
            for to, src in ((b["w1"], d["w1"]), (b["w2"], d["w2"]), (b["b2"], d["b2e"])):
                sp.dma_start(to[:, u], src[e]).then_inc(w[u], 16)

        @block.sync
        def _(sp):
            sp.dma_start(b["wg"][:], d["gwg"]).then_inc(s["wg"], 16)
            for u in range(2):
                load(sp, u, u)
            with sp.Fori(1, NE // 2) as i:
                for u in range(2):
                    sp.wait_ge(s["imm"], 1)
                    sp.wait_ge(s["Y"], TURNS * (2 * i + u - 1) + 1)
                    load(sp, 2 * i + u, u)
            with sp.Fori(2, TURNS + 2) as n:
                sp.wait_ge(s["imm"], 1)
                sp.wait_ge(s["xn"], n)
                sp.dma_start(out_rows[n - 2], b["xn"][:]).then_inc(s["stored"], 16)
            sp.wait_ge(s["stored"], 16 * (TURNS + 1))

        @block.tensor
        def _(pe):
            pe.wait_ge(s["wg"], 16)
            with pe.Fori(2, TURNS + 2) as n:
                pe.wait_ge(s["xs"], n)
                pe.wait_ge(s["lg"], n - 1)
                for c in range(2):
                    K = HALF + c
                    mm = pe.matmul(p["o0"][0:PAIR, 0:NE], b["xs"][0:K, c, :], b["wg"][0:K, c, :], start=c == 0, stop=c == 1)
                mm.then_inc(s["lg_ps"], 1)
            pe.wait_ge(s["lg"], TURNS + 1)
            with pe.Fori(1, NE // 2 + 1) as i:
                for u in range(2):
                    with pe.Fori(1, GROUPS + 1) as q:
                        pe.wait_ge(w[u], 48 * i)
                        n = GROUPS * (2 * (i - 1) + u) + q + 1
                        n0 = GROUP * (n - 2) + 2
                        cols = bass.ds((q - 1) * GCOLS, GCOLS)
                        for j in range(NFF):
                            pe.wait_ge(h_sb[j], n - 1)
                            for c in range(2):
                                K = HALF + c
                                mm = pe.matmul(h_bank[j], b["w1"][0:K, u, c, j * 128:(j + 1) * 128], keep["XT"][0:K, c, cols], start=c == 0, stop=c == 1)
                            mm.then_inc(h_ps[j], 1)
                        for j in range(NFF):
                            pe.wait_ge(h_sb[j], n)
                        for r in range(GROUP):
                            pe.wait_ge(s["ob"], n0 + max(r - 2, -1))
                            for j in range(NFF):
                                mm = pe.matmul(outs[r % 2][0:PAIR, 0:WIDTH], b["h"][:, j, r * PAIR:(r + 1) * PAIR], b["w2"][:, u, j, :],
                                               start=j == 0, stop=j == NFF - 1)
                            mm.then_inc(s["out_ps"], 1)

        @block.scalar
        def _(act):
            with act.Fori(2, TURNS + 2) as n:
                act.wait_ge(s["lg_ps"], n - 1)
                act.activation(b["xs"][:], keep["XT"][:, :, bass.ds((n - 2) * PAIR, PAIR)], ACT.Copy).then_inc(s["xs"], 1)
                act.wait_ge(s["neg"], n)
                act.wait_ge(s["em"], n - 1)
                act.activation(b["ex"][:], b["lg"][:, 0:NE], ACT.Exp, bias=b["neg"][:]).then_inc(s["ex"], 1)
            with act.Fori(2, NE * GROUPS + 2) as n:
                act.wait_ge(s["out_ps"], GROUP * (n - 2) + 1)
                for j in range(NFF):
                    act.wait_ge(h_ps[j], n)
                    act.activation(b["h"][:, j, :], h_bank[j], ACT.Relu).then_inc(h_sb[j], 1)

        @block.vector
        def _(dve):
            dve.memset(b["lg"][:, NE:], -BIG).then_inc(s["pad"], 1)
            dve.wait_ge(s["pad"], 1)
            with dve.Fori(2, TURNS + 2) as n:
                dve.wait_ge(s["lg_ps"], n)
                dve.wait_ge(s["ex"], n - 1)
                dve.tensor_copy(b["lg"][:, 0:NE], p["o0"][0:PAIR, 0:NE]).then_inc(s["lg"], 1)
                dve.wait_ge(s["imm"], 1)
                dve.wait_ge(s["lg"], n)
                dve.max(b["m8"][:], b["lg"][:]).then_inc(s["top8"], 1)
                dve.wait_ge(s["top8"], n)
                dve.tensor_scalar(b["neg"][:], b["m8"][:, 0:1], -1.0, None, ALU.mult).then_inc(s["neg"], 1)
                dve.memset(b["m8"][:, 2:8], -BIG).then_inc(s["top2"], 1)
                dve.wait_ge(s["imm"], 1)
                dve.wait_ge(s["top2"], n)
                dve.match_replace(b["left"][:], b["m8"][:], b["lg"][:], -2 * BIG).then_inc(s["left"], 1)
                dve.wait_ge(s["left"], n)
                dve.tensor_tensor(b["mask"][:], b["left"][:, 0:NE], b["lg"][:, 0:NE], ALU.not_equal).then_inc(s["mask"], 1)
                dve.wait_ge(s["mask"], n)
                dve.wait_ge(s["ex"], n)
                dve.tensor_tensor_reduce(b["em"][:], b["ex"][:], b["mask"][:], 1.0, 0.0, ALU.mult, ALU.add, b["sm"][:]).then_inc(s["em"], 1)
                dve.wait_ge(s["em"], n)
                dve.reciprocal(b["rs"][:], b["sm"][:]).then_inc(s["rs"], 1)
                dve.wait_ge(s["rs"], n)
                dve.tensor_scalar(b["gates"][:, :, bass.ds(n - 2, 1)].rearrange("p e o -> p (e o)"), b["em"][:], b["rs"][:], None, ALU.mult).then_inc(s["gates"], 1)
            dve.wait_ge(s["gates"], TURNS + 1)
            with dve.Fori(1, NE // 2 + 1) as i:
                for u in range(2):
                    with dve.Fori(1, GROUPS + 1) as q:
                        dve.wait_ge(w[u], 48 * i)
                        e = 2 * (i - 1) + u
                        n0 = GROUP * (GROUPS * e + q - 1) + 2
                        for r in range(GROUP):
                            turn = GROUP * (q - 1) + r
                            dve.wait_ge(s["out_ps"], n0 + r)
                            dve.tensor_tensor(b["ob"][:, r], outs[r % 2][0:PAIR, 0:WIDTH], b["b2"][:, u], ALU.add).then_inc(s["ob"], 1)
                            dve.wait_ge(s["ob"], n0 + r)
                            row = keep["Y"][:, bass.ds(turn, 1), :].rearrange("p o w -> p (o w)")
                            gate = b["gates"][:].rearrange("p e t -> p (e t)")[:, bass.ds(TURNS * e + turn, 1)]
                            dve.scalar_tensor_tensor(row, b["ob"][:, r], gate, row, ALU.mult, ALU.add).then_inc(s["Y"], 1)
            dve.wait_ge(s["Y"], NE * TURNS + 1)
            with dve.Fori(2, TURNS + 2) as n:
                dve.wait_ge(s["xn"], n - 1)
                dve.tensor_copy(b["y"][:], keep["Y"][:, bass.ds(n - 2, 1), :].rearrange("p o w -> p (o w)")).then_inc(s["y"], 1)
                dve.wait_ge(s["stored"], 16 * (n - 1))
                norm(dve, b, s, n, n - 1, b["y"][:], 1e-5, b["xn"][:]).then_inc(s["xn"], 1)

        @block.gpsimd
        def _(pool):
            pool.sem_inc(s["imm"], 1)
            with pool.Fori(2, TURNS + 2) as n:
                pool_rstd(pool, b, s, n, keep)


def storage(nc, ctx, d):
    keep = buffers(ctx, nc, "keep", X=(PAIR, TURNS, WIDTH), XT=(HALF + 1, 2, TOKENS), Y=(PAIR, TURNS, WIDTH), w6=(PAIR, TURNS, TOPK),
                   ident=(128, 128), half=(PAIR, 1))
    keep["rows"] = ctx.enter_context(nc.sbuf_tensor("keep_rows", [PAIR, TURNS, 8], I32))
    d["x_rows"] = nc.dram_tensor("x_rows", (TURNS, PAIR, WIDTH), F32).ap()
    d["x_flat"] = d["x_rows"].rearrange("t p w -> (t p) w")
    d["slot_token"] = nc.dram_tensor("slot_token", (CAPH, 2 * EXPERTS), I32).ap()
    d["slot_token_rows"] = d["slot_token"].rearrange("p (e o) -> (p e) o", o=1)
    d["slot_out"] = nc.dram_tensor("slot_out", (CAPH, 2 * EXPERTS, WIDTH), F32).ap()
    d["slot_out_rows"] = d["slot_out"].rearrange("p e w -> (p e) w")
    return keep, d


def program(nc, d, out):
    d = dict(d, out=out)
    with ExitStack() as ctx:
        keep, d = storage(nc, ctx, d)
        block_embed_and_latent_attention(nc, d, keep)
        block_router_and_shared_expert(nc, d, keep)
        block_routed_experts(nc, d, keep)
        block_combine(nc, d, keep)
        block_bert(nc, d, keep)
        block_residual_norm(nc, d, keep)
        block_mixture(nc, d, keep)


def rope_tables():
    inv = (1.0 / 10000.0 ** (np.arange(0, HD0, 2, dtype=np.float32) / HD0)).astype(np.float32)
    ang = np.arange(PATCHES, dtype=np.float32)[:, None] * inv[None, :]
    ang = np.concatenate([ang, ang], axis=-1).T
    sign = np.where(np.arange(HD0) < HD0 // 2, -1.0, 1.0).astype(np.float32)[:, None]
    return np.tile(np.cos(ang), (2, 2)), np.tile(np.sin(ang) * sign, (2, 2))


def position_table():
    j = np.arange(WIDTH)
    expo = (2 * (j // 2)).astype(np.float32) / np.float32(WIDTH)
    angle = np.arange(PATCHES, dtype=np.float32)[:, None] / np.power(np.float32(10000.0), expo)
    angle = angle + np.where(j % 2 == 1, np.float32(np.pi / 2), np.float32(0.0)).astype(np.float32)
    return np.tile(np.sin(angle.astype(np.float32)), (2, 1))


def constants():
    cos, sin = rope_tables()
    row, col = np.arange(128)[:, None] % SLOT, np.arange(PATCHES)[None, :]
    e = np.arange(EXPERTS)
    token = np.arange(PAIR)[:, None] + PAIR * np.arange(TURNS)[None, :]
    return {
        "cos": cos, "sin": sin, "pos": position_table(),
        "mask": np.where((row >= PATCHES) | (col <= row), 0.0, -BIG),
        "eye": np.where(row == col, np.e, 1.0), "ident": np.eye(128), "half": np.full((PAIR, 1), -0.5),
        "before": np.triu(np.ones((PAIR, PAIR)), 1), "ones": np.ones((PAIR, PAIR)),
        "slot0": np.tile(2.0 * e, (PAIR, 1)), "token": token.astype(np.uint32),
        "own": np.where(np.arange(HALF)[:, None] // 16 == np.arange(NI)[None, :], 1.0, 0.0),
        "block16": np.where(np.arange(HALF)[:, None] // 16 == np.arange(HALF)[None, :] // 16, 1.0, 0.0),
    }


def chunks(w, ones=None):
    out = w.reshape(2, HALF, -1).transpose(1, 0, 2)
    if ones is None:
        return out
    row = np.stack([np.zeros_like(ones), ones])[None]
    return np.concatenate([out, row], axis=0)


def rows_of(v):
    return np.broadcast_to(v, (PAIR, v.shape[-1]))


def layout(i):
    px = i["x"][:, :, 0:112, 0:112].reshape(TURNS, 2, 3, 7, 16, 7, 16)
    px = px.transpose(0, 2, 4, 6, 1, 3, 5).reshape(TURNS, 6, 128, PAIR).transpose(0, 2, 1, 3)
    wq, wup = i["L0_attn_Wq"], i["L0_attn_Wup"]
    turn = (np.arange(HD0) + HD0 // 2) % HD0
    swap = (np.arange(HEADS)[:, None] * HD0 + turn[None, :]).reshape(-1)
    wk = wup[:, 0:768]
    a = {
        "xp": px, "wtok": i["L0_tok_W"].reshape(WIDTH, 6, 128).transpose(2, 1, 0), "tok_b": rows_of(i["L0_tok_b"]),
        "bo0": rows_of(i["L0_attn_bo"]), "wdown": chunks(i["L0_attn_Wdown"]), "wq0": chunks(wq), "wq0r": chunks(wq[:, swap]),
        "wk0": wk, "wk0r": wk[:, swap], "wv0": wup[:, 768:].reshape(64, NI, 2, HD0).transpose(0, 2, 1, 3).reshape(64, 768),
        "wo0": i["L0_attn_Wo"].reshape(6, 128, WIDTH).transpose(1, 0, 2),
        "ln_g": i["L0_attn_ln_g"].reshape(64, 1), "ln_b": i["L0_attn_ln_b"].reshape(64, 1),
        "wg": chunks(i["L0_ffn_Wg"].T), "e_bias": rows_of(i["L0_ffn_e_bias"]),
        "wgu": i["L0_ffn_W_gate_up"].reshape(EXPERTS, 2, HALF, 2 * INTER).transpose(0, 2, 1, 3),
        "wdn": i["L0_ffn_W_down"].reshape(EXPERTS, NF, FC, WIDTH).transpose(0, 2, 1, 3),
        "wsg": chunks(i["L0_ffn_Wsg"]), "wsu": chunks(i["L0_ffn_Wsu"]),
        "wsd": i["L0_ffn_Wsd"].reshape(8, FC, WIDTH).transpose(1, 0, 2),
    }
    for n in "qkvc":
        w, bias = i[f"L1_attn_W{n}"], i[f"L1_attn_b{n}"]
        a[f"bw{n}"] = np.stack([chunks(w[l], bias[l]) for l in range(LAYERS)])
    a["bwo"] = np.stack([chunks(i["L1_attn_Wo"][l]) for l in range(LAYERS)])
    a["bwi"] = np.stack([chunks(i["L1_attn_Wi"][l], i["L1_attn_bi"][l]) for l in range(LAYERS)])
    a["bwo2"] = i["L1_attn_Wo2"].reshape(LAYERS, NFF, 128, WIDTH).transpose(0, 2, 1, 3)
    rows = [i[f"L1_attn_{n}"] for n in ("bo", "g1", "b1", "bo2", "g2", "b2")]
    a["brows"] = np.broadcast_to(np.stack(rows, axis=1)[:, None], (LAYERS, PAIR, 6, WIDTH))
    a["gwg"] = chunks(i["L1_ffn_Wg"], i["L1_ffn_bg"])
    a["w1"] = np.stack([chunks(i["L1_ffn_W1"][e], i["L1_ffn_b1"][e]) for e in range(8)])
    a["w2"] = i["L1_ffn_W2"].reshape(8, NFF, 128, WIDTH).transpose(0, 2, 1, 3)
    a["b2e"] = np.broadcast_to(i["L1_ffn_b2"][:, None], (8, PAIR, WIDTH))
    return a


def kernel(**inputs):
    import concourse.bacc as bacc
    from concourse.bass_utils import run_bass_kernel_spmd

    arrays = {n: np.ascontiguousarray(a) for n, a in layout({k: np.asarray(v) for k, v in inputs.items()}).items()}
    arrays |= {n: np.ascontiguousarray(a if a.dtype == np.uint32 else a.astype(np.float32)) for n, a in constants().items()}
    nc = bacc.Bacc("TRN2", target_bir_lowering=False, num_devices=1)
    d = {n: nc.dram_tensor(n, a.shape, mybir.dt.from_np(a.dtype), kind="ExternalInput").ap() for n, a in arrays.items()}
    out = nc.dram_tensor("out", (TOKENS, WIDTH), F32, kind="ExternalOutput").ap()
    program(nc, d, out)
    r = run_bass_kernel_spmd(nc, [arrays], core_ids=[0])
    return r.results[0]["out"].reshape(IMAGES, PATCHES, WIDTH)
```

```python
from contextlib import ExitStack

import numpy as np
import concourse.bass as bass
from concourse import mybir

F32 = mybir.dt.float32
I32 = mybir.dt.uint32
ALU = mybir.AluOpType
ACT = mybir.ActivationFunctionType
AX = mybir.AxisListType

IMAGES, PATCHES, WIDTH = 64, 49, 192
TOKENS = IMAGES * PATCHES
PAIR = 2 * PATCHES
TURNS = IMAGES // 2
HALF = WIDTH // 2
GROUP = 4
GROUPS = TURNS // GROUP
GCOLS = GROUP * PAIR
SLOT = 64
PADDED = SLOT + PATCHES
HEADS = 12
NI = HEADS // 2
HD0 = 64
EXPERTS, TOPK, CAP, INTER = 128, 6, 192, 464
FC = 116
NF = INTER // FC
SHARED = 928
CAPH = CAP // 2
ROWS = CAPH * 2 * EXPERTS
LAYERS, FFN, NFF = 4, 768, 6
BIG = 1.0e30


def signals(ctx, nc, tag, names, dma="", setup=""):
    found = {n: nc.alloc_semaphore(f"{tag}_{n}") for n in f"{names} {dma} {setup}".split()}
    for n in names.split():
        nc.gpsimd.sem_inc(found[n], 1)
    for n in dma.split():
        nc.gpsimd.sem_inc(found[n], 16)
    nc.all_engine_barrier()
    ctx.callback(nc.all_engine_barrier)
    ctx.callback(nc.clear_and_free_semaphores, list(found.values()))
    return dict(**found)


def buffers(ctx, nc, tag, **shapes):
    return dict(**{n: ctx.enter_context(nc.sbuf_tensor(f"{tag}_{n}", list(s), F32)) for n, s in shapes.items()})


def banks(ctx, nc, tag, **widths):
    return dict(**{n: ctx.enter_context(nc.psum_tensor(f"{tag}_{n}", [128, w], F32)) for n, w in widths.items()})


def heads_of(ap):
    return ap.rearrange("p (a c) -> p a c", a=2)[:, :, 0:NI * PATCHES].rearrange("p a (i r) -> p a i r", i=NI)


def packed(ap):
    return ap.rearrange("p j (m r) -> p j m r", m=2)


def slots(ap, j):
    return ap.rearrange("p (j m q) -> p j m q", j=j, m=2)[:, :, :, 0:PATCHES]


def block_embed_and_latent_attention(nc, d, keep):
    with ExitStack() as ctx:
        b = buffers(
            ctx, nc, "la", xp=(128, 6, PAIR), wtok=(128, 6, WIDTH), posb=(PAIR, WIDTH), tokb=(PAIR, WIDTH), bo=(PAIR, WIDTH),
            wdown=(HALF, 2, 64), wq=(HALF, 2, 768), wqr=(HALF, 2, 768), wk=(64, 768), wkr=(64, 768), wv=(64, 768),
            wo=(128, 6, WIDTH), lng=(64, 1), lnb=(64, 1), cos=(128, PAIR), sin=(128, PAIR), mask=(128, PATCHES),
            hs=(PAIR, WIDTH), hb=(PAIR, WIDTH), hT=(HALF, 2, PAIR), st=(PAIR, 6), mv=(PAIR, 2), ve=(PAIR, 1), rstd=(PAIR, 1),
            ckn=(PAIR, 64), ckT=(64, PADDED + 15), r1=(128, 6, PAIR), r2=(128, 6, PAIR), qT=(128, 6, 128), kT=(128, 6, PAIR),
            V=(128, 2, NI, HD0), E=(128, 2, NI, PATCHES), mx=(128, 2, NI), P=(128, NI, 2, SLOT), z=(128, 2, NI), rz=(128, 2, NI),
            PT=(128, 2, NI, SLOT), C=(128, NI, 2, HD0), CT=(128, 6, PAIR), y=(PAIR, WIDTH), st2=(PAIR, 6), mv2=(PAIR, 2),
            ve2=(PAIR, 1), rstd2=(PAIR, 1), xn=(PAIR, WIDTH))
        p = banks(ctx, nc, "la", p0=512, p1=512, p23=1024, p45=1024, p67=1024)
        s = signals(
            ctx, nc, "la", "conv h hb hT_ps hT ckv q_ps st mv ve rstd ckn ck_ps ckT rq1 rq2 qT k_ps v0_ps v1_ps "
            "V0 V1 rk1 rk2 kT s_ps masked mx shifted P z rz pt_ps PT0 PT1 ctx_ps C0 C1 ct_ps CT0 CT1 wo_ps y st2 mv2 ve2 rstd2 xn "
            "x_ps xT X", dma="xp stored", setup="imm weights ready_pos pads")
        loads = [(b["wtok"], d["wtok"]), (b["posb"], d["pos"]), (b["tokb"], d["tok_b"]), (b["bo"], d["bo0"]), (b["wdown"], d["wdown"]), (b["wq"], d["wq0"]),
                 (b["wqr"], d["wq0r"]), (b["wk"], d["wk0"]), (b["wkr"], d["wk0r"]), (b["wv"], d["wv0"]), (b["wo"], d["wo0"]), (b["lng"], d["ln_g"]), (b["lnb"], d["ln_b"]),
                 (b["cos"], d["cos"]), (b["sin"], d["sin"]), (b["mask"], d["mask"]), (keep["ident"], d["ident"]), (keep["half"], d["half"])]
        ckv_ps, ck_ps = p["p0"][0:PAIR, 384:448], p["p67"][0:64, 384:384 + PAIR]
        block = ctx.enter_context(nc.Block())

        def steps(engine, step):
            first, last = 2, TURNS + 1
            step(first, None, None)
            step(first + 1, first, None)
            with engine.Fori(first + 2, last + 1) as n:
                step(n, n - 1, n - 2)
            step(None, last, last - 1)
            step(None, None, last)

        @block.sync
        def _(sp):
            sp.dma_start(b["xp"][:], d["xp"][0]).then_inc(s["xp"], 16)
            for to, src in loads:
                sp.dma_start(to[:], src).then_inc(s["weights"], 16)

            def load(n):
                sp.wait_ge(s["imm"], 1)
                sp.wait_ge(s["conv"], n)
                sp.dma_start(b["xp"][:], d["xp"][n - 1]).then_inc(s["xp"], 16)

            def store(n):
                sp.wait_ge(s["imm"], 1)
                sp.wait_ge(s["xn"], n)
                sp.dma_start(d["x_rows"][n - 2], b["xn"][:]).then_inc(s["stored"], 16)

            load(2)
            with sp.Fori(2, TURNS) as n:
                load(n + 1)
                store(n)
            store(TURNS)
            store(TURNS + 1)
            sp.wait_ge(s["stored"], 16 * (TURNS + 1))

        @block.tensor
        def _(pe):
            pe.wait_ge(s["weights"], 16 * len(loads))
            pe.wait_ge(s["pads"], 4)

            def rotary(w, ps, of):
                for j in range(6):
                    at = (j // 3) * 512 + (j % 3) * PAIR
                    chunks_of = of(w, j)
                    for c, (left, right) in enumerate(chunks_of):
                        mm = pe.matmul(ps[:, at:at + PAIR], left, right, start=c == 0, stop=c == len(chunks_of) - 1)
                return mm

            def of_queries(w, j):
                return [(w[:, c, j * 128:(j + 1) * 128], b["hT"][:, c, :]) for c in range(2)]

            def of_keys(w, j):
                return [(w[:, j * 128:(j + 1) * 128], b["ckT"][:, 0:PAIR])]

            def values(im, ps, sem):
                for a in range(2):
                    mm = pe.matmul(ps[64 * a:64 * a + 64, 0:NI * HD0], b["ckT"][:, PATCHES * im:PATCHES * im + SLOT],
                                   b["wv"][:, a * 384:(a + 1) * 384], start=True, stop=True)
                mm.then_inc(sem, 1)

            def step(A, B, T):
                if T is not None:
                    pe.wait_ge(s["imm"], 1)
                    pe.wait_ge(s["xn"], T)
                    pe.wait_ge(s["V1"], T if B is None else B)
                    for c in range(2):
                        mm = pe.transpose(p["p1"][0:HALF, c * PAIR:(c + 1) * PAIR], b["xn"][:, c * HALF:(c + 1) * HALF], keep["ident"][0:PAIR, 0:PAIR])
                    mm.then_inc(s["x_ps"], 1)
                if A is not None:
                    pe.wait_ge(s["xp"], A * 16)
                    pe.wait_ge(s["V0"], A - 1)
                    for j in range(6):
                        mm = pe.matmul(p["p0"][0:PAIR, 0:WIDTH], b["xp"][:, j, :], b["wtok"][:, j, :], start=j == 0, stop=j == 5)
                    mm.then_inc(s["conv"], 1)
                    pe.wait_ge(s["h"], A)
                    pe.wait_ge(s["V1"], A - 1)
                    if T is not None:
                        pe.wait_ge(s["xT"], T)
                    for c in range(2):
                        mm = pe.transpose(p["p1"][0:HALF, c * PAIR:(c + 1) * PAIR], b["hs"][:, c * HALF:(c + 1) * HALF], keep["ident"][0:PAIR, 0:PAIR])
                    mm.then_inc(s["hT_ps"], 1)
                if B is not None:
                    pe.wait_ge(s["imm"], 1)
                    pe.wait_ge(s["P"], B)
                    for im in range(2):
                        rows = slice(64 * im, 64 * im + 64)
                        for i in range(NI):
                            mm = pe.transpose(p["p67"][:, 512 * im + i * SLOT:512 * im + (i + 1) * SLOT], b["P"][rows, i, :, :].rearrange("p a r -> p (a r)"),
                                              keep["ident"][rows, rows])
                    mm.then_inc(s["pt_ps"], 1)
                if A is not None:
                    pe.wait_ge(s["hT"], A)
                    for c in range(2):
                        mm = pe.matmul(ckv_ps, b["hT"][:, c, :], b["wdown"][:, c, :], start=c == 0, stop=c == 1)
                    mm.then_inc(s["ckv"], 1)
                    pe.wait_ge(s["rk2"], A - 1)
                    rotary(b["wq"], p["p23"], of_queries)
                    rotary(b["wqr"], p["p45"], of_queries).then_inc(s["q_ps"], 1)
                    pe.wait_ge(s["imm"], 1)
                    pe.wait_ge(s["ckn"], A)
                    pe.wait_ge(s["PT0"], A - 1)
                    pe.wait_ge(s["PT1"], A - 1)
                    pe.transpose(ck_ps, b["ckn"][:], keep["ident"][0:PAIR, 0:PAIR]).then_inc(s["ck_ps"], 1)
                if B is not None:
                    pe.wait_ge(s["imm"], 1)
                    pe.wait_ge(s["PT0"], B)
                    pe.wait_ge(s["PT1"], B)
                    pe.wait_ge(s["V0"], B)
                    pe.wait_ge(s["V1"], B)
                    pe.wait_ge(s["xT"], B - 1)
                    for i in range(NI):
                        for im in range(2):
                            for a, ps in enumerate((p["p0"], p["p1"])):
                                rows = slice(64 * a, 64 * a + PATCHES)
                                mm = pe.matmul(ps[64 * im:64 * im + 64, i * HD0:(i + 1) * HD0],
                                               b["PT"][rows, im, i, :], b["V"][rows, im, i, :], start=True, stop=True)
                    mm.then_inc(s["ctx_ps"], 1)
                if A is not None:
                    pe.wait_ge(s["ckT"], A)
                    pe.wait_ge(s["rq2"], A)
                    rotary(b["wk"], p["p23"], of_keys)
                    rotary(b["wkr"], p["p45"], of_keys).then_inc(s["k_ps"], 1)
                if B is not None:
                    pe.wait_ge(s["C0"], B)
                    pe.wait_ge(s["C1"], B)
                    for j in range(6):
                        at = (j // 3) * 512 + (j % 3) * 128
                        mm = pe.transpose(p["p67"][:, at:at + 128], b["C"][:, j, :, :].rearrange("p a d -> p (a d)"), keep["ident"][:, :])
                    mm.then_inc(s["ct_ps"], 1)
                if A is not None:
                    pe.wait_ge(s["imm"], 1)
                    pe.wait_ge(s["C1"], A - 1)
                    values(1, p["p1"], s["v1_ps"])
                if B is not None:
                    pe.wait_ge(s["CT0"], B)
                    pe.wait_ge(s["CT1"], B)
                    for j in range(6):
                        mm = pe.matmul(p["p0"][0:PAIR, 0:WIDTH], b["CT"][:, j, :], b["wo"][:, j, :], start=j == 0, stop=j == 5)
                    mm.then_inc(s["wo_ps"], 1)
                if A is not None:
                    pe.wait_ge(s["imm"], 1)
                    pe.wait_ge(s["qT"], A)
                    pe.wait_ge(s["kT"], A)
                    pe.wait_ge(s["CT1"], A - 1)
                    pe.wait_ge(s["CT0"], A - 1)
                    for i in range(NI):
                        for im in range(2):
                            for a in range(2):
                                rows = slice(64 * a, 64 * a + 64)
                                mm = pe.matmul(p["p67"][64 * im:64 * im + 64, 512 * a + i * PATCHES:512 * a + (i + 1) * PATCHES],
                                               b["qT"][rows, i, PATCHES * im:PATCHES * im + SLOT], b["kT"][rows, i, PATCHES * im:PATCHES * (im + 1)],
                                               start=True, stop=True)
                    mm.then_inc(s["s_ps"], 1)
                    pe.wait_ge(s["imm"], 1)
                    pe.wait_ge(s["y"], A - 1)
                    values(0, p["p0"], s["v0_ps"])

            steps(pe, step)

        @block.vector
        def _(dve):
            dve.memset(b["ckT"][:, PAIR:], 0.0).then_inc(s["pads"], 1)
            dve.memset(b["qT"][:, :, PAIR:], 0.0).then_inc(s["pads"], 1)
            dve.memset(b["P"][:, :, :, PATCHES:], 0.0).then_inc(s["pads"], 1)
            dve.memset(keep["XT"][96:97, :, :], 1.0).then_inc(s["pads"], 1)
            dve.wait_ge(s["weights"], 16 * len(loads))
            dve.tensor_tensor(b["posb"][:], b["posb"][:], b["tokb"][:], ALU.add).then_inc(s["ready_pos"], 1)
            dve.wait_ge(s["ready_pos"], 1)

            def turned(ap):
                return ap.rearrange("p (u c) -> p u c", u=2)[:, :, 0:3 * PAIR].rearrange("p u (j r) -> p u j r", j=3)

            def six(ap):
                return ap.rearrange("p (u j) r -> p u j r", u=2)

            cos = b["cos"][:].rearrange("p (u j r) -> p u j r", u=1, j=1).to_broadcast([128, 2, 3, PAIR])
            sin = b["sin"][:].rearrange("p (u j r) -> p u j r", u=1, j=1).to_broadcast([128, 2, 3, PAIR])
            mask = b["mask"][:].rearrange("p (u j r) -> p u j r", u=1, j=1).to_broadcast([128, 2, NI, PATCHES])

            def step(A, B, T):
                if A is not None:
                    dve.wait_ge(s["conv"], A)
                    dve.wait_ge(s["hb"], A - 1)
                    dve.tensor_tensor(b["hs"][:], p["p0"][0:PAIR, 0:WIDTH], b["posb"][:], ALU.add).then_inc(s["h"], 1)
                if B is not None:
                    dve.wait_ge(s["P"], B)
                    dve.tensor_reduce(b["z"][:], b["P"][:, :, :, 0:PATCHES].rearrange("p i a r -> p a i r"), AX.X, ALU.add).then_inc(s["z"], 1)
                    dve.wait_ge(s["z"], B)
                    dve.reciprocal(b["rz"][:], b["z"][:]).then_inc(s["rz"], 1)
                    dve.wait_ge(s["pt_ps"], B)
                    dve.tensor_copy(b["PT"][:, 1, :, :], p["p67"][:, 512:512 + NI * SLOT].rearrange("p (i r) -> p i r", i=NI)).then_inc(s["PT1"], 1)
                if A is not None:
                    dve.wait_ge(s["ckv"], A)
                    dve.bn_stats(b["st"][:], ckv_ps).then_inc(s["st"], 1)
                    dve.wait_ge(s["imm"], 1)
                    dve.wait_ge(s["st"], A)
                    dve.bn_aggr(b["mv"][:], b["st"][:]).then_inc(s["mv"], 1)
                    dve.wait_ge(s["mv"], A)
                    dve.tensor_scalar(b["ve"][:], b["mv"][:, 1:2], 1e-5, None, ALU.add).then_inc(s["ve"], 1)
                    dve.wait_ge(s["rstd"], A)
                    dve.tensor_scalar(b["ckn"][:], ckv_ps, b["mv"][:, 0:1], b["rstd"][:], ALU.subtract, ALU.mult).then_inc(s["ckn"], 1)
                    dve.wait_ge(s["q_ps"], A)
                    dve.tensor_tensor(six(b["r1"][:]), turned(p["p23"][:]), cos, ALU.mult).then_inc(s["rq1"], 1)
                    dve.tensor_tensor(six(b["r2"][:]), turned(p["p45"][:]), sin, ALU.mult).then_inc(s["rq2"], 1)
                    dve.wait_ge(s["ck_ps"], A)
                    dve.tensor_scalar(b["ckT"][:, 0:PAIR], ck_ps, b["lng"][:], b["lnb"][:], ALU.mult, ALU.add).then_inc(s["ckT"], 1)
                    dve.wait_ge(s["rq1"], A)
                    dve.wait_ge(s["rq2"], A)
                    dve.tensor_tensor(b["qT"][:, :, 0:PAIR], b["r1"][:], b["r2"][:], ALU.add).then_inc(s["qT"], 1)
                if B is not None:
                    dve.wait_ge(s["ctx_ps"], B)
                    dve.wait_ge(s["rz"], B)
                    for a, (ps, sem) in enumerate(((p["p0"], s["C0"]), (p["p1"], s["C1"]))):
                        dve.tensor_tensor(b["C"][:, :, a, :], ps[:, 0:NI * HD0].rearrange("p (i d) -> p i d", i=NI),
                                          b["rz"][:, a, :].unsqueeze(2).to_broadcast([128, NI, HD0]), ALU.mult).then_inc(sem, 1)
                if A is not None:
                    dve.wait_ge(s["k_ps"], A)
                    dve.wait_ge(s["qT"], A)
                    dve.tensor_tensor(six(b["r1"][:]), turned(p["p23"][:]), cos, ALU.mult).then_inc(s["rk1"], 1)
                    dve.tensor_tensor(six(b["r2"][:]), turned(p["p45"][:]), sin, ALU.mult).then_inc(s["rk2"], 1)
                    dve.wait_ge(s["rk1"], A)
                    dve.wait_ge(s["rk2"], A)
                    dve.tensor_tensor(b["kT"][:], b["r1"][:], b["r2"][:], ALU.add).then_inc(s["kT"], 1)
                if B is not None:
                    dve.wait_ge(s["ct_ps"], B)
                    dve.tensor_copy(packed(b["CT"][:, 3:6, :]), slots(p["p67"][:, 512:512 + 384], 3)).then_inc(s["CT1"], 1)
                    dve.wait_ge(s["wo_ps"], B)
                    dve.wait_ge(s["hb"], B)
                    dve.tensor_tensor(b["y"][:], p["p0"][0:PAIR, 0:WIDTH], b["hb"][:], ALU.add).then_inc(s["y"], 1)
                    dve.wait_ge(s["y"], B)
                    dve.bn_stats(b["st2"][:], b["y"][:]).then_inc(s["st2"], 1)
                    dve.wait_ge(s["imm"], 1)
                    dve.wait_ge(s["st2"], B)
                    dve.bn_aggr(b["mv2"][:], b["st2"][:]).then_inc(s["mv2"], 1)
                    dve.wait_ge(s["mv2"], B)
                    dve.tensor_scalar(b["ve2"][:], b["mv2"][:, 1:2], 1e-5, None, ALU.add).then_inc(s["ve2"], 1)
                if A is not None:
                    dve.wait_ge(s["s_ps"], A)
                    dve.tensor_tensor(b["E"][:], heads_of(p["p67"][:]), mask, ALU.add).then_inc(s["masked"], 1)
                    dve.wait_ge(s["masked"], A)
                    dve.tensor_reduce(b["mx"][:], b["E"][:], AX.X, ALU.max).then_inc(s["mx"], 1)
                    dve.wait_ge(s["mx"], A)
                    dve.tensor_tensor(b["E"][:], b["E"][:], b["mx"][:].unsqueeze(3).to_broadcast([128, 2, NI, PATCHES]), ALU.subtract).then_inc(s["shifted"], 1)
                if B is not None:
                    dve.wait_ge(s["rstd2"], B)
                    dve.wait_ge(s["X"], B - 1)
                    dve.wait_ge(s["stored"], (B - 1) * 16)
                    dve.tensor_scalar(b["xn"][:], b["y"][:], b["mv2"][:, 0:1], b["rstd2"][:], ALU.subtract, ALU.mult).then_inc(s["xn"], 1)

            steps(dve, step)

        @block.scalar
        def _(act):
            act.preload_act_table(ACT.Exp)

            def step(A, B, T):
                if T is not None:
                    act.wait_ge(s["x_ps"], T)
                    act.activation(keep["XT"][0:HALF, :, bass.ds((T - 2) * PAIR, PAIR)], p["p1"][0:HALF, 0:2 * PAIR].rearrange("p (c r) -> p c r", c=2),
                                   ACT.Copy).then_inc(s["xT"], 1)
                    act.activation(keep["X"][:, bass.ds(T - 2, 1), :], b["xn"][:].unsqueeze(1), ACT.Copy).then_inc(s["X"], 1)
                if A is not None:
                    act.wait_ge(s["hT_ps"], A)
                    act.activation(b["hT"][:], p["p1"][0:HALF, 0:2 * PAIR].rearrange("p (c r) -> p c r", c=2), ACT.Copy).then_inc(s["hT"], 1)
                if B is not None:
                    act.wait_ge(s["pt_ps"], B)
                    act.activation(b["PT"][:, 0, :, :], p["p67"][:, 0:NI * SLOT].rearrange("p (i r) -> p i r", i=NI), ACT.Copy).then_inc(s["PT0"], 1)
                    act.wait_ge(s["ct_ps"], B)
                    act.activation(packed(b["CT"][:, 0:3, :]), slots(p["p67"][:, 0:384], 3), ACT.Copy).then_inc(s["CT0"], 1)
                if A is not None:
                    for im, ps, ready, sem in ((1, p["p1"], s["v1_ps"], s["V1"]), (0, p["p0"], s["v0_ps"], s["V0"])):
                        act.wait_ge(ready, A)
                        act.activation(b["V"][:, im, :, :], ps[:, 0:NI * HD0].rearrange("p (i d) -> p i d", i=NI), ACT.Copy).then_inc(sem, 1)
                    act.wait_ge(s["shifted"], A)
                    act.activation(b["P"][:, :, :, 0:PATCHES].rearrange("p i a r -> p a i r"), b["E"][:], ACT.Exp, scale=HD0 ** -0.5).then_inc(s["P"], 1)

            steps(act, step)

        @block.gpsimd
        def _(pool):
            pool.sem_inc(s["imm"], 1)
            pool.wait_ge(s["weights"], 16 * len(loads))

            def step(A, B, T):
                if A is not None:
                    pool.wait_ge(s["ve"], A)
                    pool.tensor_tensor(b["rstd"][:], b["ve"][:], keep["half"][:], ALU.pow).then_inc(s["rstd"], 1)
                if B is not None:
                    pool.wait_ge(s["ve2"], B)
                    pool.tensor_tensor(b["rstd2"][:], b["ve2"][:], keep["half"][:], ALU.pow).then_inc(s["rstd2"], 1)
                if A is not None:
                    pool.wait_ge(s["h"], A)
                    pool.wait_ge(s["y"], A - 1)
                    pool.tensor_tensor(b["hb"][:], b["hs"][:], b["bo"][:], ALU.add).then_inc(s["hb"], 1)

            steps(pool, step)




def block_router_and_shared_expert(nc, d, keep):
    with ExitStack() as ctx:
        NS = SHARED // FC
        b = buffers(
            ctx, nc, "rt", wg=(HALF, 2, EXPERTS), ebias=(PAIR, EXPERTS), before=(PAIR, PAIR), ones=(PAIR, PAIR), slot0=(PAIR, EXPERTS),
            wsg=(HALF, 2, SHARED), wsu=(HALF, 2, SHARED), wsd=(FC, NS, WIDTH), xs=(HALF, 2, PAIR), sig=(PAIR, EXPERTS),
            choice=(PAIR, EXPERTS + 2), m8=(PAIR, 8), left=(PAIR, EXPERTS + 2), mask=(PAIR, EXPERTS), pos=(PAIR, EXPERTS),
            run=(PAIR, EXPERTS), wm=(PAIR, EXPERTS), sm=(PAIR, 1), sm1=(PAIR, 1), rs=(PAIR, 1), rs25=(PAIR, 1), sel=(PAIR, EXPERTS),
            far=(PAIR, EXPERTS), row=(PAIR, EXPERTS), row2=(PAIR, EXPERTS), code=(PAIR, EXPERTS), wsel=(PAIR, EXPERTS), s8=(PAIR, 8),
            hit=(PAIR, TOPK, EXPERTS), w6=(PAIR, TOPK), none=(PAIR, 8), sg=(FC, NS, PAIR), inter=(FC, NS, PAIR))
        into = ctx.enter_context(nc.sbuf_tensor("rt_into", [PAIR, 8], I32))
        tokens = ctx.enter_context(nc.sbuf_tensor("rt_tokens", [PAIR, TURNS], I32))
        token = ctx.enter_context(nc.sbuf_tensor("rt_token", [PAIR, 1], I32))
        zeros = ctx.enter_context(nc.sbuf_tensor("rt_zeros", [CAPH, 2 * EXPERTS], I32))
        p = banks(ctx, nc, "rt", p0=512, p1=512, p23=1024, p45=1024, p6=512, p7=512)
        s = signals(
            ctx, nc, "rt", "xs logits sig choice top8 top6 left mask pos_ps pos run wm sm rs rs25 sel far row "
            "row2 code wsel s8 w6 none into rows token landed kept g_ps u_ps sg inter out_ps Y", setup="imm weights start zeros cleared scattered")
        loads = [(b["wg"], d["wg"]), (b["ebias"], d["e_bias"]), (b["before"], d["before"]), (b["ones"], d["ones"]), (b["slot0"], d["slot0"]), (b["wsg"], d["wsg"]),
                 (b["wsu"], d["wsu"]), (b["wsd"], d["wsd"]), (tokens, d["token"])]
        block = ctx.enter_context(nc.Block())

        @block.sync
        def _(sp):
            for to, src in loads:
                sp.dma_start(to[:], src).then_inc(s["weights"], 16)
            sp.wait_ge(s["zeros"], 1)
            sp.dma_start(d["slot_token"], zeros[:]).then_inc(s["cleared"], 16)
            sp.wait_ge(s["cleared"], 16)

        @block.scalar
        def _(act):
            with act.Fori(2, TURNS + 2) as n:
                m, t = n - 1, n - 2
                act.wait_ge(s["out_ps"], m)
                act.activation(b["xs"][:], keep["XT"][0:HALF, :, bass.ds(t * PAIR, PAIR)], ACT.Copy).then_inc(s["xs"], 1)
                act.wait_ge(s["logits"], n)
                act.wait_ge(s["wsel"], m)
                act.activation(b["sig"][:], p["p0"][0:PAIR, 0:EXPERTS], ACT.Sigmoid).then_inc(s["sig"], 1)
                act.wait_ge(s["g_ps"], n)
                act.wait_ge(s["inter"], m)
                act.activation(b["sg"][:].rearrange("p (u j) r -> p u j r", u=2),
                               p["p23"][0:FC, :].rearrange("p (u c) -> p u c", u=2)[:, :, 0:4 * PAIR].rearrange("p u (j r) -> p u j r", j=4),
                               ACT.Silu).then_inc(s["sg"], 1)

        @block.tensor
        def _(pe):
            pe.wait_ge(s["weights"], 16 * len(loads))
            with pe.Fori(2, TURNS + 2) as n:
                m, t = n - 1, n - 2
                pe.wait_ge(s["xs"], n)
                pe.wait_ge(s["sig"], m)
                for c in range(2):
                    mm = pe.matmul(p["p0"][0:PAIR, 0:EXPERTS], b["xs"][:, c, :], b["wg"][:, c, :], start=c == 0, stop=c == 1)
                mm.then_inc(s["logits"], 1)
                for w, ps, free, sem in ((b["wsg"], p["p23"], s["sg"], s["g_ps"]), (b["wsu"], p["p45"], s["inter"], s["u_ps"])):
                    pe.wait_ge(free, m)
                    for j in range(NS):
                        at = (j // 4) * 512 + (j % 4) * PAIR
                        for c in range(2):
                            mm = pe.matmul(ps[0:FC, at:at + PAIR], w[:, c, j * FC:(j + 1) * FC], b["xs"][:, c, :], start=c == 0, stop=c == 1)
                    mm.then_inc(sem, 1)
                pe.wait_ge(s["mask"], n)
                pe.wait_ge(s["run"], m)
                pe.matmul(p["p1"][0:PAIR, 0:EXPERTS], b["before"][:], b["mask"][:], start=True, stop=True)
                pe.matmul(p["p1"][0:PAIR, EXPERTS:2 * EXPERTS], b["ones"][:], b["mask"][:], start=True, stop=True).then_inc(s["pos_ps"], 1)
                pe.wait_ge(s["inter"], n)
                pe.wait_ge(s["Y"], m)
                for j in range(NS):
                    mm = pe.matmul(p["p6"][0:PAIR, 0:WIDTH], b["inter"][:, j, :], b["wsd"][:, j, :], start=j == 0, stop=j == NS - 1)
                mm.then_inc(s["out_ps"], 1)

        @block.vector
        def _(dve):
            dve.memset(zeros[:], 0).then_inc(s["zeros"], 1)
            dve.memset(b["choice"][:, EXPERTS:], -BIG).then_inc(s["start"], 1)
            dve.memset(b["run"][:], 0.0).then_inc(s["start"], 1)
            dve.wait_ge(s["start"], 2)
            dve.wait_ge(s["weights"], 16 * len(loads))
            with dve.Fori(2, TURNS + 2) as n:
                m, t = n - 1, n - 2
                dve.wait_ge(s["sig"], n)
                dve.tensor_tensor(b["choice"][:, 0:EXPERTS], b["sig"][:], b["ebias"][:], ALU.add).then_inc(s["choice"], 1)
                dve.wait_ge(s["imm"], 1)
                dve.wait_ge(s["choice"], n)
                dve.max(b["m8"][:], b["choice"][:]).then_inc(s["top8"], 1)
                dve.wait_ge(s["top8"], n)
                dve.memset(b["m8"][:, TOPK:8], -BIG).then_inc(s["top6"], 1)
                dve.wait_ge(s["imm"], 1)
                dve.wait_ge(s["top6"], n)
                dve.match_replace(b["left"][:], b["m8"][:], b["choice"][:], -2 * BIG).then_inc(s["left"], 1)
                dve.wait_ge(s["left"], n)
                dve.wait_ge(s["pos_ps"], m)
                dve.tensor_tensor(b["mask"][:], b["left"][:, 0:EXPERTS], b["choice"][:, 0:EXPERTS], ALU.not_equal).then_inc(s["mask"], 1)
                dve.wait_ge(s["mask"], n)
                dve.tensor_tensor_reduce(b["wm"][:], b["sig"][:], b["mask"][:], 1.0, 0.0, ALU.mult, ALU.add, b["sm"][:]).then_inc(s["wm"], 1)
                dve.wait_ge(s["wm"], n)
                dve.tensor_scalar(b["sm1"][:], b["sm"][:], 1e-20, None, ALU.add).then_inc(s["sm"], 1)
                dve.wait_ge(s["sm"], n)
                dve.reciprocal(b["rs"][:], b["sm1"][:]).then_inc(s["rs"], 1)
                dve.wait_ge(s["rs"], n)
                dve.tensor_scalar(b["rs25"][:], b["rs"][:], 2.5, None, ALU.mult).then_inc(s["rs25"], 1)
                dve.wait_ge(s["pos_ps"], n)
                dve.tensor_tensor(b["pos"][:], p["p1"][0:PAIR, 0:EXPERTS], b["run"][:], ALU.add).then_inc(s["pos"], 1)
                dve.wait_ge(s["pos"], n)
                dve.tensor_tensor(b["run"][:], p["p1"][0:PAIR, EXPERTS:2 * EXPERTS], b["run"][:], ALU.add).then_inc(s["run"], 1)
                dve.scalar_tensor_tensor(b["sel"][:], b["pos"][:], float(CAP), b["mask"][:], ALU.is_lt, ALU.mult).then_inc(s["sel"], 1)
                dve.tensor_scalar(b["far"][:], b["pos"][:], float(CAPH), -float(CAPH * 2 * EXPERTS - 1), ALU.is_ge, ALU.mult).then_inc(s["far"], 1)
                dve.scalar_tensor_tensor(b["row"][:], b["pos"][:], 2.0 * EXPERTS, b["slot0"][:], ALU.mult, ALU.add).then_inc(s["row"], 1)
                dve.wait_ge(s["far"], n)
                dve.wait_ge(s["row"], n)
                dve.tensor_tensor(b["row2"][:], b["row"][:], b["far"][:], ALU.add).then_inc(s["row2"], 1)
                dve.wait_ge(s["row2"], n)
                dve.wait_ge(s["sel"], n)
                dve.scalar_tensor_tensor(b["code"][:], b["row2"][:], 1.0, b["sel"][:], ALU.add, ALU.mult).then_inc(s["code"], 1)
                dve.wait_ge(s["rs25"], n)
                dve.scalar_tensor_tensor(b["wsel"][:], b["wm"][:], b["rs25"][:], b["sel"][:], ALU.mult, ALU.mult).then_inc(s["wsel"], 1)
                dve.wait_ge(s["imm"], 1)
                dve.wait_ge(s["code"], n)
                dve.max(b["s8"][:], b["code"][:]).then_inc(s["s8"], 1)
                dve.wait_ge(s["s8"], n)
                dve.wait_ge(s["wsel"], n)
                dve.wait_ge(s["kept"], m)
                for k in range(TOPK):
                    ins = dve.scalar_tensor_tensor(b["hit"][:, k, :], b["code"][:], b["s8"][:, k:k + 1], b["wsel"][:], ALU.is_equal, ALU.mult,
                                                   accum_out=b["w6"][:, k:k + 1])
                ins.then_inc(s["w6"], 1)
                dve.tensor_scalar(b["none"][:], b["s8"][:], 0.0, 1.0e6, ALU.is_equal, ALU.mult).then_inc(s["none"], 1)
                dve.wait_ge(s["none"], n)
                dve.wait_ge(s["landed"], m)
                dve.scalar_tensor_tensor(into[:], b["s8"][:], -1.0, b["none"][:], ALU.add, ALU.add).then_inc(s["into"], 1)
                dve.tensor_scalar(keep["rows"][:, t, :], b["s8"][:], -1.0, 0.0, ALU.add, ALU.max).then_inc(s["rows"], 1)
                dve.wait_ge(s["sg"], n)
                dve.wait_ge(s["u_ps"], n)
                dve.wait_ge(s["out_ps"], m)
                dve.tensor_tensor(b["inter"][:].rearrange("p (u j) r -> p u j r", u=2),
                                  p["p45"][0:FC, :].rearrange("p (u c) -> p u c", u=2)[:, :, 0:4 * PAIR].rearrange("p u (j r) -> p u j r", j=4),
                                  b["sg"][:].rearrange("p (u j) r -> p u j r", u=2), ALU.mult).then_inc(s["inter"], 1)
                dve.wait_ge(s["out_ps"], n)
                dve.tensor_tensor(keep["Y"][:, t, :], p["p6"][0:PAIR, 0:WIDTH], keep["X"][:, t, :], ALU.add).then_inc(s["Y"], 1)

        @block.gpsimd
        def _(pool):
            pool.sem_inc(s["imm"], 1)
            pool.wait_ge(s["weights"], 16 * len(loads))
            pool.wait_ge(s["cleared"], 16)
            with pool.Fori(2, TURNS + 2) as n:
                m, t = n - 1, n - 2
                pool.tensor_copy(token[:], tokens[:, bass.ds(t, 1)]).then_inc(s["token"], 1)
                pool.wait_ge(s["imm"], 1)
                pool.wait_ge(s["w6"], n)
                pool.tensor_copy(keep["w6"][:, t, :], b["w6"][:]).then_inc(s["kept"], 1)
                pool.wait_ge(s["imm"], 1)
                pool.wait_ge(s["into"], n)
                pool.wait_ge(s["token"], n)
                for k in range(TOPK):
                    pool.indirect_dma_start(d["slot_token_rows"], bass.IndirectOffsetOnAxis(ap=into[:, k:k + 1], axis=0), token[:], None,
                                            bounds_check=ROWS - 1, oob_is_err=False).then_inc(s["scattered"], 16)
                pool.wait_ge(s["scattered"], 16 * TOPK * m)
                pool.sem_inc(s["landed"], 1)
            pool.wait_ge(s["scattered"], 16 * TOPK * TURNS)


def block_routed_experts(nc, d, keep):
    with ExitStack() as ctx:
        b = buffers(ctx, nc, "ex", wgu=(HALF, 2, 2, 2 * INTER), wdn=(FC, 2, NF, WIDTH), xe=(CAPH, 2, WIDTH), xT=(HALF, 2, CAP),
                    sg=(FC, NF, CAP), inter=(FC, NF, CAP), ys=(CAPH, 2, WIDTH))
        ids = ctx.enter_context(nc.sbuf_tensor("ex_ids", [CAPH, 2 * EXPERTS + 2], I32))
        idc = ctx.enter_context(nc.sbuf_tensor("ex_idc", [CAPH, 2], I32))
        p = banks(ctx, nc, "ex", pT=512, gu=2048, y=512)
        s = signals(ctx, nc, "ex", "idc x_ps xT gu0 gu1 gu2 gu3 sg0 sg1 sg2 sg3 in0 in1 in2 in3 y_ps ys", dma="stored", setup="pad ids w0 w1 xe")
        gu, sg, inter, w = (s["gu0"], s["gu1"], s["gu2"], s["gu3"]), (s["sg0"], s["sg1"], s["sg2"], s["sg3"]), (s["in0"], s["in1"], s["in2"], s["in3"]), (s["w0"], s["w1"])
        block = ctx.enter_context(nc.Block())

        def load(sp, e, u):
            sp.dma_start(b["wgu"][:, u], d["wgu"][e]).then_inc(w[u], 16)
            sp.dma_start(b["wdn"][:, u], d["wdn"][e]).then_inc(w[u], 16)

        @block.sync
        def _(sp):
            sp.wait_ge(s["pad"], 1)
            sp.dma_start(ids[:, 0:2 * EXPERTS], d["slot_token"]).then_inc(s["ids"], 16)
            for u in range(2):
                load(sp, u, u)
            def store(e):
                sp.wait_ge(s["pad"], 1)
                sp.wait_ge(s["ys"], e + 2)
                sp.dma_start(d["slot_out"][:, bass.ds(2 * e, 2), :], b["ys"][:]).then_inc(s["stored"], 16)

            with sp.Fori(0, EXPERTS // 2 - 1) as i:
                for u in range(2):
                    store(2 * i + u)
                    load(sp, 2 * i + u + 2, u)
            for u in range(2):
                store(EXPERTS - 2 + u)
            sp.wait_ge(s["stored"], 16 * (EXPERTS + 1))

        @block.gpsimd
        def _(pool):
            pool.memset(ids[:, 2 * EXPERTS:], 0).then_inc(s["pad"], 1)
            pool.wait_ge(s["ids"], 16)
            with pool.Fori(2, EXPERTS + 3) as n:
                e = n - 2
                pool.wait_ge(s["pad"], 1)
                pool.wait_ge(s["x_ps"], n - 1)
                pool.tensor_copy(idc[:], ids[:, bass.ds(2 * e, 2)]).then_inc(s["idc"], 1)
                pool.wait_ge(s["pad"], 1)
                pool.wait_ge(s["idc"], n)
                for h in range(2):
                    pool.indirect_dma_start(b["xe"][:, h, :], None, d["x_flat"], bass.IndirectOffsetOnAxis(ap=idc[:, h:h + 1], axis=0),
                                            bounds_check=TOKENS - 1, oob_is_err=False).then_inc(s["xe"], 16)
            pool.wait_ge(s["xe"], 32 * (EXPERTS + 1))

        @block.tensor
        def _(pe):
            def turn_rows(e):
                pe.wait_ge(s["xe"], 32 * (e + 1))
                pe.wait_ge(s["xT"], e + 1)
                for h in range(2):
                    for c in range(2):
                        mm = pe.transpose(p["pT"][0:HALF, c * CAP + h * CAPH:c * CAP + (h + 1) * CAPH], b["xe"][:, h, c * HALF:(c + 1) * HALF],
                                          keep["ident"][0:CAPH, 0:CAPH])
                mm.then_inc(s["x_ps"], 1)

            turn_rows(0)
            with pe.Fori(0, EXPERTS // 2) as i:
                for u in range(2):
                    e = 2 * i + u
                    pe.wait_ge(w[u], 32 * (i + 1))
                    pe.wait_ge(s["xT"], e + 2)
                    for f in range(NF):
                        pe.wait_ge(inter[f], e + 1)
                        for half in range(2):
                            for c in range(2):
                                mm = pe.matmul(p["gu"][0:FC, 512 * f + half * CAP:512 * f + (half + 1) * CAP],
                                               b["wgu"][:, u, c, half * INTER + f * FC:half * INTER + (f + 1) * FC], b["xT"][:, c, :],
                                               start=c == 0, stop=c == 1)
                        mm.then_inc(gu[f], 1)
                    turn_rows(e + 1)
                    pe.wait_ge(s["ys"], e + 1)
                    for f in range(NF):
                        pe.wait_ge(inter[f], e + 2)
                    for h in range(2):
                        for f in range(NF):
                            mm = pe.matmul(p["y"][0:CAPH, h * WIDTH:(h + 1) * WIDTH], b["inter"][:, f, h * CAPH:(h + 1) * CAPH], b["wdn"][:, u, f, :],
                                           start=f == 0, stop=f == NF - 1)
                    mm.then_inc(s["y_ps"], 1)

        @block.scalar
        def _(act):
            with act.Fori(2, EXPERTS + 2) as n:
                for f in range(NF):
                    act.wait_ge(gu[f], n)
                    act.wait_ge(inter[f], n - 1)
                    act.activation(b["sg"][:, f, :], p["gu"][0:FC, 512 * f:512 * f + CAP], ACT.Silu).then_inc(sg[f], 1)
                act.wait_ge(s["y_ps"], n)
                act.wait_ge(s["stored"], 16 * (n - 1))
                act.activation(b["ys"][:].rearrange("p h w -> p (h w)"), p["y"][0:CAPH, 0:2 * WIDTH], ACT.Copy).then_inc(s["ys"], 1)

        @block.vector
        def _(dve):
            def turned(n):
                dve.wait_ge(s["x_ps"], n)
                dve.tensor_copy(b["xT"][:].rearrange("p c r -> p (c r)"), p["pT"][0:HALF, 0:2 * CAP]).then_inc(s["xT"], 1)

            turned(2)
            with dve.Fori(2, EXPERTS + 2) as n:
                dve.wait_ge(s["y_ps"], n - 1)
                for f in range(NF):
                    dve.wait_ge(sg[f], n)
                    dve.tensor_tensor(b["inter"][:, f, :], p["gu"][0:FC, 512 * f + CAP:512 * f + 2 * CAP], b["sg"][:, f, :], ALU.mult).then_inc(inter[f], 1)
                turned(n + 1)


def block_combine(nc, d, keep):
    with ExitStack() as ctx:
        b = buffers(ctx, nc, "cb", G=(PAIR, TOPK, WIDTH), w6=(PAIR, TOPK), a=(PAIR, TOPK, WIDTH), st=(PAIR, 6), mv=(PAIR, 2), ve=(PAIR, 1),
                    rstd=(PAIR, 1), xn=(PAIR, WIDTH))
        rows = ctx.enter_context(nc.sbuf_tensor("cb_rows", [PAIR, 8], I32))
        p = banks(ctx, nc, "cb", p1=512)
        s = signals(ctx, nc, "cb", "rows w6 a0 a1 a2 a3 a4 a5 st mv ve rstd xn x_ps xT X", setup="imm g0 g1 g2 g3 g4 g5")
        got, added = (s["g0"], s["g1"], s["g2"], s["g3"], s["g4"], s["g5"]), (s["a0"], s["a1"], s["a2"], s["a3"], s["a4"], s["a5"])
        block = ctx.enter_context(nc.Block())

        @block.gpsimd
        def _(pool):
            pool.sem_inc(s["imm"], 1)
            with pool.Fori(2, TURNS + 2) as n:
                m, t = n - 1, n - 2
                pool.wait_ge(s["imm"], 1)
                pool.wait_ge(s["a5"], m)
                pool.tensor_copy(rows[:], keep["rows"][:, t, :]).then_inc(s["rows"], 1)
                for k in range(TOPK):
                    pool.wait_ge(s["imm"], 1)
                    pool.wait_ge(s["rows"], n)
                    pool.indirect_dma_start(b["G"][:, k, :], None, d["slot_out_rows"], bass.IndirectOffsetOnAxis(ap=rows[:, k:k + 1], axis=0),
                                            bounds_check=ROWS - 1, oob_is_err=False).then_inc(got[k], 16)
                pool.wait_ge(s["ve"], n)
                pool.tensor_tensor(b["rstd"][:], b["ve"][:], keep["half"][:], ALU.pow).then_inc(s["rstd"], 1)

        @block.scalar
        def _(act):
            with act.Fori(2, TURNS + 2) as n:
                m, t = n - 1, n - 2
                act.wait_ge(s["a5"], m)
                act.activation(b["w6"][:], keep["w6"][:, t, :], ACT.Copy).then_inc(s["w6"], 1)
                act.wait_ge(s["x_ps"], n)
                act.activation(keep["XT"][0:HALF, :, bass.ds(t * PAIR, PAIR)], p["p1"][0:HALF, 0:2 * PAIR].rearrange("p (c r) -> p c r", c=2),
                               ACT.Copy).then_inc(s["xT"], 1)
                act.activation(keep["X"][:, t, :], b["xn"][:], ACT.Copy).then_inc(s["X"], 1)

        @block.tensor
        def _(pe):
            with pe.Fori(2, TURNS + 2) as n:
                pe.wait_ge(s["imm"], 1)
                pe.wait_ge(s["xn"], n)
                pe.wait_ge(s["xT"], n - 1)
                for c in range(2):
                    mm = pe.transpose(p["p1"][0:HALF, c * PAIR:(c + 1) * PAIR], b["xn"][:, c * HALF:(c + 1) * HALF], keep["ident"][0:PAIR, 0:PAIR])
                mm.then_inc(s["x_ps"], 1)

        @block.vector
        def _(dve):
            with dve.Fori(2, TURNS + 2) as n:
                m, t = n - 1, n - 2
                dve.wait_ge(s["w6"], n)
                for k in range(TOPK):
                    dve.wait_ge(got[k], 16 * m)
                    if k:
                        dve.wait_ge(added[k - 1], n)
                    before = b["a"][:, k - 1, :] if k else keep["Y"][:, t, :]
                    dve.scalar_tensor_tensor(b["a"][:, k, :], b["G"][:, k, :], b["w6"][:, k:k + 1], before, ALU.mult, ALU.add).then_inc(added[k], 1)
                dve.wait_ge(s["a5"], n)
                dve.bn_stats(b["st"][:], b["a"][:, 5, :]).then_inc(s["st"], 1)
                dve.wait_ge(s["imm"], 1)
                dve.wait_ge(s["st"], n)
                dve.bn_aggr(b["mv"][:], b["st"][:]).then_inc(s["mv"], 1)
                dve.wait_ge(s["mv"], n)
                dve.tensor_scalar(b["ve"][:], b["mv"][:, 1:2], 1e-5, None, ALU.add).then_inc(s["ve"], 1)
                dve.wait_ge(s["rstd"], n)
                dve.wait_ge(s["X"], m)
                dve.tensor_scalar(b["xn"][:], b["a"][:, 5, :], b["mv"][:, 0:1], b["rstd"][:], ALU.subtract, ALU.mult).then_inc(s["xn"], 1)


def norm(dve, b, s, n, prev, y, eps, to, free=()):
    dve.wait_ge(s["y"], n)
    dve.bn_stats(b["st"][:], y).then_inc(s["st"], 1)
    dve.wait_ge(s["imm"], 1)
    dve.wait_ge(s["st"], n)
    dve.bn_aggr(b["mv"][:], b["st"][:]).then_inc(s["mv"], 1)
    dve.wait_ge(s["mv"], n)
    dve.tensor_scalar(b["ve"][:], b["mv"][:, 1:2], eps, None, ALU.add).then_inc(s["ve"], 1)
    dve.wait_ge(s["rstd"], n)
    for sem in free:
        dve.wait_ge(sem, prev)
    return dve.tensor_scalar(to, y, b["mv"][:, 0:1], b["rstd"][:], ALU.subtract, ALU.mult)


def pool_rstd(pool, b, s, n, keep):
    pool.wait_ge(s["ve"], n)
    pool.tensor_tensor(b["rstd"][:], b["ve"][:], keep["half"][:], ALU.pow).then_inc(s["rstd"], 1)


def block_bert(nc, d, keep):
    with ExitStack() as ctx:
        b = buffers(
            ctx, nc, "ba", wq=(HALF + 1, 2, WIDTH), wk=(HALF + 1, 2, WIDTH), wc=(HALF + 1, 2, WIDTH), wv=(HALF + 1, 2, WIDTH),
            wo=(HALF, 2, WIDTH), rows=(PAIR, 6, WIDTH), own=(HALF, NI), block16=(HALF, HALF), eye=(128, PATCHES),
            xs=(HALF + 1, 2, 128), hb=(PAIR, WIDTH), qT=(HALF, 2, 128), kd=(HALF, 2, NI, PAIR), c=(HALF, 2, PAIR), c2=(HALF, 2, PAIR),
            n2=(HALF, 2 * PAIR), rn=(HALF, 2 * PAIR), cT=(HALF, 2, 128), cd=(HALF, 2, NI, PAIR), V=(128, 2, NI, 16),
            E1=(128, 2, NI, PATCHES), E2=(128, 2, NI, PATCHES), mx=(128, 2, NI), z1=(128, 2, NI), z2=(128, 2, NI), rz1=(128, 2, NI),
            rz2=(128, 2, NI), P=(128, NI, 2, SLOT), PT=(128, 2, NI, SLOT), C=(128, 2, HALF), CT=(HALF, 2, PAIR), y=(PAIR, WIDTH),
            st=(PAIR, 6), mv=(PAIR, 2), ve=(PAIR, 1), rstd=(PAIR, 1), yn=(PAIR, WIDTH), yg=(PAIR, WIDTH), xn=(PAIR, WIDTH))
        f = buffers(
            ctx, nc, "bf", wi=(HALF + 1, 2, FFN), wo2=(128, NFF, WIDTH), h=(128, NFF, GCOLS), hb=(PAIR, GROUP, WIDTH),
            y=(PAIR, GROUP, WIDTH), st=(PAIR, GROUP, 6), mv=(PAIR, GROUP, 2), ve=(PAIR, GROUP), rstd=(PAIR, GROUP),
            yn=(PAIR, GROUP, WIDTH), yg=(PAIR, GROUP, WIDTH), xn=(PAIR, GROUP, WIDTH))
        p = banks(ctx, nc, "ba", p0=512, p1=512, p2=512, p3=512, p45=1024, p67=1024)
        s = signals(
            ctx, nc, "ba", "xs hb q_ps k_ps c_ps v_ps qT kd c c2 n2_ps n2 rn cT cd V s1_ps s2_ps mx "
            "shifted E2 E1 E1x z1 z2 rz1 rz2 P1 P2 P pt_ps PT0 PT1 ctx_ps C ct_ps CT wo_ps y st mv ve rstd yn yg xn x_ps xT X",
            setup="imm consts pads saved attn_w")
        g = signals(ctx, nc, "bf", "h0 h1 h2 h3 h4 h5 a0 a1 a2 a3 a4 a5 hb out_ps y st mv ve rstd yn yg xn x_ps0 x_ps1 xT0 xT1 X",
                    setup="ffn_w")
        h_ps, h_sb = (g["h0"], g["h1"], g["h2"], g["h3"], g["h4"], g["h5"]), (g["a0"], g["a1"], g["a2"], g["a3"], g["a4"], g["a5"])
        x_ps, xT = (g["x_ps0"], g["x_ps1"]), (g["xT0"], g["xT1"])
        h_bank = [p["p0"][:], p["p1"][:], p["p2"][:], p["p3"][:], p["p45"][:, 0:512], p["p45"][:, 512:1024]]
        consts = [(b["own"], d["own"]), (b["block16"], d["block16"]), (b["eye"], d["eye"])]
        AW, FW = 6, 2
        block = ctx.enter_context(nc.Block())

        def attention_steps(engine, l, step):
            first, last = TURNS * (l - 1) + 2, TURNS * l + 1
            step(first, None, None, first - 1, 0)
            step(first + 1, first, None, first - 1, 1)
            with engine.Fori(2, TURNS) as q:
                n = TURNS * (l - 1) + q + 2
                step(n, n - 1, n - 2, n - 2, q)
            step(None, last, last - 1, last - 1, TURNS)
            step(None, None, last, last, TURNS + 1)

        def mlp_steps(engine, l, step):
            first = GROUPS * (l - 1) + 2
            step(first, None, 0)
            with engine.Fori(1, GROUPS) as q:
                n = GROUPS * (l - 1) + q + 2
                step(n, n - 1, q)
            step(None, GROUPS * l + 1, GROUPS)

        @block.sync
        def _(sp):
            for to, src in consts:
                sp.dma_start(to[:], src).then_inc(s["consts"], 16)

            def load_attention(l):
                for to, src in ((b["wq"], d["bwq"]), (b["wk"], d["bwk"]), (b["wc"], d["bwc"]), (b["wv"], d["bwv"]), (b["wo"], d["bwo"]), (b["rows"], d["brows"])):
                    sp.dma_start(to[:], src[l]).then_inc(s["attn_w"], 16)

            def load_ffn(l):
                for to, src in ((f["wi"], d["bwi"]), (f["wo2"], d["bwo2"])):
                    sp.dma_start(to[:], src[l]).then_inc(g["ffn_w"], 16)

            load_attention(0)
            load_ffn(0)
            with sp.Fori(1, LAYERS) as l:
                sp.wait_ge(s["imm"], 1)
                sp.wait_ge(g["xn"], l * GROUPS + 1)
                load_attention(l)
                sp.wait_ge(g["out_ps"], l * TURNS + 1)
                load_ffn(l)

        @block.tensor
        def _(pe):
            pe.wait_ge(s["consts"], 16 * len(consts))
            pe.wait_ge(s["pads"], 5)

            def project(w, ps, sem):
                for a in range(2):
                    for c in range(2):
                        K = HALF + c
                        mm = pe.matmul(ps[0:HALF, a * PAIR:(a + 1) * PAIR], w[0:K, c, a * HALF:(a + 1) * HALF], b["xs"][0:K, c, 0:PAIR],
                                       start=c == 0, stop=c == 1)
                mm.then_inc(sem, 1)

            def values(im):
                for a in range(2):
                    for c in range(2):
                        K = HALF + c
                        mm = pe.matmul(p["p3"][64 * a:64 * a + 64, im * HALF:(im + 1) * HALF], b["xs"][0:K, c, PATCHES * im:PATCHES * im + SLOT],
                                       b["wv"][0:K, c, a * HALF:(a + 1) * HALF], start=c == 0, stop=c == 1)
                return mm

            def scores(ps, left, right, sem):
                for im in range(2):
                    for a in range(2):
                        mm = pe.matmul(ps[64 * im:64 * im + 64, 512 * a:512 * a + NI * PATCHES], left[:, a, PATCHES * im:PATCHES * im + SLOT],
                                       right[:, a, :, PATCHES * im:PATCHES * (im + 1)], start=True, stop=True)
                mm.then_inc(sem, 1)

            def attention(A, B, T, old, q):
                if A is not None:
                    pe.wait_ge(s["xs"], A)
                    pe.wait_ge(s["n2"], A - 1)
                    project(b["wc"], p["p2"], s["c_ps"])
                    pe.wait_ge(s["CT"], old)
                    project(b["wq"], p["p0"], s["q_ps"])
                    pe.wait_ge(s["y"], old)
                    project(b["wk"], p["p1"], s["k_ps"])
                if T is not None:
                    pe.wait_ge(s["imm"], 1)
                    pe.wait_ge(s["xn"], T)
                    pe.wait_ge(s["V"], T if B is None else B)
                    for c in range(2):
                        mm = pe.transpose(p["p3"][0:HALF, c * PAIR:(c + 1) * PAIR], b["xn"][:, c * HALF:(c + 1) * HALF], keep["ident"][0:PAIR, 0:PAIR])
                    mm.then_inc(s["x_ps"], 1)
                if A is not None:
                    pe.wait_ge(s["c2"], A)
                    pe.wait_ge(s["c"], A)
                    pe.matmul(p["p2"][0:HALF, 0:2 * PAIR], b["block16"][:], b["c2"][:].rearrange("p c r -> p (c r)"), start=True, stop=True).then_inc(s["n2_ps"], 1)
                if B is not None:
                    pe.wait_ge(s["imm"], 1)
                    pe.wait_ge(s["P"], B)
                    for im in range(2):
                        rows = slice(64 * im, 64 * im + 64)
                        for i in range(NI):
                            mm = pe.transpose(p["p45"][:, 512 * im + i * SLOT:512 * im + (i + 1) * SLOT], b["P"][rows, i, :, :].rearrange("p a r -> p (a r)"),
                                              keep["ident"][rows, rows])
                    mm.then_inc(s["pt_ps"], 1)
                if A is not None:
                    pe.wait_ge(s["xT"], old)
                    values(0)
                if B is not None:
                    pe.wait_ge(s["imm"], 1)
                    pe.wait_ge(s["PT0"], B)
                    pe.wait_ge(s["PT1"], B)
                    pe.wait_ge(s["V"], B)
                    for i in range(NI):
                        for im in range(2):
                            for a in range(2):
                                rows = slice(64 * a, 64 * a + PATCHES)
                                mm = pe.matmul(p["p67"][64 * im:64 * im + 64, 512 * a + i * 16:512 * a + (i + 1) * 16],
                                               b["PT"][rows, im, i, :], b["V"][rows, im, i, :], start=True, stop=True)
                    mm.then_inc(s["ctx_ps"], 1)
                if A is not None:
                    values(1).then_inc(s["v_ps"], 1)
                    pe.wait_ge(s["qT"], A)
                    pe.wait_ge(s["kd"], A)
                    pe.wait_ge(s["C"], A - 1)
                    scores(p["p67"], b["qT"], b["kd"], s["s2_ps"])
                if B is not None:
                    pe.wait_ge(s["C"], B)
                    pe.wait_ge(s["qT"], B if A is None else A)
                    for a in range(2):
                        mm = pe.transpose(p["p0"][0:HALF, a * 128:(a + 1) * 128], b["C"][:, a, :], keep["ident"][:, :])
                    mm.then_inc(s["ct_ps"], 1)
                if A is not None:
                    pe.wait_ge(s["cT"], A)
                    pe.wait_ge(s["cd"], A)
                    pe.wait_ge(s["PT0"], A - 1)
                    pe.wait_ge(s["PT1"], A - 1)
                    scores(p["p45"], b["cT"], b["cd"], s["s1_ps"])
                if B is not None:
                    pe.wait_ge(s["CT"], B)
                    pe.wait_ge(s["kd"], B if A is None else A)
                    for c in range(2):
                        mm = pe.matmul(p["p1"][0:PAIR, 0:WIDTH], b["CT"][:, c, :], b["wo"][:, c, :], start=c == 0, stop=c == 1)
                    mm.then_inc(s["wo_ps"], 1)

            def mlp(A, B, q):
                if A is not None:
                    cols = bass.ds(q * GCOLS, GCOLS)
                    for j in range(NFF):
                        pe.wait_ge(h_sb[j], A - 1)
                        for c in range(2):
                            K = HALF + c
                            mm = pe.matmul(h_bank[j][:, 0:GCOLS], f["wi"][0:K, c, j * 128:(j + 1) * 128], keep["XT"][0:K, c, cols], start=c == 0, stop=c == 1)
                        mm.then_inc(h_ps[j], 1)
                if B is not None:
                    for u in range(2):
                        pe.wait_ge(s["imm"], 1)
                        pe.wait_ge(g["xn"], B)
                        for r in range(2):
                            for c in range(2):
                                at = 512 * u + (2 * r + c) * PAIR
                                mm = pe.transpose(p["p67"][0:HALF, at:at + PAIR], f["xn"][:, 2 * u + r, c * HALF:(c + 1) * HALF],
                                                  keep["ident"][0:PAIR, 0:PAIR])
                        mm.then_inc(x_ps[u], 1)
                if A is not None:
                    for j in range(NFF):
                        pe.wait_ge(h_sb[j], A)
                    n0 = GROUP * (A - 2) + 2
                    for r in range(GROUP):
                        if r < 2:
                            pe.wait_ge(xT[r], A - 1)
                        else:
                            pe.wait_ge(g["y"], n0 + r - 2)
                        for j in range(NFF):
                            mm = pe.matmul(p["p67"][0:PAIR, 512 * (r % 2):512 * (r % 2) + WIDTH], f["h"][:, j, r * PAIR:(r + 1) * PAIR], f["wo2"][:, j, :],
                                           start=j == 0, stop=j == NFF - 1)
                        mm.then_inc(g["out_ps"], 1)

            with pe.Fori(1, LAYERS + 1) as l:
                pe.wait_ge(s["attn_w"], 16 * AW * l)
                for u in range(2):
                    pe.wait_ge(xT[u], GROUPS * (l - 1) + 1)
                attention_steps(pe, l, attention)
                pe.wait_ge(g["ffn_w"], 16 * FW * l)
                pe.wait_ge(s["xT"], TURNS * l + 1)
                mlp_steps(pe, l, mlp)

        @block.vector
        def _(dve):
            dve.memset(b["xs"][:, :, PAIR:], 0.0).then_inc(s["pads"], 1)
            dve.memset(b["qT"][:, :, PAIR:], 0.0).then_inc(s["pads"], 1)
            dve.memset(b["cT"][:, :, PAIR:], 0.0).then_inc(s["pads"], 1)
            dve.memset(b["P"][:, :, :, PATCHES:], 0.0).then_inc(s["pads"], 1)
            dve.memset(b["PT"][:], 0.0).then_inc(s["pads"], 1)
            dve.tensor_copy(keep["Y"][:], keep["X"][:]).then_inc(s["saved"], 1)
            dve.wait_ge(s["consts"], 16 * len(consts))
            dve.wait_ge(s["pads"], 5)

            def each(ap):
                return ap.unsqueeze(3).to_broadcast([128, 2, NI, PATCHES])

            def attention(A, B, T, old, q):
                if A is not None:
                    dve.wait_ge(s["k_ps"], A)
                    dve.wait_ge(s["s2_ps"], A - 1)
                    for a in range(2):
                        ins = dve.tensor_tensor(b["kd"][:, a], p["p1"][0:HALF, a * PAIR:(a + 1) * PAIR].unsqueeze(1).to_broadcast([HALF, NI, PAIR]),
                                                b["own"][:].unsqueeze(2).to_broadcast([HALF, NI, PAIR]), ALU.mult)
                    ins.then_inc(s["kd"], 1)
                if B is not None:
                    dve.wait_ge(s["pt_ps"], B)
                    dve.tensor_copy(b["PT"][:, 1], p["p45"][:, 512:512 + NI * SLOT].rearrange("p (i r) -> p i r", i=NI)).then_inc(s["PT1"], 1)
                    dve.wait_ge(s["ctx_ps"], B)
                    dve.tensor_copy(b["C"][:], p["p67"][:].rearrange("p (a c) -> p a c", a=2)[:, :, 0:HALF]).then_inc(s["C"], 1)
                if A is not None:
                    dve.wait_ge(s["s2_ps"], A)
                    dve.tensor_reduce(b["mx"][:], heads_of(p["p67"][:]), AX.X, ALU.max).then_inc(s["mx"], 1)
                    dve.wait_ge(s["mx"], A)
                    dve.tensor_tensor(b["E2"][:], heads_of(p["p67"][:]), each(b["mx"][:]), ALU.subtract).then_inc(s["shifted"], 1)
                if B is not None:
                    dve.wait_ge(s["ct_ps"], B)
                    dve.tensor_copy(packed(b["CT"][:]), slots(p["p0"][0:HALF, 0:256], 2)).then_inc(s["CT"], 1)
                if A is not None:
                    dve.wait_ge(s["E2"], A)
                    dve.tensor_reduce(b["z2"][:], b["E2"][:], AX.X, ALU.add).then_inc(s["z2"], 1)
                    dve.wait_ge(s["z2"], A)
                    dve.reciprocal(b["rz2"][:], b["z2"][:]).then_inc(s["rz2"], 1)
                    dve.wait_ge(s["rz2"], A)
                    dve.tensor_tensor(b["E2"][:], b["E2"][:], each(b["rz2"][:]), ALU.mult).then_inc(s["P2"], 1)
                if B is not None:
                    dve.wait_ge(s["wo_ps"], B)
                    dve.wait_ge(s["hb"], B)
                    dve.tensor_tensor(b["y"][:], p["p1"][0:PAIR, 0:WIDTH], b["hb"][:], ALU.add).then_inc(s["y"], 1)
                    dve.wait_ge(s["y"], B)
                    dve.bn_stats(b["st"][:], b["y"][:]).then_inc(s["st"], 1)
                    dve.wait_ge(s["imm"], 1)
                    dve.wait_ge(s["st"], B)
                    dve.bn_aggr(b["mv"][:], b["st"][:]).then_inc(s["mv"], 1)
                    dve.wait_ge(s["mv"], B)
                    dve.tensor_scalar(b["ve"][:], b["mv"][:, 1:2], 1e-12, None, ALU.add).then_inc(s["ve"], 1)
                if A is not None:
                    dve.wait_ge(s["E1x"], A)
                    dve.tensor_reduce(b["z1"][:], b["E1"][:], AX.X, ALU.add).then_inc(s["z1"], 1)
                    dve.wait_ge(s["z1"], A)
                    dve.reciprocal(b["rz1"][:], b["z1"][:]).then_inc(s["rz1"], 1)
                    dve.wait_ge(s["rz1"], A)
                    dve.tensor_tensor(b["E1"][:], b["E1"][:], each(b["rz1"][:]), ALU.mult).then_inc(s["P1"], 1)
                    dve.wait_ge(s["P1"], A)
                    dve.wait_ge(s["P2"], A)
                    dve.tensor_tensor(b["P"][:, :, :, 0:PATCHES].rearrange("p i a r -> p a i r"), b["E1"][:], b["E2"][:], ALU.add).then_inc(s["P"], 1)
                if B is not None:
                    dve.wait_ge(s["rstd"], B)
                    dve.wait_ge(s["yg"], B - 1)
                    dve.tensor_scalar(b["yn"][:], b["y"][:], b["mv"][:, 0:1], b["rstd"][:], ALU.subtract, ALU.mult).then_inc(s["yn"], 1)

            def mlp(A, B, q):
                if A is None:
                    return
                n0 = GROUP * (A - 2) + 2
                dve.wait_ge(g["hb"], A)
                for r in range(GROUP):
                    dve.wait_ge(g["out_ps"], n0 + r)
                    dve.tensor_tensor(f["y"][:, r], p["p67"][0:PAIR, 512 * (r % 2):512 * (r % 2) + WIDTH], f["hb"][:, r], ALU.add).then_inc(g["y"], 1)
                    dve.wait_ge(g["y"], n0 + r)
                    dve.bn_stats(f["st"][:, r], f["y"][:, r]).then_inc(g["st"], 1)
                for r in range(GROUP):
                    dve.wait_ge(s["imm"], 1)
                    dve.wait_ge(g["st"], n0 + r)
                    dve.bn_aggr(f["mv"][:, r], f["st"][:, r]).then_inc(g["mv"], 1)
                dve.wait_ge(g["mv"], n0 + GROUP - 1)
                dve.tensor_scalar(f["ve"][:], f["mv"][:, :, 1], 1e-12, None, ALU.add).then_inc(g["ve"], 1)
                dve.wait_ge(g["rstd"], A)
                dve.wait_ge(g["yg"], A - 1)
                for r in range(GROUP):
                    dve.tensor_scalar(f["yn"][:, r], f["y"][:, r], f["mv"][:, r, 0:1], f["rstd"][:, r:r + 1], ALU.subtract, ALU.mult).then_inc(g["yn"], 1)

            with dve.Fori(1, LAYERS + 1) as l:
                attention_steps(dve, l, attention)
                mlp_steps(dve, l, mlp)

        @block.scalar
        def _(act):
            act.wait_ge(s["pads"], 5)
            act.wait_ge(s["saved"], 1)

            def attention(A, B, T, old, q):
                if A is not None:
                    act.wait_ge(s["v_ps"], A - 1)
                    act.activation(b["xs"][:, :, 0:PAIR], keep["XT"][:, :, bass.ds(q * PAIR, PAIR)], ACT.Copy).then_inc(s["xs"], 1)
                    act.wait_ge(s["c_ps"], A)
                    act.wait_ge(s["n2_ps"], A - 1)
                    act.wait_ge(s["cT"], A - 1)
                    act.activation(b["c2"][:].rearrange("p a r -> p (a r)"), p["p2"][0:HALF, 0:2 * PAIR], ACT.Square).then_inc(s["c2"], 1)
                    act.activation(b["c"][:].rearrange("p a r -> p (a r)"), p["p2"][0:HALF, 0:2 * PAIR], ACT.Copy).then_inc(s["c"], 1)
                    act.wait_ge(s["q_ps"], A)
                    act.wait_ge(s["s2_ps"], A - 1)
                    act.activation(b["qT"][:, :, 0:PAIR], p["p0"][0:HALF, 0:2 * PAIR].rearrange("p (a r) -> p a r", a=2), ACT.Copy, scale=0.25).then_inc(s["qT"], 1)
                if T is not None:
                    act.wait_ge(s["imm"], 1)
                    act.wait_ge(s["x_ps"], T)
                    act.activation(keep["XT"][0:HALF, :, bass.ds((q - 2) * PAIR, PAIR)], p["p3"][0:HALF, 0:2 * PAIR].rearrange("p (c r) -> p c r", c=2),
                                   ACT.Copy).then_inc(s["xT"], 1)
                if A is not None:
                    act.wait_ge(s["n2_ps"], A)
                    act.activation(b["n2"][:], p["p2"][0:HALF, 0:2 * PAIR], ACT.Ln).then_inc(s["n2"], 1)
                    act.wait_ge(s["n2"], A)
                    act.activation(b["rn"][:], b["n2"][:], ACT.Exp, scale=-0.5).then_inc(s["rn"], 1)
                if T is not None:
                    act.activation(keep["X"][:, bass.ds(q - 2, 1), :], b["xn"][:].unsqueeze(1), ACT.Copy).then_inc(s["X"], 1)
                if B is not None:
                    act.wait_ge(s["pt_ps"], B)
                    act.activation(b["PT"][:, 0], p["p45"][:, 0:NI * SLOT].rearrange("p (i r) -> p i r", i=NI), ACT.Copy).then_inc(s["PT0"], 1)
                if A is not None:
                    act.wait_ge(s["v_ps"], A)
                    act.wait_ge(s["ctx_ps"], A - 1)
                    act.activation(b["V"][:].rearrange("p m i d -> p (m i d)"), p["p3"][:, 0:WIDTH], ACT.Copy, scale=0.5).then_inc(s["V"], 1)
                    act.wait_ge(s["shifted"], A)
                    act.activation(b["E2"][:], b["E2"][:], ACT.Exp).then_inc(s["E2"], 1)
                    act.wait_ge(s["s1_ps"], A)
                    act.wait_ge(s["P"], A - 1)
                    act.activation(b["E1"][:], heads_of(p["p45"][:]), ACT.Exp, bias=1.0, scale=-1.0).then_inc(s["E1"], 1)

            def mlp(A, B, q):
                if A is not None:
                    act.wait_ge(g["out_ps"], GROUP * (A - 2) + 1)
                    for j in range(NFF):
                        act.wait_ge(h_ps[j], A)
                        act.activation(f["h"][:, j, :], h_bank[j][:, 0:GCOLS], ACT.Gelu).then_inc(h_sb[j], 1)
                if B is not None:
                    for u in range(2):
                        act.wait_ge(s["imm"], 1)
                        act.wait_ge(x_ps[u], B)
                        act.activation(keep["XT"][0:HALF, :, bass.ds((q - 1) * GCOLS + 2 * u * PAIR, 2 * PAIR)].rearrange("p c (t r) -> p t c r", t=2),
                                       p["p67"][0:HALF, 512 * u:512 * u + 4 * PAIR].rearrange("p (t c r) -> p t c r", t=2, c=2),
                                       ACT.Copy).then_inc(xT[u], 1)
                    act.activation(keep["X"][:, bass.ds((q - 1) * GROUP, GROUP), :], f["xn"][:], ACT.Copy).then_inc(g["X"], 1)

            with act.Fori(1, LAYERS + 1) as l:
                act.preload_act_table_set("natural_log_exp_and_others")
                for u in range(2):
                    act.wait_ge(xT[u], GROUPS * (l - 1) + 1)
                attention_steps(act, l, attention)
                mlp_steps(act, l, mlp)

        @block.gpsimd
        def _(pool):
            pool.sem_inc(s["imm"], 1)
            pool.wait_ge(s["consts"], 16 * len(consts))
            pool.wait_ge(s["pads"], 5)

            def attention(A, B, T, old, q):
                if A is not None:
                    pool.wait_ge(s["rn"], A)
                    pool.wait_ge(s["c"], A)
                    pool.wait_ge(s["s1_ps"], A - 1)
                    pool.tensor_tensor(b["cT"][:, :, 0:PAIR], b["c"][:], b["rn"][:].rearrange("p (a r) -> p a r", a=2), ALU.mult).then_inc(s["cT"], 1)
                    pool.wait_ge(s["cT"], A)
                    for a in range(2):
                        ins = pool.tensor_tensor(b["cd"][:, a], b["cT"][:, a, 0:PAIR].unsqueeze(1).to_broadcast([HALF, NI, PAIR]),
                                                 b["own"][:].unsqueeze(2).to_broadcast([HALF, NI, PAIR]), ALU.mult)
                    ins.then_inc(s["cd"], 1)
                if B is not None:
                    pool.wait_ge(s["y"], B - 1)
                    pool.tensor_tensor(b["hb"][:], keep["X"][:, bass.ds(q - 1, 1), :].rearrange("p o w -> p (o w)"), b["rows"][:, 0, :], ALU.add).then_inc(s["hb"], 1)
                if A is not None:
                    pool.wait_ge(s["E1"], A)
                    E1 = b["E1"][:].rearrange("p a i r -> p (a i) r")
                    pool.tensor_tensor(E1, E1, b["eye"][:].unsqueeze(1).to_broadcast([128, HEADS, PATCHES]), ALU.mult).then_inc(s["E1x"], 1)
                if B is not None:
                    pool_rstd(pool, b, s, B, keep)
                    pool.wait_ge(s["yn"], B)
                    pool.tensor_tensor(b["yg"][:], b["yn"][:], b["rows"][:, 1, :], ALU.mult).then_inc(s["yg"], 1)
                    pool.wait_ge(s["yg"], B)
                    pool.wait_ge(s["x_ps"], B - 1)
                    pool.wait_ge(s["X"], B - 1)
                    pool.tensor_tensor(b["xn"][:], b["yg"][:], b["rows"][:, 2, :], ALU.add).then_inc(s["xn"], 1)

            def mlp(A, B, q):
                if A is None:
                    return
                def row(k):
                    return b["rows"][:, k, :].unsqueeze(1).to_broadcast([PAIR, GROUP, WIDTH])

                pool.wait_ge(g["y"], GROUP * (A - 2) + 1)
                pool.tensor_tensor(f["hb"][:], keep["X"][:, bass.ds(GROUP * q, GROUP), :], row(3), ALU.add).then_inc(g["hb"], 1)
                pool.wait_ge(g["ve"], A)
                pool.tensor_tensor(f["rstd"][:], f["ve"][:], keep["half"][:].to_broadcast([PAIR, GROUP]), ALU.pow).then_inc(g["rstd"], 1)
                pool.wait_ge(g["yn"], GROUP * (A - 1) + 1)
                pool.tensor_tensor(f["yg"][:], f["yn"][:], row(4), ALU.mult).then_inc(g["yg"], 1)
                pool.wait_ge(g["yg"], A)
                for u in range(2):
                    pool.wait_ge(x_ps[u], A - 1)
                pool.wait_ge(g["X"], A - 1)
                pool.tensor_tensor(f["xn"][:], f["yg"][:], row(5), ALU.add).then_inc(g["xn"], 1)

            with pool.Fori(1, LAYERS + 1) as l:
                pool.wait_ge(s["attn_w"], 16 * AW * l)
                pool.wait_ge(g["X"], GROUPS * (l - 1) + 1)
                attention_steps(pool, l, attention)
                pool.wait_ge(s["X"], TURNS * l + 1)
                mlp_steps(pool, l, mlp)


def block_residual_norm(nc, d, keep):
    with ExitStack() as ctx:
        b = buffers(ctx, nc, "rn", y=(PAIR, WIDTH), st=(PAIR, 6), mv=(PAIR, 2), ve=(PAIR, 1), rstd=(PAIR, 1), xn=(PAIR, WIDTH))
        p = banks(ctx, nc, "rn", p1=512)
        s = signals(ctx, nc, "rn", "y st mv ve rstd xn x_ps xT X", setup="imm")
        block = ctx.enter_context(nc.Block())

        @block.vector
        def _(dve):
            with dve.Fori(2, TURNS + 2) as n:
                m, t = n - 1, n - 2
                dve.wait_ge(s["xn"], m)
                dve.tensor_tensor(b["y"][:], keep["X"][:, bass.ds(t, 1), :].rearrange("p o w -> p (o w)"),
                                  keep["Y"][:, bass.ds(t, 1), :].rearrange("p o w -> p (o w)"), ALU.add).then_inc(s["y"], 1)
                norm(dve, b, s, n, m, b["y"][:], 1e-5, b["xn"][:], (s["X"], s["x_ps"])).then_inc(s["xn"], 1)

        @block.gpsimd
        def _(pool):
            pool.sem_inc(s["imm"], 1)
            with pool.Fori(2, TURNS + 2) as n:
                pool_rstd(pool, b, s, n, keep)

        @block.tensor
        def _(pe):
            with pe.Fori(2, TURNS + 2) as n:
                pe.wait_ge(s["imm"], 1)
                pe.wait_ge(s["xn"], n)
                pe.wait_ge(s["xT"], n - 1)
                for c in range(2):
                    mm = pe.transpose(p["p1"][0:HALF, c * PAIR:(c + 1) * PAIR], b["xn"][:, c * HALF:(c + 1) * HALF], keep["ident"][0:PAIR, 0:PAIR])
                mm.then_inc(s["x_ps"], 1)

        @block.scalar
        def _(act):
            with act.Fori(2, TURNS + 2) as n:
                act.wait_ge(s["x_ps"], n)
                act.activation(keep["XT"][0:HALF, :, bass.ds((n - 2) * PAIR, PAIR)], p["p1"][0:HALF, 0:2 * PAIR].rearrange("p (c r) -> p c r", c=2),
                               ACT.Copy).then_inc(s["xT"], 1)
                act.activation(keep["Y"][:, bass.ds(n - 2, 1), :], b["xn"][:].unsqueeze(1), ACT.Copy).then_inc(s["X"], 1)


def block_mixture(nc, d, keep):
    NE = 8
    with ExitStack() as ctx:
        b = buffers(ctx, nc, "mx", wg=(HALF + 1, 2, NE), xs=(HALF + 1, 2, PAIR), lg=(PAIR, 10), m8=(PAIR, 8), neg=(PAIR, 1), left=(PAIR, 10),
                    mask=(PAIR, NE), ex=(PAIR, NE), em=(PAIR, NE), sm=(PAIR, 1), rs=(PAIR, 1), gates=(PAIR, NE, TURNS),
                    w1=(HALF + 1, 2, 2, FFN), w2=(128, 2, NFF, WIDTH), b2=(PAIR, 2, WIDTH), h=(128, NFF, GCOLS), ob=(PAIR, GROUP, WIDTH),
                    y=(PAIR, WIDTH), st=(PAIR, 6), mv=(PAIR, 2), ve=(PAIR, 1), rstd=(PAIR, 1), xn=(PAIR, WIDTH))
        p = banks(ctx, nc, "mx", hp=3072, o0=512, o1=512)
        s = signals(ctx, nc, "mx", "xs lg_ps lg top8 top2 left mask neg ex em rs gates h0 h1 h2 h3 h4 h5 a0 a1 a2 a3 a4 a5 "
                                   "out_ps ob Y y st mv ve rstd xn", dma="stored", setup="imm wg w0 w1 pad")
        h_ps, h_sb, w = (s["h0"], s["h1"], s["h2"], s["h3"], s["h4"], s["h5"]), (s["a0"], s["a1"], s["a2"], s["a3"], s["a4"], s["a5"]), (s["w0"], s["w1"])
        h_bank = [p["hp"][:, 512 * j:512 * j + GCOLS] for j in range(NFF)]
        outs = (p["o0"], p["o1"])
        out_rows = d["out"].rearrange("(t p) w -> t p w", p=PAIR)
        block = ctx.enter_context(nc.Block())

        def load(sp, e, u):
            for to, src in ((b["w1"], d["w1"]), (b["w2"], d["w2"]), (b["b2"], d["b2e"])):
                sp.dma_start(to[:, u], src[e]).then_inc(w[u], 16)

        @block.sync
        def _(sp):
            sp.dma_start(b["wg"][:], d["gwg"]).then_inc(s["wg"], 16)
            for u in range(2):
                load(sp, u, u)
            with sp.Fori(1, NE // 2) as i:
                for u in range(2):
                    sp.wait_ge(s["imm"], 1)
                    sp.wait_ge(s["Y"], TURNS * (2 * i + u - 1) + 1)
                    load(sp, 2 * i + u, u)
            with sp.Fori(2, TURNS + 2) as n:
                sp.wait_ge(s["imm"], 1)
                sp.wait_ge(s["xn"], n)
                sp.dma_start(out_rows[n - 2], b["xn"][:]).then_inc(s["stored"], 16)
            sp.wait_ge(s["stored"], 16 * (TURNS + 1))

        @block.tensor
        def _(pe):
            pe.wait_ge(s["wg"], 16)
            with pe.Fori(2, TURNS + 2) as n:
                pe.wait_ge(s["xs"], n)
                pe.wait_ge(s["lg"], n - 1)
                for c in range(2):
                    K = HALF + c
                    mm = pe.matmul(p["o0"][0:PAIR, 0:NE], b["xs"][0:K, c, :], b["wg"][0:K, c, :], start=c == 0, stop=c == 1)
                mm.then_inc(s["lg_ps"], 1)
            pe.wait_ge(s["lg"], TURNS + 1)
            with pe.Fori(1, NE // 2 + 1) as i:
                for u in range(2):
                    with pe.Fori(1, GROUPS + 1) as q:
                        pe.wait_ge(w[u], 48 * i)
                        n = GROUPS * (2 * (i - 1) + u) + q + 1
                        n0 = GROUP * (n - 2) + 2
                        cols = bass.ds((q - 1) * GCOLS, GCOLS)
                        for j in range(NFF):
                            pe.wait_ge(h_sb[j], n - 1)
                            for c in range(2):
                                K = HALF + c
                                mm = pe.matmul(h_bank[j], b["w1"][0:K, u, c, j * 128:(j + 1) * 128], keep["XT"][0:K, c, cols], start=c == 0, stop=c == 1)
                            mm.then_inc(h_ps[j], 1)
                        for j in range(NFF):
                            pe.wait_ge(h_sb[j], n)
                        for r in range(GROUP):
                            pe.wait_ge(s["ob"], n0 + max(r - 2, -1))
                            for j in range(NFF):
                                mm = pe.matmul(outs[r % 2][0:PAIR, 0:WIDTH], b["h"][:, j, r * PAIR:(r + 1) * PAIR], b["w2"][:, u, j, :],
                                               start=j == 0, stop=j == NFF - 1)
                            mm.then_inc(s["out_ps"], 1)

        @block.scalar
        def _(act):
            with act.Fori(2, TURNS + 2) as n:
                act.wait_ge(s["lg_ps"], n - 1)
                act.activation(b["xs"][:], keep["XT"][:, :, bass.ds((n - 2) * PAIR, PAIR)], ACT.Copy).then_inc(s["xs"], 1)
                act.wait_ge(s["neg"], n)
                act.wait_ge(s["em"], n - 1)
                act.activation(b["ex"][:], b["lg"][:, 0:NE], ACT.Exp, bias=b["neg"][:]).then_inc(s["ex"], 1)
            with act.Fori(2, NE * GROUPS + 2) as n:
                act.wait_ge(s["out_ps"], GROUP * (n - 2) + 1)
                for j in range(NFF):
                    act.wait_ge(h_ps[j], n)
                    act.activation(b["h"][:, j, :], h_bank[j], ACT.Relu).then_inc(h_sb[j], 1)

        @block.vector
        def _(dve):
            dve.memset(b["lg"][:, NE:], -BIG).then_inc(s["pad"], 1)
            dve.wait_ge(s["pad"], 1)
            with dve.Fori(2, TURNS + 2) as n:
                dve.wait_ge(s["lg_ps"], n)
                dve.wait_ge(s["ex"], n - 1)
                dve.tensor_copy(b["lg"][:, 0:NE], p["o0"][0:PAIR, 0:NE]).then_inc(s["lg"], 1)
                dve.wait_ge(s["imm"], 1)
                dve.wait_ge(s["lg"], n)
                dve.max(b["m8"][:], b["lg"][:]).then_inc(s["top8"], 1)
                dve.wait_ge(s["top8"], n)
                dve.tensor_scalar(b["neg"][:], b["m8"][:, 0:1], -1.0, None, ALU.mult).then_inc(s["neg"], 1)
                dve.memset(b["m8"][:, 2:8], -BIG).then_inc(s["top2"], 1)
                dve.wait_ge(s["imm"], 1)
                dve.wait_ge(s["top2"], n)
                dve.match_replace(b["left"][:], b["m8"][:], b["lg"][:], -2 * BIG).then_inc(s["left"], 1)
                dve.wait_ge(s["left"], n)
                dve.tensor_tensor(b["mask"][:], b["left"][:, 0:NE], b["lg"][:, 0:NE], ALU.not_equal).then_inc(s["mask"], 1)
                dve.wait_ge(s["mask"], n)
                dve.wait_ge(s["ex"], n)
                dve.tensor_tensor_reduce(b["em"][:], b["ex"][:], b["mask"][:], 1.0, 0.0, ALU.mult, ALU.add, b["sm"][:]).then_inc(s["em"], 1)
                dve.wait_ge(s["em"], n)
                dve.reciprocal(b["rs"][:], b["sm"][:]).then_inc(s["rs"], 1)
                dve.wait_ge(s["rs"], n)
                dve.tensor_scalar(b["gates"][:, :, bass.ds(n - 2, 1)].rearrange("p e o -> p (e o)"), b["em"][:], b["rs"][:], None, ALU.mult).then_inc(s["gates"], 1)
            dve.wait_ge(s["gates"], TURNS + 1)
            with dve.Fori(1, NE // 2 + 1) as i:
                for u in range(2):
                    with dve.Fori(1, GROUPS + 1) as q:
                        dve.wait_ge(w[u], 48 * i)
                        e = 2 * (i - 1) + u
                        n0 = GROUP * (GROUPS * e + q - 1) + 2
                        for r in range(GROUP):
                            turn = GROUP * (q - 1) + r
                            dve.wait_ge(s["out_ps"], n0 + r)
                            dve.tensor_tensor(b["ob"][:, r], outs[r % 2][0:PAIR, 0:WIDTH], b["b2"][:, u], ALU.add).then_inc(s["ob"], 1)
                            dve.wait_ge(s["ob"], n0 + r)
                            row = keep["Y"][:, bass.ds(turn, 1), :].rearrange("p o w -> p (o w)")
                            gate = b["gates"][:].rearrange("p e t -> p (e t)")[:, bass.ds(TURNS * e + turn, 1)]
                            dve.scalar_tensor_tensor(row, b["ob"][:, r], gate, row, ALU.mult, ALU.add).then_inc(s["Y"], 1)
            dve.wait_ge(s["Y"], NE * TURNS + 1)
            with dve.Fori(2, TURNS + 2) as n:
                dve.wait_ge(s["xn"], n - 1)
                dve.tensor_copy(b["y"][:], keep["Y"][:, bass.ds(n - 2, 1), :].rearrange("p o w -> p (o w)")).then_inc(s["y"], 1)
                dve.wait_ge(s["stored"], 16 * (n - 1))
                norm(dve, b, s, n, n - 1, b["y"][:], 1e-5, b["xn"][:]).then_inc(s["xn"], 1)

        @block.gpsimd
        def _(pool):
            pool.sem_inc(s["imm"], 1)
            with pool.Fori(2, TURNS + 2) as n:
                pool_rstd(pool, b, s, n, keep)


def storage(nc, ctx, d):
    keep = buffers(ctx, nc, "keep", X=(PAIR, TURNS, WIDTH), XT=(HALF + 1, 2, TOKENS), Y=(PAIR, TURNS, WIDTH), w6=(PAIR, TURNS, TOPK),
                   ident=(128, 128), half=(PAIR, 1))
    keep["rows"] = ctx.enter_context(nc.sbuf_tensor("keep_rows", [PAIR, TURNS, 8], I32))
    d["x_rows"] = nc.dram_tensor("x_rows", (TURNS, PAIR, WIDTH), F32).ap()
    d["x_flat"] = d["x_rows"].rearrange("t p w -> (t p) w")
    d["slot_token"] = nc.dram_tensor("slot_token", (CAPH, 2 * EXPERTS), I32).ap()
    d["slot_token_rows"] = d["slot_token"].rearrange("p (e o) -> (p e) o", o=1)
    d["slot_out"] = nc.dram_tensor("slot_out", (CAPH, 2 * EXPERTS, WIDTH), F32).ap()
    d["slot_out_rows"] = d["slot_out"].rearrange("p e w -> (p e) w")
    return keep, d


def program(nc, d, out):
    d = dict(d, out=out)
    with ExitStack() as ctx:
        keep, d = storage(nc, ctx, d)
        block_embed_and_latent_attention(nc, d, keep)
        block_router_and_shared_expert(nc, d, keep)
        block_routed_experts(nc, d, keep)
        block_combine(nc, d, keep)
        block_bert(nc, d, keep)
        block_residual_norm(nc, d, keep)
        block_mixture(nc, d, keep)


def rope_tables():
    inv = (1.0 / 10000.0 ** (np.arange(0, HD0, 2, dtype=np.float32) / HD0)).astype(np.float32)
    ang = np.arange(PATCHES, dtype=np.float32)[:, None] * inv[None, :]
    ang = np.concatenate([ang, ang], axis=-1).T
    sign = np.where(np.arange(HD0) < HD0 // 2, -1.0, 1.0).astype(np.float32)[:, None]
    return np.tile(np.cos(ang), (2, 2)), np.tile(np.sin(ang) * sign, (2, 2))


def position_table():
    j = np.arange(WIDTH)
    expo = (2 * (j // 2)).astype(np.float32) / np.float32(WIDTH)
    angle = np.arange(PATCHES, dtype=np.float32)[:, None] / np.power(np.float32(10000.0), expo)
    angle = angle + np.where(j % 2 == 1, np.float32(np.pi / 2), np.float32(0.0)).astype(np.float32)
    return np.tile(np.sin(angle.astype(np.float32)), (2, 1))


def constants():
    cos, sin = rope_tables()
    row, col = np.arange(128)[:, None] % SLOT, np.arange(PATCHES)[None, :]
    e = np.arange(EXPERTS)
    token = np.arange(PAIR)[:, None] + PAIR * np.arange(TURNS)[None, :]
    return {
        "cos": cos, "sin": sin, "pos": position_table(),
        "mask": np.where((row >= PATCHES) | (col <= row), 0.0, -BIG),
        "eye": np.where(row == col, np.e, 1.0), "ident": np.eye(128), "half": np.full((PAIR, 1), -0.5),
        "before": np.triu(np.ones((PAIR, PAIR)), 1), "ones": np.ones((PAIR, PAIR)),
        "slot0": np.tile(2.0 * e, (PAIR, 1)), "token": token.astype(np.uint32),
        "own": np.where(np.arange(HALF)[:, None] // 16 == np.arange(NI)[None, :], 1.0, 0.0),
        "block16": np.where(np.arange(HALF)[:, None] // 16 == np.arange(HALF)[None, :] // 16, 1.0, 0.0),
    }


def chunks(w, ones=None):
    out = w.reshape(2, HALF, -1).transpose(1, 0, 2)
    if ones is None:
        return out
    row = np.stack([np.zeros_like(ones), ones])[None]
    return np.concatenate([out, row], axis=0)


def rows_of(v):
    return np.broadcast_to(v, (PAIR, v.shape[-1]))


def layout(i):
    px = i["x"][:, :, 0:112, 0:112].reshape(TURNS, 2, 3, 7, 16, 7, 16)
    px = px.transpose(0, 2, 4, 6, 1, 3, 5).reshape(TURNS, 6, 128, PAIR).transpose(0, 2, 1, 3)
    wq, wup = i["L0_attn_Wq"], i["L0_attn_Wup"]
    turn = (np.arange(HD0) + HD0 // 2) % HD0
    swap = (np.arange(HEADS)[:, None] * HD0 + turn[None, :]).reshape(-1)
    wk = wup[:, 0:768]
    a = {
        "xp": px, "wtok": i["L0_tok_W"].reshape(WIDTH, 6, 128).transpose(2, 1, 0), "tok_b": rows_of(i["L0_tok_b"]),
        "bo0": rows_of(i["L0_attn_bo"]), "wdown": chunks(i["L0_attn_Wdown"]), "wq0": chunks(wq), "wq0r": chunks(wq[:, swap]),
        "wk0": wk, "wk0r": wk[:, swap], "wv0": wup[:, 768:].reshape(64, NI, 2, HD0).transpose(0, 2, 1, 3).reshape(64, 768),
        "wo0": i["L0_attn_Wo"].reshape(6, 128, WIDTH).transpose(1, 0, 2),
        "ln_g": i["L0_attn_ln_g"].reshape(64, 1), "ln_b": i["L0_attn_ln_b"].reshape(64, 1),
        "wg": chunks(i["L0_ffn_Wg"].T), "e_bias": rows_of(i["L0_ffn_e_bias"]),
        "wgu": i["L0_ffn_W_gate_up"].reshape(EXPERTS, 2, HALF, 2 * INTER).transpose(0, 2, 1, 3),
        "wdn": i["L0_ffn_W_down"].reshape(EXPERTS, NF, FC, WIDTH).transpose(0, 2, 1, 3),
        "wsg": chunks(i["L0_ffn_Wsg"]), "wsu": chunks(i["L0_ffn_Wsu"]),
        "wsd": i["L0_ffn_Wsd"].reshape(8, FC, WIDTH).transpose(1, 0, 2),
    }
    for n in "qkvc":
        w, bias = i[f"L1_attn_W{n}"], i[f"L1_attn_b{n}"]
        a[f"bw{n}"] = np.stack([chunks(w[l], bias[l]) for l in range(LAYERS)])
    a["bwo"] = np.stack([chunks(i["L1_attn_Wo"][l]) for l in range(LAYERS)])
    a["bwi"] = np.stack([chunks(i["L1_attn_Wi"][l], i["L1_attn_bi"][l]) for l in range(LAYERS)])
    a["bwo2"] = i["L1_attn_Wo2"].reshape(LAYERS, NFF, 128, WIDTH).transpose(0, 2, 1, 3)
    rows = [i[f"L1_attn_{n}"] for n in ("bo", "g1", "b1", "bo2", "g2", "b2")]
    a["brows"] = np.broadcast_to(np.stack(rows, axis=1)[:, None], (LAYERS, PAIR, 6, WIDTH))
    a["gwg"] = chunks(i["L1_ffn_Wg"], i["L1_ffn_bg"])
    a["w1"] = np.stack([chunks(i["L1_ffn_W1"][e], i["L1_ffn_b1"][e]) for e in range(8)])
    a["w2"] = i["L1_ffn_W2"].reshape(8, NFF, 128, WIDTH).transpose(0, 2, 1, 3)
    a["b2e"] = np.broadcast_to(i["L1_ffn_b2"][:, None], (8, PAIR, WIDTH))
    return a


def kernel(**inputs):
    import concourse.bacc as bacc
    from concourse.bass_utils import run_bass_kernel_spmd

    arrays = {n: np.ascontiguousarray(a) for n, a in layout({k: np.asarray(v) for k, v in inputs.items()}).items()}
    arrays |= {n: np.ascontiguousarray(a if a.dtype == np.uint32 else a.astype(np.float32)) for n, a in constants().items()}
    nc = bacc.Bacc("TRN2", target_bir_lowering=False, num_devices=1)
    d = {n: nc.dram_tensor(n, a.shape, mybir.dt.from_np(a.dtype), kind="ExternalInput").ap() for n, a in arrays.items()}
    out = nc.dram_tensor("out", (TOKENS, WIDTH), F32, kind="ExternalOutput").ap()
    program(nc, d, out)
    r = run_bass_kernel_spmd(nc, [arrays], core_ids=[0])
    return r.results[0]["out"].reshape(IMAGES, PATCHES, WIDTH)
```

```python
from contextlib import ExitStack

import numpy as np
import concourse.bass as bass
from concourse import mybir

F32 = mybir.dt.float32
I32 = mybir.dt.uint32
ALU = mybir.AluOpType
ACT = mybir.ActivationFunctionType
AX = mybir.AxisListType

IMAGES, PATCHES, WIDTH = 64, 49, 192
TOKENS = IMAGES * PATCHES
PAIR = 2 * PATCHES
TURNS = IMAGES // 2
HALF = WIDTH // 2
GROUP = 4
GROUPS = TURNS // GROUP
GCOLS = GROUP * PAIR
SLOT = 64
PADDED = SLOT + PATCHES
HEADS = 12
NI = HEADS // 2
HD0 = 64
EXPERTS, TOPK, CAP, INTER = 128, 6, 192, 464
FC = 116
NF = INTER // FC
SHARED = 928
CAPH = CAP // 2
ROWS = CAPH * 2 * EXPERTS
LAYERS, FFN, NFF = 4, 768, 6
BIG = 1.0e30


def signals(ctx, nc, tag, names, dma="", setup=""):
    found = {n: nc.alloc_semaphore(f"{tag}_{n}") for n in f"{names} {dma} {setup}".split()}
    for n in names.split():
        nc.gpsimd.sem_inc(found[n], 1)
    for n in dma.split():
        nc.gpsimd.sem_inc(found[n], 16)
    nc.all_engine_barrier()
    ctx.callback(nc.all_engine_barrier)
    ctx.callback(nc.clear_and_free_semaphores, list(found.values()))
    return dict(**found)


def buffers(ctx, nc, tag, **shapes):
    return dict(**{n: ctx.enter_context(nc.sbuf_tensor(f"{tag}_{n}", list(s), F32)) for n, s in shapes.items()})


def banks(ctx, nc, tag, **widths):
    return dict(**{n: ctx.enter_context(nc.psum_tensor(f"{tag}_{n}", [128, w], F32)) for n, w in widths.items()})


def heads_of(ap):
    return ap.rearrange("p (a c) -> p a c", a=2)[:, :, 0:NI * PATCHES].rearrange("p a (i r) -> p a i r", i=NI)


def packed(ap):
    return ap.rearrange("p j (m r) -> p j m r", m=2)


def slots(ap, j):
    return ap.rearrange("p (j m q) -> p j m q", j=j, m=2)[:, :, :, 0:PATCHES]


def block_embed_and_latent_attention(nc, d, keep):
    with ExitStack() as ctx:
        b = buffers(
            ctx, nc, "la", xp=(128, 6, PAIR), wtok=(128, 6, WIDTH), posb=(PAIR, WIDTH), tokb=(PAIR, WIDTH), bo=(PAIR, WIDTH),
            wdown=(HALF, 2, 64), wq=(HALF, 2, 768), wqr=(HALF, 2, 768), wk=(64, 768), wkr=(64, 768), wv=(64, 768),
            wo=(128, 6, WIDTH), lng=(64, 1), lnb=(64, 1), cos=(128, PAIR), sin=(128, PAIR), mask=(128, PATCHES),
            hs=(PAIR, WIDTH), hb=(PAIR, WIDTH), hT=(HALF, 2, PAIR), st=(PAIR, 6), mv=(PAIR, 2), ve=(PAIR, 1), rstd=(PAIR, 1),
            ckn=(PAIR, 64), ckT=(64, PADDED + 15), r1=(128, 6, PAIR), r2=(128, 6, PAIR), qT=(128, 6, 128), kT=(128, 6, PAIR),
            V=(128, 2, NI, HD0), E=(128, 2, NI, PATCHES), mx=(128, 2, NI), P=(128, NI, 2, SLOT), z=(128, 2, NI), rz=(128, 2, NI),
            PT=(128, 2, NI, SLOT), C=(128, NI, 2, HD0), CT=(128, 6, PAIR), y=(PAIR, WIDTH), st2=(PAIR, 6), mv2=(PAIR, 2),
            ve2=(PAIR, 1), rstd2=(PAIR, 1), xn=(PAIR, WIDTH))
        p = banks(ctx, nc, "la", p0=512, p1=512, p23=1024, p45=1024, p67=1024)
        s = signals(
            ctx, nc, "la", "conv h hb hT_ps hT ckv q_ps st mv ve rstd ckn ck_ps ckT rq1 rq2 qT k_ps v0_ps v1_ps "
            "V0 V1 rk1 rk2 kT s_ps masked mx shifted P z rz pt0_ps pt1_ps PT0 PT1 ctx_ps C0 C1 ct_ps CT0 CT1 wo_ps y st2 mv2 ve2 rstd2 xn "
            "x_ps xT X", dma="xp stored", setup="imm weights ready_pos pads")
        loads = [(b["wtok"], d["wtok"]), (b["posb"], d["pos"]), (b["tokb"], d["tok_b"]), (b["bo"], d["bo0"]), (b["wdown"], d["wdown"]), (b["wq"], d["wq0"]),
                 (b["wqr"], d["wq0r"]), (b["wk"], d["wk0"]), (b["wkr"], d["wk0r"]), (b["wv"], d["wv0"]), (b["wo"], d["wo0"]), (b["lng"], d["ln_g"]), (b["lnb"], d["ln_b"]),
                 (b["cos"], d["cos"]), (b["sin"], d["sin"]), (b["mask"], d["mask"]), (keep["ident"], d["ident"]), (keep["half"], d["half"])]
        ckv_ps, ck_ps = p["p0"][0:PAIR, 384:448], p["p67"][0:64, 384:384 + PAIR]
        block = ctx.enter_context(nc.Block())

        def steps(engine, step):
            first, last = 2, TURNS + 1
            step(first, None, None)
            step(first + 1, first, None)
            with engine.Fori(first + 2, last + 1) as n:
                step(n, n - 1, n - 2)
            step(None, last, last - 1)
            step(None, None, last)

        @block.sync
        def _(sp):
            sp.dma_start(b["xp"][:], d["xp"][0]).then_inc(s["xp"], 16)
            for to, src in loads:
                sp.dma_start(to[:], src).then_inc(s["weights"], 16)

            def load(n):
                sp.wait_ge(s["imm"], 1)
                sp.wait_ge(s["conv"], n)
                sp.dma_start(b["xp"][:], d["xp"][n - 1]).then_inc(s["xp"], 16)

            def store(n):
                sp.wait_ge(s["imm"], 1)
                sp.wait_ge(s["xn"], n)
                sp.dma_start(d["x_rows"][n - 2], b["xn"][:]).then_inc(s["stored"], 16)

            load(2)
            with sp.Fori(2, TURNS) as n:
                load(n + 1)
                store(n)
            store(TURNS)
            store(TURNS + 1)
            sp.wait_ge(s["stored"], 16 * (TURNS + 1))

        @block.tensor
        def _(pe):
            pe.wait_ge(s["weights"], 16 * len(loads))
            pe.wait_ge(s["pads"], 4)

            def rotary(w, ps, of):
                for j in range(6):
                    at = (j // 3) * 512 + (j % 3) * PAIR
                    chunks_of = of(w, j)
                    for c, (left, right) in enumerate(chunks_of):
                        mm = pe.matmul(ps[:, at:at + PAIR], left, right, start=c == 0, stop=c == len(chunks_of) - 1)
                return mm

            def of_queries(w, j):
                return [(w[:, c, j * 128:(j + 1) * 128], b["hT"][:, c, :]) for c in range(2)]

            def of_keys(w, j):
                return [(w[:, j * 128:(j + 1) * 128], b["ckT"][:, 0:PAIR])]

            def values(im, ps, sem):
                for a in range(2):
                    mm = pe.matmul(ps[64 * a:64 * a + 64, 0:NI * HD0], b["ckT"][:, PATCHES * im:PATCHES * im + SLOT],
                                   b["wv"][:, a * 384:(a + 1) * 384], start=True, stop=True)
                mm.then_inc(sem, 1)

            def probabilities(im, sem):
                rows = slice(64 * im, 64 * im + 64)
                for i in range(NI):
                    mm = pe.transpose(p["p67"][:, 512 * im + i * SLOT:512 * im + (i + 1) * SLOT], b["P"][rows, i, :, :].rearrange("p a r -> p (a r)"),
                                      keep["ident"][rows, rows])
                mm.then_inc(sem, 1)

            def step(A, B, T):
                if A is not None:
                    pe.wait_ge(s["xp"], A * 16)
                    pe.wait_ge(s["V1"], A - 1)
                    for j in range(6):
                        mm = pe.matmul(p["p1"][0:PAIR, 0:WIDTH], b["xp"][:, j, :], b["wtok"][:, j, :], start=j == 0, stop=j == 5)
                    mm.then_inc(s["conv"], 1)
                if B is not None:
                    pe.wait_ge(s["imm"], 1)
                    pe.wait_ge(s["P"], B)
                    probabilities(0, s["pt0_ps"])
                if A is not None:
                    pe.wait_ge(s["h"], A)
                    pe.wait_ge(s["V0"], A - 1)
                    for c in range(2):
                        mm = pe.transpose(p["p0"][0:HALF, c * PAIR:(c + 1) * PAIR], b["hs"][:, c * HALF:(c + 1) * HALF], keep["ident"][0:PAIR, 0:PAIR])
                    mm.then_inc(s["hT_ps"], 1)
                if B is not None:
                    probabilities(1, s["pt1_ps"])
                if T is not None:
                    pe.wait_ge(s["imm"], 1)
                    pe.wait_ge(s["xn"], T)
                    pe.wait_ge(s["V1"], T if B is None else B)
                    for c in range(2):
                        mm = pe.transpose(p["p1"][0:HALF, c * PAIR:(c + 1) * PAIR], b["xn"][:, c * HALF:(c + 1) * HALF], keep["ident"][0:PAIR, 0:PAIR])
                    mm.then_inc(s["x_ps"], 1)
                if A is not None:
                    pe.wait_ge(s["hT"], A)
                    for c in range(2):
                        mm = pe.matmul(ckv_ps, b["hT"][:, c, :], b["wdown"][:, c, :], start=c == 0, stop=c == 1)
                    mm.then_inc(s["ckv"], 1)
                    pe.wait_ge(s["rk2"], A - 1)
                    rotary(b["wq"], p["p23"], of_queries)
                    rotary(b["wqr"], p["p45"], of_queries).then_inc(s["q_ps"], 1)
                    pe.wait_ge(s["imm"], 1)
                    pe.wait_ge(s["ckn"], A)
                    pe.wait_ge(s["PT0"], A - 1)
                    pe.wait_ge(s["PT1"], A - 1)
                    pe.transpose(ck_ps, b["ckn"][:], keep["ident"][0:PAIR, 0:PAIR]).then_inc(s["ck_ps"], 1)
                if B is not None:
                    pe.wait_ge(s["imm"], 1)
                    pe.wait_ge(s["PT0"], B)
                    pe.wait_ge(s["PT1"], B)
                    pe.wait_ge(s["V0"], B)
                    pe.wait_ge(s["V1"], B)
                    pe.wait_ge(s["xT"], B - 1)
                    for im in range(2):
                        for a, ps in enumerate((p["p0"], p["p1"])):
                            for i in range(NI):
                                rows = slice(64 * a, 64 * a + PATCHES)
                                mm = pe.matmul(ps[64 * im:64 * im + 64, i * HD0:(i + 1) * HD0],
                                               b["PT"][rows, im, i, :], b["V"][rows, im, i, :], start=True, stop=True)
                    mm.then_inc(s["ctx_ps"], 1)
                if A is not None:
                    pe.wait_ge(s["ckT"], A)
                    pe.wait_ge(s["rq2"], A)
                    rotary(b["wk"], p["p23"], of_keys)
                    rotary(b["wkr"], p["p45"], of_keys).then_inc(s["k_ps"], 1)
                if B is not None:
                    pe.wait_ge(s["C0"], B)
                    pe.wait_ge(s["C1"], B)
                    for j in range(6):
                        at = (j // 3) * 512 + (j % 3) * 128
                        mm = pe.transpose(p["p67"][:, at:at + 128], b["C"][:, j, :, :].rearrange("p a d -> p (a d)"), keep["ident"][:, :])
                    mm.then_inc(s["ct_ps"], 1)
                if A is not None:
                    pe.wait_ge(s["imm"], 1)
                    pe.wait_ge(s["C1"], A - 1)
                    values(1, p["p1"], s["v1_ps"])
                if B is not None:
                    pe.wait_ge(s["CT0"], B)
                    pe.wait_ge(s["CT1"], B)
                    for j in range(6):
                        mm = pe.matmul(p["p0"][0:PAIR, 0:WIDTH], b["CT"][:, j, :], b["wo"][:, j, :], start=j == 0, stop=j == 5)
                    mm.then_inc(s["wo_ps"], 1)
                if A is not None:
                    pe.wait_ge(s["imm"], 1)
                    pe.wait_ge(s["qT"], A)
                    pe.wait_ge(s["kT"], A)
                    pe.wait_ge(s["CT1"], A - 1)
                    pe.wait_ge(s["CT0"], A - 1)
                    for im in range(2):
                        for a in range(2):
                            for i in range(NI):
                                rows = slice(64 * a, 64 * a + 64)
                                mm = pe.matmul(p["p67"][64 * im:64 * im + 64, 512 * a + i * PATCHES:512 * a + (i + 1) * PATCHES],
                                               b["qT"][rows, i, PATCHES * im:PATCHES * im + SLOT], b["kT"][rows, i, PATCHES * im:PATCHES * (im + 1)],
                                               start=True, stop=True)
                    mm.then_inc(s["s_ps"], 1)
                    pe.wait_ge(s["imm"], 1)
                    pe.wait_ge(s["y"], A - 1)
                    values(0, p["p0"], s["v0_ps"])

            steps(pe, step)

        @block.vector
        def _(dve):
            dve.memset(b["ckT"][:, PAIR:], 0.0).then_inc(s["pads"], 1)
            dve.memset(b["qT"][:, :, PAIR:], 0.0).then_inc(s["pads"], 1)
            dve.memset(b["P"][:, :, :, PATCHES:], 0.0).then_inc(s["pads"], 1)
            dve.memset(keep["XT"][96:97, :, :], 1.0).then_inc(s["pads"], 1)
            dve.wait_ge(s["weights"], 16 * len(loads))
            dve.tensor_tensor(b["posb"][:], b["posb"][:], b["tokb"][:], ALU.add).then_inc(s["ready_pos"], 1)
            dve.wait_ge(s["ready_pos"], 1)

            def turned(ap):
                return ap.rearrange("p (u c) -> p u c", u=2)[:, :, 0:3 * PAIR].rearrange("p u (j r) -> p u j r", j=3)

            def six(ap):
                return ap.rearrange("p (u j) r -> p u j r", u=2)

            cos = b["cos"][:].rearrange("p (u j r) -> p u j r", u=1, j=1).to_broadcast([128, 2, 3, PAIR])
            sin = b["sin"][:].rearrange("p (u j r) -> p u j r", u=1, j=1).to_broadcast([128, 2, 3, PAIR])
            mask = b["mask"][:].rearrange("p (u j r) -> p u j r", u=1, j=1).to_broadcast([128, 2, NI, PATCHES])

            def step(A, B, T):
                if A is not None:
                    dve.wait_ge(s["conv"], A)
                    dve.wait_ge(s["hb"], A - 1)
                    dve.tensor_tensor(b["hs"][:], p["p1"][0:PAIR, 0:WIDTH], b["posb"][:], ALU.add).then_inc(s["h"], 1)
                if B is not None:
                    dve.wait_ge(s["pt1_ps"], B)
                    dve.tensor_copy(b["PT"][:, 1, :, :], p["p67"][:, 512:512 + NI * SLOT].rearrange("p (i r) -> p i r", i=NI)).then_inc(s["PT1"], 1)
                    dve.wait_ge(s["P"], B)
                    dve.tensor_reduce(b["z"][:], b["P"][:, :, :, 0:PATCHES].rearrange("p i a r -> p a i r"), AX.X, ALU.add).then_inc(s["z"], 1)
                    dve.wait_ge(s["z"], B)
                    dve.reciprocal(b["rz"][:], b["z"][:]).then_inc(s["rz"], 1)
                if A is not None:
                    dve.wait_ge(s["ckv"], A)
                    dve.bn_stats(b["st"][:], ckv_ps).then_inc(s["st"], 1)
                    dve.wait_ge(s["imm"], 1)
                    dve.wait_ge(s["st"], A)
                    dve.bn_aggr(b["mv"][:], b["st"][:]).then_inc(s["mv"], 1)
                    dve.wait_ge(s["mv"], A)
                    dve.tensor_scalar(b["ve"][:], b["mv"][:, 1:2], 1e-5, None, ALU.add).then_inc(s["ve"], 1)
                    dve.wait_ge(s["rstd"], A)
                    dve.tensor_scalar(b["ckn"][:], ckv_ps, b["mv"][:, 0:1], b["rstd"][:], ALU.subtract, ALU.mult).then_inc(s["ckn"], 1)
                    dve.wait_ge(s["q_ps"], A)
                    dve.tensor_tensor(six(b["r1"][:]), turned(p["p23"][:]), cos, ALU.mult).then_inc(s["rq1"], 1)
                    dve.tensor_tensor(six(b["r2"][:]), turned(p["p45"][:]), sin, ALU.mult).then_inc(s["rq2"], 1)
                    dve.wait_ge(s["ck_ps"], A)
                    dve.tensor_scalar(b["ckT"][:, 0:PAIR], ck_ps, b["lng"][:], b["lnb"][:], ALU.mult, ALU.add).then_inc(s["ckT"], 1)
                    dve.wait_ge(s["rq1"], A)
                    dve.wait_ge(s["rq2"], A)
                    dve.tensor_tensor(b["qT"][:, :, 0:PAIR], b["r1"][:], b["r2"][:], ALU.add).then_inc(s["qT"], 1)
                if B is not None:
                    dve.wait_ge(s["ctx_ps"], B)
                    dve.wait_ge(s["rz"], B)
                    for a, (ps, sem) in enumerate(((p["p0"], s["C0"]), (p["p1"], s["C1"]))):
                        dve.tensor_tensor(b["C"][:, :, a, :], ps[:, 0:NI * HD0].rearrange("p (i d) -> p i d", i=NI),
                                          b["rz"][:, a, :].unsqueeze(2).to_broadcast([128, NI, HD0]), ALU.mult).then_inc(sem, 1)
                if A is not None:
                    dve.wait_ge(s["k_ps"], A)
                    dve.wait_ge(s["qT"], A)
                    dve.tensor_tensor(six(b["r1"][:]), turned(p["p23"][:]), cos, ALU.mult).then_inc(s["rk1"], 1)
                    dve.tensor_tensor(six(b["r2"][:]), turned(p["p45"][:]), sin, ALU.mult).then_inc(s["rk2"], 1)
                if B is not None:
                    dve.wait_ge(s["ct_ps"], B)
                    dve.tensor_copy(packed(b["CT"][:, 3:6, :]), slots(p["p67"][:, 512:512 + 384], 3)).then_inc(s["CT1"], 1)
                if A is not None:
                    dve.wait_ge(s["rk1"], A)
                    dve.wait_ge(s["rk2"], A)
                    dve.tensor_tensor(b["kT"][:], b["r1"][:], b["r2"][:], ALU.add).then_inc(s["kT"], 1)
                if B is not None:
                    dve.wait_ge(s["wo_ps"], B)
                    dve.wait_ge(s["hb"], B)
                    dve.tensor_tensor(b["y"][:], p["p0"][0:PAIR, 0:WIDTH], b["hb"][:], ALU.add).then_inc(s["y"], 1)
                    dve.wait_ge(s["y"], B)
                    dve.bn_stats(b["st2"][:], b["y"][:]).then_inc(s["st2"], 1)
                    dve.wait_ge(s["imm"], 1)
                    dve.wait_ge(s["st2"], B)
                    dve.bn_aggr(b["mv2"][:], b["st2"][:]).then_inc(s["mv2"], 1)
                    dve.wait_ge(s["mv2"], B)
                    dve.tensor_scalar(b["ve2"][:], b["mv2"][:, 1:2], 1e-5, None, ALU.add).then_inc(s["ve2"], 1)
                if A is not None:
                    dve.wait_ge(s["s_ps"], A)
                    dve.tensor_tensor(b["E"][:], heads_of(p["p67"][:]), mask, ALU.add).then_inc(s["masked"], 1)
                    dve.wait_ge(s["masked"], A)
                    dve.tensor_reduce(b["mx"][:], b["E"][:], AX.X, ALU.max).then_inc(s["mx"], 1)
                    dve.wait_ge(s["mx"], A)
                    dve.tensor_tensor(b["E"][:], b["E"][:], b["mx"][:].unsqueeze(3).to_broadcast([128, 2, NI, PATCHES]), ALU.subtract).then_inc(s["shifted"], 1)
                if B is not None:
                    dve.wait_ge(s["rstd2"], B)
                    dve.wait_ge(s["X"], B - 1)
                    dve.wait_ge(s["stored"], (B - 1) * 16)
                    dve.tensor_scalar(b["xn"][:], b["y"][:], b["mv2"][:, 0:1], b["rstd2"][:], ALU.subtract, ALU.mult).then_inc(s["xn"], 1)

            steps(dve, step)

        @block.scalar
        def _(act):
            act.preload_act_table(ACT.Exp)

            def step(A, B, T):
                if A is not None:
                    act.wait_ge(s["hT_ps"], A)
                    act.activation(b["hT"][:], p["p0"][0:HALF, 0:2 * PAIR].rearrange("p (c r) -> p c r", c=2), ACT.Copy).then_inc(s["hT"], 1)
                if B is not None:
                    act.wait_ge(s["pt0_ps"], B)
                    act.activation(b["PT"][:, 0, :, :], p["p67"][:, 0:NI * SLOT].rearrange("p (i r) -> p i r", i=NI), ACT.Copy).then_inc(s["PT0"], 1)
                if T is not None:
                    act.wait_ge(s["x_ps"], T)
                    act.activation(keep["XT"][0:HALF, :, bass.ds((T - 2) * PAIR, PAIR)], p["p1"][0:HALF, 0:2 * PAIR].rearrange("p (c r) -> p c r", c=2),
                                   ACT.Copy).then_inc(s["xT"], 1)
                    act.activation(keep["X"][:, bass.ds(T - 2, 1), :], b["xn"][:].unsqueeze(1), ACT.Copy).then_inc(s["X"], 1)
                if B is not None:
                    act.wait_ge(s["ct_ps"], B)
                    act.activation(packed(b["CT"][:, 0:3, :]), slots(p["p67"][:, 0:384], 3), ACT.Copy).then_inc(s["CT0"], 1)
                if A is not None:
                    for im, ps, ready, sem in ((1, p["p1"], s["v1_ps"], s["V1"]), (0, p["p0"], s["v0_ps"], s["V0"])):
                        act.wait_ge(ready, A)
                        act.activation(b["V"][:, im, :, :], ps[:, 0:NI * HD0].rearrange("p (i d) -> p i d", i=NI), ACT.Copy).then_inc(sem, 1)
                    act.wait_ge(s["shifted"], A)
                    act.activation(b["P"][:, :, :, 0:PATCHES].rearrange("p i a r -> p a i r"), b["E"][:], ACT.Exp, scale=HD0 ** -0.5).then_inc(s["P"], 1)

            steps(act, step)

        @block.gpsimd
        def _(pool):
            pool.sem_inc(s["imm"], 1)
            pool.wait_ge(s["weights"], 16 * len(loads))

            def step(A, B, T):
                if A is not None:
                    pool.wait_ge(s["ve"], A)
                    pool.tensor_tensor(b["rstd"][:], b["ve"][:], keep["half"][:], ALU.pow).then_inc(s["rstd"], 1)
                if B is not None:
                    pool.wait_ge(s["ve2"], B)
                    pool.tensor_tensor(b["rstd2"][:], b["ve2"][:], keep["half"][:], ALU.pow).then_inc(s["rstd2"], 1)
                if A is not None:
                    pool.wait_ge(s["h"], A)
                    pool.wait_ge(s["y"], A - 1)
                    pool.tensor_tensor(b["hb"][:], b["hs"][:], b["bo"][:], ALU.add).then_inc(s["hb"], 1)

            steps(pool, step)




def block_router_and_shared_expert(nc, d, keep):
    with ExitStack() as ctx:
        NS = SHARED // FC
        b = buffers(
            ctx, nc, "rt", wg=(HALF, 2, EXPERTS), ebias=(PAIR, EXPERTS), before=(PAIR, PAIR), ones=(PAIR, PAIR), slot0=(PAIR, EXPERTS),
            wsg=(HALF, 2, SHARED), wsu=(HALF, 2, SHARED), wsd=(FC, NS, WIDTH), xs=(HALF, 2, PAIR), sig=(PAIR, EXPERTS),
            choice=(PAIR, EXPERTS + 2), m8=(PAIR, 8), left=(PAIR, EXPERTS + 2), mask=(PAIR, EXPERTS), pos=(PAIR, EXPERTS),
            run=(PAIR, EXPERTS), wm=(PAIR, EXPERTS), sm=(PAIR, 1), sm1=(PAIR, 1), rs=(PAIR, 1), rs25=(PAIR, 1), sel=(PAIR, EXPERTS),
            far=(PAIR, EXPERTS), row=(PAIR, EXPERTS), row2=(PAIR, EXPERTS), code=(PAIR, EXPERTS), wsel=(PAIR, EXPERTS), s8=(PAIR, 8),
            hit=(PAIR, TOPK, EXPERTS), w6=(PAIR, TOPK), none=(PAIR, 8), sg=(FC, NS, PAIR), inter=(FC, NS, PAIR))
        into = ctx.enter_context(nc.sbuf_tensor("rt_into", [PAIR, 8], I32))
        tokens = ctx.enter_context(nc.sbuf_tensor("rt_tokens", [PAIR, TURNS], I32))
        token = ctx.enter_context(nc.sbuf_tensor("rt_token", [PAIR, 1], I32))
        zeros = ctx.enter_context(nc.sbuf_tensor("rt_zeros", [CAPH, 2 * EXPERTS], I32))
        p = banks(ctx, nc, "rt", p0=512, p1=512, p23=1024, p45=1024, p6=512, p7=512)
        s = signals(
            ctx, nc, "rt", "xs logits sig choice top8 top6 left mask pos_ps pos run wm sm rs rs25 sel far row "
            "row2 code wsel s8 w6 none into rows token landed kept g_ps u_ps sg inter out_ps Y", setup="imm weights start zeros cleared scattered")
        loads = [(b["wg"], d["wg"]), (b["ebias"], d["e_bias"]), (b["before"], d["before"]), (b["ones"], d["ones"]), (b["slot0"], d["slot0"]), (b["wsg"], d["wsg"]),
                 (b["wsu"], d["wsu"]), (b["wsd"], d["wsd"]), (tokens, d["token"])]
        block = ctx.enter_context(nc.Block())

        @block.sync
        def _(sp):
            for to, src in loads:
                sp.dma_start(to[:], src).then_inc(s["weights"], 16)
            sp.wait_ge(s["zeros"], 1)
            sp.dma_start(d["slot_token"], zeros[:]).then_inc(s["cleared"], 16)
            sp.wait_ge(s["cleared"], 16)

        @block.scalar
        def _(act):
            with act.Fori(2, TURNS + 2) as n:
                m, t = n - 1, n - 2
                act.wait_ge(s["u_ps"], m)
                act.activation(b["xs"][:], keep["XT"][0:HALF, :, bass.ds(t * PAIR, PAIR)], ACT.Copy).then_inc(s["xs"], 1)
                act.wait_ge(s["logits"], n)
                act.wait_ge(s["wsel"], m)
                act.activation(b["sig"][:], p["p0"][0:PAIR, 0:EXPERTS], ACT.Sigmoid).then_inc(s["sig"], 1)
                act.wait_ge(s["g_ps"], n)
                act.wait_ge(s["inter"], m)
                act.activation(b["sg"][:].rearrange("p (u j) r -> p u j r", u=2),
                               p["p23"][0:FC, :].rearrange("p (u c) -> p u c", u=2)[:, :, 0:4 * PAIR].rearrange("p u (j r) -> p u j r", j=4),
                               ACT.Silu).then_inc(s["sg"], 1)

        @block.tensor
        def _(pe):
            pe.wait_ge(s["weights"], 16 * len(loads))
            with pe.Fori(2, TURNS + 2) as n:
                m, t = n - 1, n - 2
                pe.wait_ge(s["xs"], n)
                pe.wait_ge(s["sig"], m)
                for c in range(2):
                    mm = pe.matmul(p["p0"][0:PAIR, 0:EXPERTS], b["xs"][:, c, :], b["wg"][:, c, :], start=c == 0, stop=c == 1)
                mm.then_inc(s["logits"], 1)
                for w, ps, free, sem in ((b["wsg"], p["p23"], s["sg"], s["g_ps"]), (b["wsu"], p["p45"], s["inter"], s["u_ps"])):
                    pe.wait_ge(free, m)
                    for j in range(NS):
                        at = (j // 4) * 512 + (j % 4) * PAIR
                        for c in range(2):
                            mm = pe.matmul(ps[0:FC, at:at + PAIR], w[:, c, j * FC:(j + 1) * FC], b["xs"][:, c, :], start=c == 0, stop=c == 1)
                    mm.then_inc(sem, 1)
                pe.wait_ge(s["mask"], n)
                pe.wait_ge(s["run"], m)
                pe.matmul(p["p1"][0:PAIR, 0:EXPERTS], b["before"][:], b["mask"][:], start=True, stop=True)
                pe.matmul(p["p1"][0:PAIR, EXPERTS:2 * EXPERTS], b["ones"][:], b["mask"][:], start=True, stop=True).then_inc(s["pos_ps"], 1)
                pe.wait_ge(s["inter"], n)
                pe.wait_ge(s["Y"], m)
                for j in range(NS):
                    mm = pe.matmul(p["p6"][0:PAIR, 0:WIDTH], b["inter"][:, j, :], b["wsd"][:, j, :], start=j == 0, stop=j == NS - 1)
                mm.then_inc(s["out_ps"], 1)

        @block.vector
        def _(dve):
            dve.memset(zeros[:], 0).then_inc(s["zeros"], 1)
            dve.memset(b["choice"][:, EXPERTS:], -BIG).then_inc(s["start"], 1)
            dve.memset(b["run"][:], 0.0).then_inc(s["start"], 1)
            dve.wait_ge(s["start"], 2)
            dve.wait_ge(s["weights"], 16 * len(loads))
            with dve.Fori(2, TURNS + 2) as n:
                m, t = n - 1, n - 2
                dve.wait_ge(s["sig"], n)
                dve.tensor_tensor(b["choice"][:, 0:EXPERTS], b["sig"][:], b["ebias"][:], ALU.add).then_inc(s["choice"], 1)
                dve.wait_ge(s["imm"], 1)
                dve.wait_ge(s["choice"], n)
                dve.max(b["m8"][:], b["choice"][:]).then_inc(s["top8"], 1)
                dve.wait_ge(s["top8"], n)
                dve.memset(b["m8"][:, TOPK:8], -BIG).then_inc(s["top6"], 1)
                dve.wait_ge(s["imm"], 1)
                dve.wait_ge(s["top6"], n)
                dve.match_replace(b["left"][:], b["m8"][:], b["choice"][:], -2 * BIG).then_inc(s["left"], 1)
                dve.wait_ge(s["left"], n)
                dve.wait_ge(s["pos_ps"], m)
                dve.tensor_tensor(b["mask"][:], b["left"][:, 0:EXPERTS], b["choice"][:, 0:EXPERTS], ALU.not_equal).then_inc(s["mask"], 1)
                dve.wait_ge(s["mask"], n)
                dve.tensor_tensor_reduce(b["wm"][:], b["sig"][:], b["mask"][:], 1.0, 0.0, ALU.mult, ALU.add, b["sm"][:]).then_inc(s["wm"], 1)
                dve.wait_ge(s["wm"], n)
                dve.tensor_scalar(b["sm1"][:], b["sm"][:], 1e-20, None, ALU.add).then_inc(s["sm"], 1)
                dve.wait_ge(s["sm"], n)
                dve.reciprocal(b["rs"][:], b["sm1"][:]).then_inc(s["rs"], 1)
                dve.wait_ge(s["rs"], n)
                dve.tensor_scalar(b["rs25"][:], b["rs"][:], 2.5, None, ALU.mult).then_inc(s["rs25"], 1)
                dve.wait_ge(s["sg"], n)
                dve.wait_ge(s["u_ps"], n)
                dve.wait_ge(s["out_ps"], m)
                dve.tensor_tensor(b["inter"][:].rearrange("p (u j) r -> p u j r", u=2),
                                  p["p45"][0:FC, :].rearrange("p (u c) -> p u c", u=2)[:, :, 0:4 * PAIR].rearrange("p u (j r) -> p u j r", j=4),
                                  b["sg"][:].rearrange("p (u j) r -> p u j r", u=2), ALU.mult).then_inc(s["inter"], 1)
                dve.wait_ge(s["pos_ps"], n)
                dve.tensor_tensor(b["pos"][:], p["p1"][0:PAIR, 0:EXPERTS], b["run"][:], ALU.add).then_inc(s["pos"], 1)
                dve.wait_ge(s["pos"], n)
                dve.tensor_tensor(b["run"][:], p["p1"][0:PAIR, EXPERTS:2 * EXPERTS], b["run"][:], ALU.add).then_inc(s["run"], 1)
                dve.scalar_tensor_tensor(b["sel"][:], b["pos"][:], float(CAP), b["mask"][:], ALU.is_lt, ALU.mult).then_inc(s["sel"], 1)
                dve.tensor_scalar(b["far"][:], b["pos"][:], float(CAPH), -float(CAPH * 2 * EXPERTS - 1), ALU.is_ge, ALU.mult).then_inc(s["far"], 1)
                dve.scalar_tensor_tensor(b["row"][:], b["pos"][:], 2.0 * EXPERTS, b["slot0"][:], ALU.mult, ALU.add).then_inc(s["row"], 1)
                dve.wait_ge(s["far"], n)
                dve.wait_ge(s["row"], n)
                dve.tensor_tensor(b["row2"][:], b["row"][:], b["far"][:], ALU.add).then_inc(s["row2"], 1)
                dve.wait_ge(s["row2"], n)
                dve.wait_ge(s["sel"], n)
                dve.scalar_tensor_tensor(b["code"][:], b["row2"][:], 1.0, b["sel"][:], ALU.add, ALU.mult).then_inc(s["code"], 1)
                dve.wait_ge(s["rs25"], n)
                dve.scalar_tensor_tensor(b["wsel"][:], b["wm"][:], b["rs25"][:], b["sel"][:], ALU.mult, ALU.mult).then_inc(s["wsel"], 1)
                dve.wait_ge(s["imm"], 1)
                dve.wait_ge(s["code"], n)
                dve.max(b["s8"][:], b["code"][:]).then_inc(s["s8"], 1)
                dve.wait_ge(s["s8"], n)
                dve.wait_ge(s["wsel"], n)
                dve.wait_ge(s["kept"], m)
                for k in range(TOPK):
                    ins = dve.scalar_tensor_tensor(b["hit"][:, k, :], b["code"][:], b["s8"][:, k:k + 1], b["wsel"][:], ALU.is_equal, ALU.mult,
                                                   accum_out=b["w6"][:, k:k + 1])
                ins.then_inc(s["w6"], 1)
                dve.tensor_scalar(b["none"][:], b["s8"][:], 0.0, 1.0e6, ALU.is_equal, ALU.mult).then_inc(s["none"], 1)
                dve.wait_ge(s["none"], n)
                dve.wait_ge(s["landed"], m)
                dve.scalar_tensor_tensor(into[:], b["s8"][:], -1.0, b["none"][:], ALU.add, ALU.add).then_inc(s["into"], 1)
                dve.tensor_scalar(keep["rows"][:, t, :], b["s8"][:], -1.0, 0.0, ALU.add, ALU.max).then_inc(s["rows"], 1)
                dve.wait_ge(s["out_ps"], n)
                dve.tensor_tensor(keep["Y"][:, t, :], p["p6"][0:PAIR, 0:WIDTH], keep["X"][:, t, :], ALU.add).then_inc(s["Y"], 1)

        @block.gpsimd
        def _(pool):
            pool.sem_inc(s["imm"], 1)
            pool.wait_ge(s["weights"], 16 * len(loads))
            pool.wait_ge(s["cleared"], 16)
            with pool.Fori(2, TURNS + 2) as n:
                m, t = n - 1, n - 2
                pool.tensor_copy(token[:], tokens[:, bass.ds(t, 1)]).then_inc(s["token"], 1)
                pool.wait_ge(s["imm"], 1)
                pool.wait_ge(s["w6"], n)
                pool.tensor_copy(keep["w6"][:, t, :], b["w6"][:]).then_inc(s["kept"], 1)
                pool.wait_ge(s["imm"], 1)
                pool.wait_ge(s["into"], n)
                pool.wait_ge(s["token"], n)
                for k in range(TOPK):
                    pool.indirect_dma_start(d["slot_token_rows"], bass.IndirectOffsetOnAxis(ap=into[:, k:k + 1], axis=0), token[:], None,
                                            bounds_check=ROWS - 1, oob_is_err=False).then_inc(s["scattered"], 16)
                pool.wait_ge(s["scattered"], 16 * TOPK * m)
                pool.sem_inc(s["landed"], 1)
            pool.wait_ge(s["scattered"], 16 * TOPK * TURNS)


def block_routed_experts(nc, d, keep):
    with ExitStack() as ctx:
        b = buffers(ctx, nc, "ex", wgu=(HALF, 2, 2, 2 * INTER), wdn=(FC, 2, NF, WIDTH), xe=(CAPH, 2, WIDTH), xT=(HALF, 2, CAP),
                    sg=(FC, NF, CAP), inter=(FC, NF, CAP), ys=(CAPH, 2, WIDTH))
        ids = ctx.enter_context(nc.sbuf_tensor("ex_ids", [CAPH, 2 * EXPERTS + 2], I32))
        idc = ctx.enter_context(nc.sbuf_tensor("ex_idc", [CAPH, 2], I32))
        p = banks(ctx, nc, "ex", pT=512, gu=2048, y=512)
        s = signals(ctx, nc, "ex", "idc x_ps xT gu0 gu1 gu2 gu3 sg0 sg1 sg2 sg3 in0 in1 in2 in3 y_ps ys", dma="stored", setup="pad ids w0 w1 xe")
        gu, sg, inter, w = (s["gu0"], s["gu1"], s["gu2"], s["gu3"]), (s["sg0"], s["sg1"], s["sg2"], s["sg3"]), (s["in0"], s["in1"], s["in2"], s["in3"]), (s["w0"], s["w1"])
        block = ctx.enter_context(nc.Block())

        def load(sp, e, u):
            sp.dma_start(b["wgu"][:, u], d["wgu"][e]).then_inc(w[u], 16)
            sp.dma_start(b["wdn"][:, u], d["wdn"][e]).then_inc(w[u], 16)

        @block.sync
        def _(sp):
            sp.wait_ge(s["pad"], 1)
            sp.dma_start(ids[:, 0:2 * EXPERTS], d["slot_token"]).then_inc(s["ids"], 16)
            for u in range(2):
                load(sp, u, u)
            def store(e):
                sp.wait_ge(s["pad"], 1)
                sp.wait_ge(s["ys"], e + 2)
                sp.dma_start(d["slot_out"][:, bass.ds(2 * e, 2), :], b["ys"][:]).then_inc(s["stored"], 16)

            with sp.Fori(0, EXPERTS // 2 - 1) as i:
                for u in range(2):
                    store(2 * i + u)
                    load(sp, 2 * i + u + 2, u)
            for u in range(2):
                store(EXPERTS - 2 + u)
            sp.wait_ge(s["stored"], 16 * (EXPERTS + 1))

        @block.gpsimd
        def _(pool):
            pool.memset(ids[:, 2 * EXPERTS:], 0).then_inc(s["pad"], 1)
            pool.wait_ge(s["ids"], 16)
            with pool.Fori(2, EXPERTS + 3) as n:
                e = n - 2
                pool.wait_ge(s["pad"], 1)
                pool.wait_ge(s["x_ps"], n - 1)
                pool.tensor_copy(idc[:], ids[:, bass.ds(2 * e, 2)]).then_inc(s["idc"], 1)
                pool.wait_ge(s["pad"], 1)
                pool.wait_ge(s["idc"], n)
                for h in range(2):
                    pool.indirect_dma_start(b["xe"][:, h, :], None, d["x_flat"], bass.IndirectOffsetOnAxis(ap=idc[:, h:h + 1], axis=0),
                                            bounds_check=TOKENS - 1, oob_is_err=False).then_inc(s["xe"], 16)
            pool.wait_ge(s["xe"], 32 * (EXPERTS + 1))

        @block.tensor
        def _(pe):
            def turn_rows(e):
                pe.wait_ge(s["xe"], 32 * (e + 1))
                pe.wait_ge(s["xT"], e + 1)
                for h in range(2):
                    for c in range(2):
                        mm = pe.transpose(p["pT"][0:HALF, c * CAP + h * CAPH:c * CAP + (h + 1) * CAPH], b["xe"][:, h, c * HALF:(c + 1) * HALF],
                                          keep["ident"][0:CAPH, 0:CAPH])
                mm.then_inc(s["x_ps"], 1)

            turn_rows(0)
            with pe.Fori(0, EXPERTS // 2) as i:
                for u in range(2):
                    e = 2 * i + u
                    pe.wait_ge(w[u], 32 * (i + 1))
                    pe.wait_ge(s["xT"], e + 2)
                    for f in range(NF):
                        pe.wait_ge(inter[f], e + 1)
                        for half in range(2):
                            for c in range(2):
                                mm = pe.matmul(p["gu"][0:FC, 512 * f + half * CAP:512 * f + (half + 1) * CAP],
                                               b["wgu"][:, u, c, half * INTER + f * FC:half * INTER + (f + 1) * FC], b["xT"][:, c, :],
                                               start=c == 0, stop=c == 1)
                        mm.then_inc(gu[f], 1)
                    turn_rows(e + 1)
                    pe.wait_ge(s["ys"], e + 1)
                    for h in range(2):
                        for f in range(NF):
                            if h == 0:
                                pe.wait_ge(inter[f], e + 2)
                            mm = pe.matmul(p["y"][0:CAPH, h * WIDTH:(h + 1) * WIDTH], b["inter"][:, f, h * CAPH:(h + 1) * CAPH], b["wdn"][:, u, f, :],
                                           start=f == 0, stop=f == NF - 1)
                    mm.then_inc(s["y_ps"], 1)

        @block.scalar
        def _(act):
            with act.Fori(2, EXPERTS + 2) as n:
                for f in range(NF):
                    act.wait_ge(gu[f], n)
                    act.wait_ge(inter[f], n - 1)
                    act.activation(b["sg"][:, f, :], p["gu"][0:FC, 512 * f:512 * f + CAP], ACT.Silu).then_inc(sg[f], 1)
                act.wait_ge(s["y_ps"], n)
                act.wait_ge(s["stored"], 16 * (n - 1))
                act.activation(b["ys"][:].rearrange("p h w -> p (h w)"), p["y"][0:CAPH, 0:2 * WIDTH], ACT.Copy).then_inc(s["ys"], 1)

        @block.vector
        def _(dve):
            def turned(n):
                dve.wait_ge(s["x_ps"], n)
                dve.tensor_copy(b["xT"][:].rearrange("p c r -> p (c r)"), p["pT"][0:HALF, 0:2 * CAP]).then_inc(s["xT"], 1)

            turned(2)
            with dve.Fori(2, EXPERTS + 2) as n:
                dve.wait_ge(s["y_ps"], n - 1)
                for f in range(NF):
                    dve.wait_ge(sg[f], n)
                    dve.tensor_tensor(b["inter"][:, f, :], p["gu"][0:FC, 512 * f + CAP:512 * f + 2 * CAP], b["sg"][:, f, :], ALU.mult).then_inc(inter[f], 1)
                turned(n + 1)


def block_combine(nc, d, keep):
    with ExitStack() as ctx:
        b = buffers(ctx, nc, "cb", G=(PAIR, 2, TOPK, WIDTH), w6=(PAIR, TOPK), a=(PAIR, TOPK, WIDTH), st=(PAIR, 6), mv=(PAIR, 2),
                    ve=(PAIR, 1), rstd=(PAIR, 1), xn=(PAIR, WIDTH))
        rows = ctx.enter_context(nc.sbuf_tensor("cb_rows", [PAIR, 2, 8], I32))
        p = banks(ctx, nc, "cb", p1=512)
        s = signals(ctx, nc, "cb", "w6 a0 a1 a2 a3 a4 a5 st mv ve rstd xn x_ps xT X", setup="imm got0 got1 rows0 rows1")
        got, taken, added = (s["got0"], s["got1"]), (s["rows0"], s["rows1"]), (s["a0"], s["a1"], s["a2"], s["a3"], s["a4"], s["a5"])
        block = ctx.enter_context(nc.Block())

        @block.gpsimd
        def _(pool):
            pool.sem_inc(s["imm"], 1)

            def gather(i, u):
                pool.wait_ge(s["imm"], 1)
                if not isinstance(i, int):
                    pool.wait_ge(s["a5"], 2 * i + u - 2)
                pool.tensor_copy(rows[:, u], keep["rows"][:, bass.ds(2 * i + u - 2, 1), :].rearrange("p o k -> p (o k)")).then_inc(taken[u], 1)
                for k in range(TOPK):
                    pool.wait_ge(s["imm"], 1)
                    pool.wait_ge(taken[u], i)
                    pool.indirect_dma_start(b["G"][:, u, k, :], None, d["slot_out_rows"], bass.IndirectOffsetOnAxis(ap=rows[:, u, k:k + 1], axis=0),
                                            bounds_check=ROWS - 1, oob_is_err=False).then_inc(got[u], 16)

            def rstd(n):
                pool.wait_ge(s["ve"], n)
                pool.tensor_tensor(b["rstd"][:], b["ve"][:], keep["half"][:], ALU.pow).then_inc(s["rstd"], 1)

            gather(1, 0)
            gather(1, 1)
            with pool.Fori(2, TURNS // 2 + 1) as i:
                for u in range(2):
                    rstd(2 * i + u - 2)
                    gather(i, u)
            rstd(TURNS)
            rstd(TURNS + 1)

        @block.scalar
        def _(act):
            with act.Fori(2, TURNS + 2) as n:
                m, t = n - 1, n - 2
                act.wait_ge(s["a5"], m)
                act.activation(b["w6"][:], keep["w6"][:, t, :], ACT.Copy).then_inc(s["w6"], 1)
                act.wait_ge(s["x_ps"], n)
                act.activation(keep["XT"][0:HALF, :, bass.ds(t * PAIR, PAIR)], p["p1"][0:HALF, 0:2 * PAIR].rearrange("p (c r) -> p c r", c=2),
                               ACT.Copy).then_inc(s["xT"], 1)
                act.activation(keep["X"][:, t, :], b["xn"][:], ACT.Copy).then_inc(s["X"], 1)

        @block.tensor
        def _(pe):
            with pe.Fori(2, TURNS + 2) as n:
                pe.wait_ge(s["imm"], 1)
                pe.wait_ge(s["xn"], n)
                pe.wait_ge(s["xT"], n - 1)
                for c in range(2):
                    mm = pe.transpose(p["p1"][0:HALF, c * PAIR:(c + 1) * PAIR], b["xn"][:, c * HALF:(c + 1) * HALF], keep["ident"][0:PAIR, 0:PAIR])
                mm.then_inc(s["x_ps"], 1)

        @block.vector
        def _(dve):
            with dve.Fori(1, TURNS // 2 + 1) as i:
                for u in range(2):
                    n = 2 * i + u
                    t = n - 2
                    dve.wait_ge(s["w6"], n)
                    dve.wait_ge(got[u], 16 * TOPK * i)
                    for k in range(TOPK):
                        if k:
                            dve.wait_ge(added[k - 1], n)
                        before = b["a"][:, k - 1, :] if k else keep["Y"][:, bass.ds(t, 1), :].rearrange("p o w -> p (o w)")
                        dve.scalar_tensor_tensor(b["a"][:, k, :], b["G"][:, u, k, :], b["w6"][:, k:k + 1], before, ALU.mult, ALU.add).then_inc(added[k], 1)
                    dve.wait_ge(s["a5"], n)
                    dve.bn_stats(b["st"][:], b["a"][:, 5, :]).then_inc(s["st"], 1)
                    dve.wait_ge(s["imm"], 1)
                    dve.wait_ge(s["st"], n)
                    dve.bn_aggr(b["mv"][:], b["st"][:]).then_inc(s["mv"], 1)
                    dve.wait_ge(s["mv"], n)
                    dve.tensor_scalar(b["ve"][:], b["mv"][:, 1:2], 1e-5, None, ALU.add).then_inc(s["ve"], 1)
                    dve.wait_ge(s["rstd"], n)
                    dve.wait_ge(s["X"], n - 1)
                    dve.tensor_scalar(b["xn"][:], b["a"][:, 5, :], b["mv"][:, 0:1], b["rstd"][:], ALU.subtract, ALU.mult).then_inc(s["xn"], 1)


def norm(dve, b, s, n, prev, y, eps, to, free=()):
    dve.wait_ge(s["y"], n)
    dve.bn_stats(b["st"][:], y).then_inc(s["st"], 1)
    dve.wait_ge(s["imm"], 1)
    dve.wait_ge(s["st"], n)
    dve.bn_aggr(b["mv"][:], b["st"][:]).then_inc(s["mv"], 1)
    dve.wait_ge(s["mv"], n)
    dve.tensor_scalar(b["ve"][:], b["mv"][:, 1:2], eps, None, ALU.add).then_inc(s["ve"], 1)
    dve.wait_ge(s["rstd"], n)
    for sem in free:
        dve.wait_ge(sem, prev)
    return dve.tensor_scalar(to, y, b["mv"][:, 0:1], b["rstd"][:], ALU.subtract, ALU.mult)


def pool_rstd(pool, b, s, n, keep):
    pool.wait_ge(s["ve"], n)
    pool.tensor_tensor(b["rstd"][:], b["ve"][:], keep["half"][:], ALU.pow).then_inc(s["rstd"], 1)


def norm_group(dve, b, s, n, eps, to, sem, free=()):
    dve.wait_ge(s["y"], n)
    for r in range(GROUP):
        ins = dve.bn_stats(b["st"][:, r], b["y"][:, r])
    ins.then_inc(s["st"], 1)
    dve.wait_ge(s["imm"], 1)
    dve.wait_ge(s["st"], n)
    for r in range(GROUP):
        ins = dve.bn_aggr(b["mv"][:, r], b["st"][:, r])
    ins.then_inc(s["mv"], 1)
    dve.wait_ge(s["mv"], n)
    dve.tensor_scalar(b["ve"][:], b["mv"][:, :, 1], eps, None, ALU.add).then_inc(s["ve"], 1)
    for reader, count in free:
        dve.wait_ge(reader, count)
    dve.wait_ge(s["rstd"], n)
    for r in range(GROUP):
        dve.tensor_scalar(to[:, r], b["y"][:, r], b["mv"][:, r, 0:1], b["rstd"][:, r:r + 1], ALU.subtract, ALU.mult).then_inc(sem, 1)


def pool_rstd_group(pool, b, s, n, keep):
    pool.wait_ge(s["ve"], n)
    pool.tensor_tensor(b["rstd"][:], b["ve"][:], keep["half"][:].to_broadcast([PAIR, GROUP]), ALU.pow).then_inc(s["rstd"], 1)


def block_bert(nc, d, keep):
    with ExitStack() as ctx:
        b = buffers(
            ctx, nc, "ba", wq=(HALF + 1, 2, WIDTH), wk=(HALF + 1, 2, WIDTH), wc=(HALF + 1, 2, WIDTH), wv=(HALF + 1, 2, WIDTH),
            wo=(HALF, 2, WIDTH), rows=(PAIR, 6, WIDTH), own=(HALF, NI), block16=(HALF, HALF), eye=(128, PATCHES),
            xs=(HALF + 1, 2, 128), hb=(PAIR, WIDTH), qT=(HALF, 2, 128), kT=(HALF, 2, PAIR), kd=(HALF, 2, NI, PAIR), c=(HALF, 2, PAIR), c2=(HALF, 2, PAIR),
            n2=(HALF, 2 * PAIR), rn=(HALF, 2 * PAIR), cT=(HALF, 2, 128), cd=(HALF, 2, NI, PAIR), V=(128, 2, NI, 2, 16),
            E1=(128, 2, NI, PATCHES), E2=(128, 2, NI, PATCHES), mx=(128, 2, NI), z1=(128, 2, NI), z2=(128, 2, NI), rz1=(128, 2, NI),
            rz2=(128, 2, NI), P=(128, NI, 2, SLOT), PT=(128, 2, NI, SLOT), C=(128, 2, HALF), CT=(HALF, 2, PAIR), y=(PAIR, WIDTH),
            st=(PAIR, 6), mv=(PAIR, 2), ve=(PAIR, 1), rstd=(PAIR, 1), yn=(PAIR, WIDTH), yg=(PAIR, WIDTH), xn=(PAIR, WIDTH))
        f = buffers(
            ctx, nc, "bf", wi=(HALF + 1, 2, FFN), wo2=(128, NFF, WIDTH), h=(128, NFF, GCOLS), hb=(PAIR, GROUP, WIDTH),
            y=(PAIR, GROUP, WIDTH), st=(PAIR, GROUP, 6), mv=(PAIR, GROUP, 2), ve=(PAIR, GROUP), rstd=(PAIR, GROUP),
            yn=(PAIR, GROUP, WIDTH), yg=(PAIR, GROUP, WIDTH), xn=(PAIR, GROUP, WIDTH))
        p = banks(ctx, nc, "ba", p0=512, p1=512, p2=512, p3=512, p45=1024, p67=1024)
        s = signals(
            ctx, nc, "ba", "xs hb q_ps k_ps c_ps v_ps qT kT kd0 kd1 c c2 n2_ps n2 rn cT cd V s1_ps s2_ps mx "
            "shifted E2 E1 E1x z1 z2 rz1 rz2 P1 P2 P pt_ps PT0 PT1 ctx_ps C ct_ps CT wo_ps y st mv ve rstd yn yg xn x_ps xT X",
            setup="imm consts pads saved attn_w")
        g = signals(ctx, nc, "bf", "h0 h1 h2 h3 h4 h5 a0 a1 a2 a3 a4 a5 hb out_ps y st mv ve rstd yn yg xn x_ps0 x_ps1 xT0 xT1 X",
                    setup="ffn_w")
        h_ps, h_sb = (g["h0"], g["h1"], g["h2"], g["h3"], g["h4"], g["h5"]), (g["a0"], g["a1"], g["a2"], g["a3"], g["a4"], g["a5"])
        x_ps, xT = (g["x_ps0"], g["x_ps1"]), (g["xT0"], g["xT1"])
        h_bank = [p["p0"][:], p["p1"][:], p["p2"][:], p["p3"][:], p["p45"][:, 0:512], p["p45"][:, 512:1024]]
        consts = [(b["own"], d["own"]), (b["block16"], d["block16"]), (b["eye"], d["eye"])]
        SPLIT = 4
        AW, FW = 6, 2
        block = ctx.enter_context(nc.Block())

        def attention_steps(engine, l, step):
            first, last = TURNS * (l - 1) + 2, TURNS * l + 1
            step(first, None, None, first - 1, 0)
            step(first + 1, first, None, first - 1, 1)
            with engine.Fori(2, TURNS - 1) as q:
                n = TURNS * (l - 1) + q + 2
                step(n, n - 1, n - 2, n - 2, q)
            step(last, last - 1, last - 2, last - 2, TURNS - 1)
            step(None, last, last - 1, last - 1, TURNS)
            step(None, None, last, last, TURNS + 1)

        def mlp_steps(engine, l, step):
            first = GROUPS * (l - 1) + 2
            step(first, None, 0)
            with engine.Fori(1, GROUPS) as q:
                n = GROUPS * (l - 1) + q + 2
                step(n, n - 1, q)
            step(None, GROUPS * l + 1, GROUPS)

        @block.sync
        def _(sp):
            for to, src in consts:
                sp.dma_start(to[:], src).then_inc(s["consts"], 16)

            def load_attention(l):
                for to, src in ((b["wq"], d["bwq"]), (b["wk"], d["bwk"]), (b["wc"], d["bwc"]), (b["wv"], d["bwv"]), (b["wo"], d["bwo"]), (b["rows"], d["brows"])):
                    sp.dma_start(to[:], src[l]).then_inc(s["attn_w"], 16)

            def load_ffn(l):
                for to, src in ((f["wi"], d["bwi"]), (f["wo2"], d["bwo2"])):
                    sp.dma_start(to[:], src[l]).then_inc(g["ffn_w"], 16)

            load_attention(0)
            load_ffn(0)
            with sp.Fori(1, LAYERS) as l:
                sp.wait_ge(s["imm"], 1)
                sp.wait_ge(g["xn"], l * GROUPS + 1)
                load_attention(l)
                sp.wait_ge(g["out_ps"], l * TURNS + 1)
                load_ffn(l)

        @block.tensor
        def _(pe):
            pe.wait_ge(s["consts"], 16 * len(consts))
            pe.wait_ge(s["pads"], 6)

            def images(ap):
                return ap.rearrange("p (m q) -> p m q", m=2)[:, :, 0:PATCHES]

            def project(w, ps, sem):
                for a in range(2):
                    for c in range(2):
                        K = HALF + c
                        mm = pe.matmul(ps[0:HALF, a * PAIR:(a + 1) * PAIR].rearrange("p (m r) -> p m r", m=2), w[0:K, c, a * HALF:(a + 1) * HALF],
                                       images(b["xs"][0:K, c, :]), start=c == 0, stop=c == 1)
                mm.then_inc(sem, 1)

            def values(c):
                K = HALF + c
                return pe.matmul(p["p3"][:, 0:WIDTH], b["xs"][0:K, c, :], b["wv"][0:K, c, :], start=c == 0, stop=c == 1)

            def scores(ps, left, right, sem):
                for im in range(2):
                    for a in range(2):
                        mm = pe.matmul(ps[64 * im:64 * im + 64, 512 * a:512 * a + NI * PATCHES], left[:, a, PATCHES * im:PATCHES * im + SLOT],
                                       right[:, a, :, PATCHES * im:PATCHES * (im + 1)], start=True, stop=True)
                mm.then_inc(sem, 1)

            def turn_back(T, newest, context):
                pe.wait_ge(s["imm"], 1)
                pe.wait_ge(s["xn"], T)
                pe.wait_ge(s["n2"], newest)
                pe.wait_ge(s["C"], context)
                for c in range(2):
                    mm = pe.transpose(p["p2"][0:HALF, c * PAIR:(c + 1) * PAIR], b["xn"][:, c * HALF:(c + 1) * HALF], keep["ident"][0:PAIR, 0:PAIR])
                mm.then_inc(s["x_ps"], 1)

            def attention(A, B, T, old, q):
                if A is not None:
                    pe.wait_ge(s["xs"], A)
                    pe.wait_ge(s["n2"], A - 1)
                    pe.wait_ge(s["C"], old)
                    pe.wait_ge(s["xT"], old if T is None else A - 3)
                    project(b["wc"], p["p2"], s["c_ps"])
                    pe.wait_ge(s["CT"], old)
                    project(b["wq"], p["p0"], s["q_ps"])
                    pe.wait_ge(s["y"], old)
                    project(b["wk"], p["p1"], s["k_ps"])
                    pe.wait_ge(s["c2"], A)
                    pe.wait_ge(s["c"], A)
                    pe.matmul(p["p2"][0:HALF, 0:2 * PAIR], b["block16"][:], b["c2"][:].rearrange("p c r -> p (c r)"), start=True, stop=True).then_inc(s["n2_ps"], 1)
                    pe.wait_ge(s["V"], A - 1)
                    values(0)
                if T is not None and A is None:
                    turn_back(T, T if B is None else B, T)
                if B is not None:
                    pe.wait_ge(s["imm"], 1)
                    pe.wait_ge(s["P"], B)
                    for im in range(2):
                        rows = slice(64 * im, 64 * im + 64)
                        for i in range(NI):
                            mm = pe.transpose(p["p45"][:, 512 * im + i * SLOT:512 * im + (i + 1) * SLOT], b["P"][rows, i, :, :].rearrange("p a r -> p (a r)"),
                                              keep["ident"][rows, rows])
                    mm.then_inc(s["pt_ps"], 1)
                if A is not None:
                    pe.wait_ge(s["qT"], A)
                    pe.wait_ge(s["kd0"], A)
                    pe.wait_ge(s["kd1"], A)
                    scores(p["p67"], b["qT"], b["kd"], s["s2_ps"])
                if B is not None:
                    pe.wait_ge(s["imm"], 1)
                    pe.wait_ge(s["PT0"], B)
                    pe.wait_ge(s["PT1"], B)
                    pe.wait_ge(s["V"], B)
                    pe.wait_ge(s["n2"], B if A is None else A)
                    if A is None:
                        pe.wait_ge(s["xT"], T)
                    for im in range(2):
                        for i in range(NI):
                            mm = pe.matmul(p["p2"][64 * im:64 * im + 64, i * 32:(i + 1) * 32],
                                           b["PT"][:, im, i, :], b["V"][:, im, i, :, :].rearrange("p a d -> p (a d)"), start=True, stop=True)
                    mm.then_inc(s["ctx_ps"], 1)
                if A is not None:
                    values(1).then_inc(s["v_ps"], 1)
                if B is not None:
                    pe.wait_ge(s["C"], B)
                    pe.wait_ge(s["qT"], B if A is None else A)
                    for a in range(2):
                        mm = pe.transpose(p["p0"][0:HALF, a * 128:(a + 1) * 128], b["C"][:, a, :], keep["ident"][:, :])
                    mm.then_inc(s["ct_ps"], 1)
                if A is not None:
                    pe.wait_ge(s["cT"], A)
                    pe.wait_ge(s["cd"], A)
                    pe.wait_ge(s["PT0"], A - 1)
                    pe.wait_ge(s["PT1"], A - 1)
                    scores(p["p45"], b["cT"], b["cd"], s["s1_ps"])
                    if T is not None:
                        turn_back(T, A, B)
                if B is not None:
                    pe.wait_ge(s["CT"], B)
                    pe.wait_ge(s["kT"], B if A is None else A)
                    for c in range(2):
                        mm = pe.matmul(p["p1"][0:PAIR, 0:WIDTH], b["CT"][:, c, :], b["wo"][:, c, :], start=c == 0, stop=c == 1)
                    mm.then_inc(s["wo_ps"], 1)

            def mlp(A, B, q):
                if A is not None:
                    cols = bass.ds(q * GCOLS, GCOLS)
                    for j in range(NFF):
                        pe.wait_ge(h_sb[j], A - 1)
                        for c in range(2):
                            K = HALF + c
                            mm = pe.matmul(h_bank[j][:, 0:GCOLS], f["wi"][0:K, c, j * 128:(j + 1) * 128], keep["XT"][0:K, c, cols], start=c == 0, stop=c == 1)
                        mm.then_inc(h_ps[j], 1)
                if B is not None:
                    for u in range(2):
                        pe.wait_ge(s["imm"], 1)
                        pe.wait_ge(g["xn"], B)
                        for r in range(2):
                            for c in range(2):
                                at = 512 * u + (2 * r + c) * PAIR
                                mm = pe.transpose(p["p67"][0:HALF, at:at + PAIR], f["xn"][:, 2 * u + r, c * HALF:(c + 1) * HALF],
                                                  keep["ident"][0:PAIR, 0:PAIR])
                        mm.then_inc(x_ps[u], 1)
                if A is not None:
                    n0 = GROUP * (A - 2) + 2
                    for r in range(GROUP):
                        if r < 2:
                            pe.wait_ge(xT[r], A - 1)
                        else:
                            pe.wait_ge(g["y"], n0 + r - 2)
                        for j in range(NFF):
                            if r == 0:
                                pe.wait_ge(h_sb[j], A)
                            mm = pe.matmul(p["p67"][0:PAIR, 512 * (r % 2):512 * (r % 2) + WIDTH], f["h"][:, j, r * PAIR:(r + 1) * PAIR], f["wo2"][:, j, :],
                                           start=j == 0, stop=j == NFF - 1)
                        mm.then_inc(g["out_ps"], 1)

            with pe.Fori(1, LAYERS + 1) as l:
                pe.wait_ge(s["attn_w"], 16 * AW * l)
                for u in range(2):
                    pe.wait_ge(xT[u], GROUPS * (l - 1) + 1)
                attention_steps(pe, l, attention)
                pe.wait_ge(g["ffn_w"], 16 * FW * l)
                pe.wait_ge(s["xT"], TURNS * l + 1)
                mlp_steps(pe, l, mlp)

        @block.vector
        def _(dve):
            dve.memset(b["xs"][:], 0.0).then_inc(s["pads"], 1)
            dve.memset(b["qT"][:, :, PAIR:], 0.0).then_inc(s["pads"], 1)
            dve.memset(b["cT"][:, :, PAIR:], 0.0).then_inc(s["pads"], 1)
            dve.memset(b["P"][:, :, :, PATCHES:], 0.0).then_inc(s["pads"], 1)
            dve.memset(b["PT"][:], 0.0).then_inc(s["pads"], 1)
            dve.memset(b["V"][:], 0.0).then_inc(s["pads"], 1)
            dve.tensor_copy(keep["Y"][:], keep["X"][:]).then_inc(s["saved"], 1)
            dve.wait_ge(s["consts"], 16 * len(consts))
            dve.wait_ge(s["pads"], 6)

            def each(ap):
                return ap.unsqueeze(3).to_broadcast([128, 2, NI, PATCHES])

            def attention(A, B, T, old, q):
                if T is not None:
                    dve.wait_ge(s["y"], T)
                    dve.bn_stats(b["st"][:], b["y"][:]).then_inc(s["st"], 1)
                if B is not None:
                    dve.wait_ge(s["E1x"], B)
                    dve.tensor_reduce(b["z1"][:], b["E1"][:], AX.X, ALU.add).then_inc(s["z1"], 1)
                if T is not None:
                    dve.wait_ge(s["imm"], 1)
                    dve.wait_ge(s["st"], T)
                    dve.bn_aggr(b["mv"][:], b["st"][:]).then_inc(s["mv"], 1)
                if B is not None:
                    dve.wait_ge(s["z1"], B)
                    dve.reciprocal(b["rz1"][:], b["z1"][:]).then_inc(s["rz1"], 1)
                if T is not None:
                    dve.wait_ge(s["mv"], T)
                    dve.tensor_scalar(b["ve"][:], b["mv"][:, 1:2], 1e-12, None, ALU.add).then_inc(s["ve"], 1)
                if B is not None:
                    dve.wait_ge(s["rz1"], B)
                    dve.tensor_tensor(b["E1"][:], b["E1"][:], each(b["rz1"][:]), ALU.mult).then_inc(s["P1"], 1)
                    dve.wait_ge(s["P1"], B)
                    dve.wait_ge(s["P2"], B)
                    dve.tensor_tensor(b["P"][:, :, :, 0:PATCHES].rearrange("p i a r -> p a i r"), b["E1"][:], b["E2"][:], ALU.add).then_inc(s["P"], 1)
                if A is not None:
                    dve.wait_ge(s["kT"], A)
                    dve.wait_ge(s["s2_ps"], A - 1)
                    for a, count in ((0, NI), (1, SPLIT)):
                        ins = dve.tensor_tensor(b["kd"][:, a, 0:count], b["kT"][:, a, :].unsqueeze(1).to_broadcast([HALF, count, PAIR]),
                                                b["own"][:, 0:count].unsqueeze(2).to_broadcast([HALF, count, PAIR]), ALU.mult)
                    ins.then_inc(s["kd0"], 1)
                if T is not None:
                    dve.wait_ge(s["rstd"], T)
                    dve.wait_ge(s["yg"], T - 1)
                    dve.tensor_scalar(b["yn"][:], b["y"][:], b["mv"][:, 0:1], b["rstd"][:], ALU.subtract, ALU.mult).then_inc(s["yn"], 1)
                if A is not None:
                    dve.wait_ge(s["s2_ps"], A)
                    dve.tensor_reduce(b["mx"][:], heads_of(p["p67"][:]), AX.X, ALU.max).then_inc(s["mx"], 1)
                    dve.wait_ge(s["mx"], A)
                    dve.tensor_tensor(b["E2"][:], heads_of(p["p67"][:]), each(b["mx"][:]), ALU.subtract).then_inc(s["shifted"], 1)
                    dve.wait_ge(s["E2"], A)
                    dve.tensor_reduce(b["z2"][:], b["E2"][:], AX.X, ALU.add).then_inc(s["z2"], 1)
                    dve.wait_ge(s["z2"], A)
                    dve.reciprocal(b["rz2"][:], b["z2"][:]).then_inc(s["rz2"], 1)
                    dve.wait_ge(s["rz2"], A)
                    dve.tensor_tensor(b["E2"][:], b["E2"][:], each(b["rz2"][:]), ALU.mult).then_inc(s["P2"], 1)
                if B is not None:
                    dve.wait_ge(s["wo_ps"], B)
                    dve.wait_ge(s["hb"], B)
                    dve.tensor_tensor(b["y"][:], p["p1"][0:PAIR, 0:WIDTH], b["hb"][:], ALU.add).then_inc(s["y"], 1)

            def mlp(A, B, q):
                if A is None:
                    return
                n0 = GROUP * (A - 2) + 2
                dve.wait_ge(g["hb"], A)
                for r in range(GROUP):
                    dve.wait_ge(g["out_ps"], n0 + r)
                    dve.tensor_tensor(f["y"][:, r], p["p67"][0:PAIR, 512 * (r % 2):512 * (r % 2) + WIDTH], f["hb"][:, r], ALU.add).then_inc(g["y"], 1)
                    dve.wait_ge(g["y"], n0 + r)
                    dve.bn_stats(f["st"][:, r], f["y"][:, r]).then_inc(g["st"], 1)
                for r in range(GROUP):
                    dve.wait_ge(s["imm"], 1)
                    dve.wait_ge(g["st"], n0 + r)
                    dve.bn_aggr(f["mv"][:, r], f["st"][:, r]).then_inc(g["mv"], 1)
                dve.wait_ge(g["mv"], n0 + GROUP - 1)
                dve.tensor_scalar(f["ve"][:], f["mv"][:, :, 1], 1e-12, None, ALU.add).then_inc(g["ve"], 1)
                dve.wait_ge(g["rstd"], A)
                dve.wait_ge(g["yg"], A - 1)
                for r in range(GROUP):
                    dve.tensor_scalar(f["yn"][:, r], f["y"][:, r], f["mv"][:, r, 0:1], f["rstd"][:, r:r + 1], ALU.subtract, ALU.mult).then_inc(g["yn"], 1)

            with dve.Fori(1, LAYERS + 1) as l:
                attention_steps(dve, l, attention)
                mlp_steps(dve, l, mlp)

        @block.scalar
        def _(act):
            act.wait_ge(s["pads"], 6)
            act.wait_ge(s["saved"], 1)

            def normed(T, q):
                act.wait_ge(s["imm"], 1)
                act.wait_ge(s["x_ps"], T)
                act.activation(keep["XT"][0:HALF, :, bass.ds((q - 2) * PAIR, PAIR)], p["p2"][0:HALF, 0:2 * PAIR].rearrange("p (c r) -> p c r", c=2),
                               ACT.Copy).then_inc(s["xT"], 1)
                act.activation(keep["X"][:, bass.ds(q - 2, 1), :], b["xn"][:].unsqueeze(1), ACT.Copy).then_inc(s["X"], 1)

            def columns(n, q):
                act.wait_ge(s["v_ps"], n - 1)
                act.activation(b["xs"][:].rearrange("p c (m q) -> p c m q", m=2)[:, :, :, 0:PATCHES],
                               keep["XT"][:, :, bass.ds(q * PAIR, PAIR)].rearrange("p c (m r) -> p c m r", m=2), ACT.Copy).then_inc(s["xs"], 1)

            def attention(A, B, T, old, q):
                if A is not None:
                    if B is None:
                        columns(A, q)
                    act.wait_ge(s["c_ps"], A)
                    act.wait_ge(s["n2_ps"], A - 1)
                    act.wait_ge(s["cT"], A - 1)
                    act.activation(b["c2"][:].rearrange("p a r -> p (a r)"), p["p2"][0:HALF, 0:2 * PAIR], ACT.Square).then_inc(s["c2"], 1)
                    act.activation(b["c"][:].rearrange("p a r -> p (a r)"), p["p2"][0:HALF, 0:2 * PAIR], ACT.Copy).then_inc(s["c"], 1)
                    act.wait_ge(s["q_ps"], A)
                    act.wait_ge(s["s2_ps"], A - 1)
                    act.activation(b["qT"][:, :, 0:PAIR], p["p0"][0:HALF, 0:2 * PAIR].rearrange("p (a r) -> p a r", a=2), ACT.Copy, scale=0.25).then_inc(s["qT"], 1)
                    act.wait_ge(s["k_ps"], A)
                    act.activation(b["kT"][:].rearrange("p a r -> p (a r)"), p["p1"][0:HALF, 0:2 * PAIR], ACT.Copy).then_inc(s["kT"], 1)
                    act.wait_ge(s["n2_ps"], A)
                    act.activation(b["n2"][:], p["p2"][0:HALF, 0:2 * PAIR], ACT.Ln).then_inc(s["n2"], 1)
                    act.wait_ge(s["n2"], A)
                    act.activation(b["rn"][:], b["n2"][:], ACT.Exp, scale=-0.5).then_inc(s["rn"], 1)
                    act.wait_ge(s["kT"], A)
                    for i in range(SPLIT, NI):
                        ins = act.activation(b["kd"][:, 1, i], b["kT"][:, 1, :], ACT.Copy, scale=b["own"][:, i:i + 1])
                    ins.then_inc(s["kd1"], 1)
                if T is not None and A is None:
                    normed(T, q)
                if B is not None:
                    act.wait_ge(s["pt_ps"], B)
                    for im, sem in ((0, s["PT0"]), (1, s["PT1"])):
                        act.activation(b["PT"][:, im], p["p45"][:, 512 * im:512 * im + NI * SLOT].rearrange("p (i r) -> p i r", i=NI), ACT.Copy).then_inc(sem, 1)
                    act.wait_ge(s["ctx_ps"], B)
                    act.activation(b["C"][:].rearrange("p a (i d) -> p i a d", i=NI),
                                   p["p2"][:, 0:2 * HALF].rearrange("p (i a d) -> p i a d", i=NI, a=2), ACT.Copy).then_inc(s["C"], 1)
                if A is not None:
                    act.wait_ge(s["shifted"], A)
                    act.activation(b["E2"][:], b["E2"][:], ACT.Exp).then_inc(s["E2"], 1)
                if B is not None:
                    act.wait_ge(s["ct_ps"], B)
                    act.activation(packed(b["CT"][:]), slots(p["p0"][0:HALF, 0:256], 2), ACT.Copy).then_inc(s["CT"], 1)
                if A is not None:
                    act.wait_ge(s["s1_ps"], A)
                    act.wait_ge(s["P"], A - 1)
                    act.activation(b["E1"][:], heads_of(p["p45"][:]), ACT.Exp, bias=1.0, scale=-1.0).then_inc(s["E1"], 1)
                    if not (isinstance(q, int) and q == TURNS - 1):
                        columns(A + 1, q + 1)
                if T is not None and A is not None:
                    normed(T, q)
                if A is not None:
                    act.wait_ge(s["v_ps"], A)
                    act.wait_ge(s["ctx_ps"], A - 1)
                    for a in range(2):
                        for im in range(2):
                            ins = act.activation(b["V"][64 * a:64 * a + 64, im, :, a, :],
                                                 p["p3"][64 * im:64 * im + 64, a * HALF:(a + 1) * HALF].rearrange("p (i d) -> p i d", i=NI),
                                                 ACT.Copy, scale=0.5)
                    ins.then_inc(s["V"], 1)

            def mlp(A, B, q):
                if A is not None:
                    act.wait_ge(g["out_ps"], GROUP * (A - 2) + 1)
                    for j in range(NFF):
                        act.wait_ge(h_ps[j], A)
                        act.activation(f["h"][:, j, :], h_bank[j][:, 0:GCOLS], ACT.Gelu).then_inc(h_sb[j], 1)
                if B is not None:
                    for u in range(2):
                        act.wait_ge(s["imm"], 1)
                        act.wait_ge(x_ps[u], B)
                        act.activation(keep["XT"][0:HALF, :, bass.ds((q - 1) * GCOLS + 2 * u * PAIR, 2 * PAIR)].rearrange("p c (t r) -> p t c r", t=2),
                                       p["p67"][0:HALF, 512 * u:512 * u + 4 * PAIR].rearrange("p (t c r) -> p t c r", t=2, c=2),
                                       ACT.Copy).then_inc(xT[u], 1)
                    act.activation(keep["X"][:, bass.ds((q - 1) * GROUP, GROUP), :], f["xn"][:], ACT.Copy).then_inc(g["X"], 1)

            with act.Fori(1, LAYERS + 1) as l:
                act.preload_act_table_set("natural_log_exp_and_others")
                for u in range(2):
                    act.wait_ge(xT[u], GROUPS * (l - 1) + 1)
                attention_steps(act, l, attention)
                mlp_steps(act, l, mlp)

        @block.gpsimd
        def _(pool):
            pool.sem_inc(s["imm"], 1)
            pool.wait_ge(s["consts"], 16 * len(consts))
            pool.wait_ge(s["pads"], 6)

            def attention(A, B, T, old, q):
                if B is not None:
                    pool.wait_ge(s["E1"], B)
                    E1 = b["E1"][:].rearrange("p a i r -> p (a i) r")
                    pool.tensor_tensor(E1, E1, b["eye"][:].unsqueeze(1).to_broadcast([128, HEADS, PATCHES]), ALU.mult).then_inc(s["E1x"], 1)
                if T is not None:
                    pool_rstd(pool, b, s, T, keep)
                if A is not None:
                    pool.wait_ge(s["rn"], A)
                    pool.wait_ge(s["c"], A)
                    pool.wait_ge(s["s1_ps"], A - 1)
                    pool.tensor_tensor(b["cT"][:, :, 0:PAIR], b["c"][:], b["rn"][:].rearrange("p (a r) -> p a r", a=2), ALU.mult).then_inc(s["cT"], 1)
                    pool.wait_ge(s["cT"], A)
                    for a in range(2):
                        ins = pool.tensor_tensor(b["cd"][:, a], b["cT"][:, a, 0:PAIR].unsqueeze(1).to_broadcast([HALF, NI, PAIR]),
                                                 b["own"][:].unsqueeze(2).to_broadcast([HALF, NI, PAIR]), ALU.mult)
                    ins.then_inc(s["cd"], 1)
                if T is not None:
                    pool.wait_ge(s["yn"], T)
                    pool.tensor_tensor(b["yg"][:], b["yn"][:], b["rows"][:, 1, :], ALU.mult).then_inc(s["yg"], 1)
                    pool.wait_ge(s["yg"], T)
                    pool.wait_ge(s["x_ps"], T - 1)
                    pool.wait_ge(s["X"], T - 1)
                    pool.tensor_tensor(b["xn"][:], b["yg"][:], b["rows"][:, 2, :], ALU.add).then_inc(s["xn"], 1)
                if B is not None:
                    pool.wait_ge(s["y"], B - 1)
                    pool.tensor_tensor(b["hb"][:], keep["X"][:, bass.ds(q - 1, 1), :].rearrange("p o w -> p (o w)"), b["rows"][:, 0, :], ALU.add).then_inc(s["hb"], 1)

            def mlp(A, B, q):
                if A is None:
                    return
                def row(k):
                    return b["rows"][:, k, :].unsqueeze(1).to_broadcast([PAIR, GROUP, WIDTH])

                pool.wait_ge(g["y"], GROUP * (A - 2) + 1)
                pool.tensor_tensor(f["hb"][:], keep["X"][:, bass.ds(GROUP * q, GROUP), :], row(3), ALU.add).then_inc(g["hb"], 1)
                pool.wait_ge(g["ve"], A)
                pool.tensor_tensor(f["rstd"][:], f["ve"][:], keep["half"][:].to_broadcast([PAIR, GROUP]), ALU.pow).then_inc(g["rstd"], 1)
                pool.wait_ge(g["yn"], GROUP * (A - 1) + 1)
                pool.tensor_tensor(f["yg"][:], f["yn"][:], row(4), ALU.mult).then_inc(g["yg"], 1)
                pool.wait_ge(g["yg"], A)
                for u in range(2):
                    pool.wait_ge(x_ps[u], A - 1)
                pool.wait_ge(g["X"], A - 1)
                pool.tensor_tensor(f["xn"][:], f["yg"][:], row(5), ALU.add).then_inc(g["xn"], 1)

            with pool.Fori(1, LAYERS + 1) as l:
                pool.wait_ge(s["attn_w"], 16 * AW * l)
                pool.wait_ge(g["X"], GROUPS * (l - 1) + 1)
                attention_steps(pool, l, attention)
                pool.wait_ge(s["X"], TURNS * l + 1)
                mlp_steps(pool, l, mlp)


def block_mixture(nc, d, keep):
    NE = 8
    with ExitStack() as ctx:
        b = buffers(ctx, nc, "mx", wg=(HALF + 1, 2, NE), xs=(HALF + 1, 2, GROUP, PAIR), order=(PAIR, NE), lg=(PAIR, TURNS, NE),
                    m1=(PAIR, TURNS), m2=(PAIR, TURNS), first=(PAIR, TURNS), second=(PAIR, TURNS), e1=(PAIR, TURNS, NE), e2=(PAIR, TURNS, NE),
                    o1=(PAIR, TURNS, NE), o2=(PAIR, TURNS, NE), left=(PAIR, TURNS, NE), ex=(PAIR, TURNS, NE), em=(PAIR, TURNS, NE),
                    sm=(PAIR, TURNS), rs=(PAIR, TURNS), gates=(PAIR, TURNS, NE),
                    w1=(HALF + 1, 2, 2, FFN), w2=(128, 2, NFF, WIDTH), b2=(PAIR, 2, WIDTH), h=(128, NFF, GCOLS), ob=(PAIR, GROUP, WIDTH),
                    y=(PAIR, GROUP, WIDTH), st=(PAIR, GROUP, 6), mv=(PAIR, GROUP, 2), ve=(PAIR, GROUP), rstd=(PAIR, GROUP),
                    xn=(PAIR, GROUP, WIDTH))
        p = banks(ctx, nc, "mx", hp=3072, out0=512, out1=512)
        s = signals(ctx, nc, "mx", "m1 e1 first o1 left m2 e2 second o2 mask shifted ex em sm rs h0 h1 h2 h3 h4 h5 a0 a1 a2 a3 a4 a5 "
                                   "out_ps ob Y", setup="imm wg w0 w1 ones gates")
        g = signals(ctx, nc, "rn", "y st mv ve rstd xn x_ps0 x_ps1 xs xT Y lg_ps lg")
        f = signals(ctx, nc, "fn", "y st mv ve rstd xn", dma="stored")
        g["imm"] = f["imm"] = s["imm"]
        h_ps, h_sb, w = (s["h0"], s["h1"], s["h2"], s["h3"], s["h4"], s["h5"]), (s["a0"], s["a1"], s["a2"], s["a3"], s["a4"], s["a5"]), (s["w0"], s["w1"])
        h_bank = [p["hp"][:, 512 * j:512 * j + GCOLS] for j in range(NFF)]
        outs, x_ps = (p["out0"], p["out1"]), (g["x_ps0"], g["x_ps1"])
        out_rows = d["out"].rearrange("(g t p) w -> g p t w", t=GROUP, p=PAIR)
        block = ctx.enter_context(nc.Block())

        def load(sp, e, u):
            for to, src in ((b["w1"], d["w1"]), (b["w2"], d["w2"]), (b["b2"], d["b2e"])):
                sp.dma_start(to[:, u], src[e]).then_inc(w[u], 16)

        @block.sync
        def _(sp):
            sp.dma_start(b["wg"][:], d["gwg"]).then_inc(s["wg"], 16)
            sp.dma_start(b["order"][:], d["order"]).then_inc(s["wg"], 16)
            for u in range(2):
                load(sp, u, u)
            with sp.Fori(1, NE // 2) as i:
                for u in range(2):
                    sp.wait_ge(s["imm"], 1)
                    sp.wait_ge(s["Y"], TURNS * (2 * i + u - 1) + 1)
                    load(sp, 2 * i + u, u)
            with sp.Fori(2, GROUPS + 2) as n:
                sp.wait_ge(s["imm"], 1)
                sp.wait_ge(f["xn"], GROUP * (n - 1) + 1)
                sp.dma_start(out_rows[n - 2], b["xn"][:]).then_inc(f["stored"], 16)
            sp.wait_ge(f["stored"], 16 * (GROUPS + 1))

        @block.tensor
        def _(pe):
            pe.wait_ge(s["wg"], 32)
            pe.wait_ge(s["ones"], 1)
            with pe.Fori(2, GROUPS + 2) as n:
                for u in range(2):
                    pe.wait_ge(s["imm"], 1)
                    pe.wait_ge(g["xn"], GROUP * (n - 1) + 1)
                    pe.wait_ge(g["xs"], n - 1)
                    for r in range(2):
                        for c in range(2):
                            at = (2 * r + c) * PAIR
                            mm = pe.transpose(h_bank[u][0:HALF, at:at + PAIR], b["xn"][:, 2 * u + r, c * HALF:(c + 1) * HALF],
                                              keep["ident"][0:PAIR, 0:PAIR])
                    mm.then_inc(x_ps[u], 1)
                pe.wait_ge(g["xs"], n)
                pe.wait_ge(g["lg"], n - 1)
                for r in range(GROUP):
                    for c in range(2):
                        K = HALF + c
                        mm = pe.matmul(p["out0"][0:PAIR, r * NE:(r + 1) * NE], b["xs"][0:K, c, r, :], b["wg"][0:K, c, :], start=c == 0, stop=c == 1)
                mm.then_inc(g["lg_ps"], 1)
            pe.wait_ge(g["lg"], GROUPS + 1)
            pe.wait_ge(g["xT"], GROUPS + 1)
            with pe.Fori(1, NE // 2 + 1) as i:
                for u in range(2):
                    with pe.Fori(1, GROUPS + 1) as q:
                        pe.wait_ge(w[u], 48 * i)
                        n = GROUPS * (2 * (i - 1) + u) + q + 1
                        n0 = GROUP * (n - 2) + 2
                        cols = bass.ds((q - 1) * GCOLS, GCOLS)
                        for j in range(NFF):
                            pe.wait_ge(h_sb[j], n - 1)
                            for c in range(2):
                                K = HALF + c
                                mm = pe.matmul(h_bank[j], b["w1"][0:K, u, c, j * 128:(j + 1) * 128], keep["XT"][0:K, c, cols], start=c == 0, stop=c == 1)
                            mm.then_inc(h_ps[j], 1)
                        for r in range(GROUP):
                            pe.wait_ge(s["ob"], n0 + max(r - 2, -1))
                            for j in range(NFF):
                                if r == 0:
                                    pe.wait_ge(h_sb[j], n)
                                mm = pe.matmul(outs[r % 2][0:PAIR, 0:WIDTH], b["h"][:, j, r * PAIR:(r + 1) * PAIR], b["w2"][:, u, j, :],
                                               start=j == 0, stop=j == NFF - 1)
                            mm.then_inc(s["out_ps"], 1)

        @block.scalar
        def _(act):
            act.activation(b["xs"][HALF:HALF + 1, :, :, :].rearrange("p c t r -> p c (t r)"), keep["XT"][HALF:HALF + 1, :, 0:GCOLS], ACT.Copy).then_inc(s["ones"], 1)
            with act.Fori(2, GROUPS + 2) as n:
                for u in range(2):
                    act.wait_ge(x_ps[u], n)
                    act.wait_ge(g["lg_ps"], n - 1)
                    act.wait_ge(g["xT"], n - 1)
                    ins = act.activation(b["xs"][0:HALF, :, 2 * u:2 * u + 2, :].rearrange("p c t r -> p t c r"),
                                         h_bank[u][0:HALF, :].rearrange("p (t c r) -> p t c r", t=2, c=2), ACT.Copy)
                ins.then_inc(g["xs"], 1)
                act.activation(keep["Y"][:, bass.ds((n - 2) * GROUP, GROUP), :], b["xn"][:], ACT.Copy).then_inc(g["Y"], 1)
                act.wait_ge(g["lg_ps"], n)
                act.activation(b["lg"][:, bass.ds((n - 2) * GROUP, GROUP), :], p["out0"][0:PAIR, 0:GROUP * NE].rearrange("p (t e) -> p t e", t=GROUP),
                               ACT.Copy).then_inc(g["lg"], 1)
                act.activation(keep["XT"][0:HALF, :, bass.ds((n - 2) * GCOLS, GCOLS)], b["xs"][0:HALF, :, :, :].rearrange("p c t r -> p c (t r)"),
                               ACT.Copy).then_inc(g["xT"], 1)
            act.wait_ge(s["shifted"], 2)
            act.activation(b["ex"][:], b["ex"][:], ACT.Exp).then_inc(s["ex"], 1)
            with act.Fori(2, NE * GROUPS + 2) as n:
                act.wait_ge(s["out_ps"], GROUP * (n - 2) + 1)
                for j in range(NFF):
                    act.wait_ge(h_ps[j], n)
                    act.activation(b["h"][:, j, :], h_bank[j], ACT.Relu).then_inc(h_sb[j], 1)

        @block.vector
        def _(dve):
            dve.wait_ge(s["wg"], 32)
            with dve.Fori(2, GROUPS + 2) as n:
                at = bass.ds((n - 2) * GROUP, GROUP)
                dve.wait_ge(g["xn"], GROUP * (n - 2) + 1)
                dve.tensor_tensor(b["y"][:], keep["X"][:, at, :], keep["Y"][:, at, :], ALU.add).then_inc(g["y"], 1)
                norm_group(dve, b, g, n, 1e-5, b["xn"], g["xn"], ((g["x_ps0"], n - 1), (g["x_ps1"], n - 1), (g["Y"], n - 1)))
            dve.wait_ge(g["lg"], GROUPS + 1)

            def each(ap):
                return ap.unsqueeze(2).to_broadcast([PAIR, TURNS, NE])

            order = b["order"][:].unsqueeze(1).to_broadcast([PAIR, TURNS, NE])
            for values, best, equal, place, chosen, sems in (
                    (b["lg"], b["m1"], b["e1"], b["first"], b["o1"], (s["m1"], s["e1"], s["first"], s["o1"])),
                    (b["left"], b["m2"], b["e2"], b["second"], b["o2"], (s["m2"], s["e2"], s["second"], s["o2"]))):
                dve.tensor_reduce(best[:], values[:], AX.X, ALU.max).then_inc(sems[0], 1)
                dve.wait_ge(sems[0], 2)
                dve.tensor_tensor(equal[:], values[:], each(best[:]), ALU.is_equal).then_inc(sems[1], 1)
                dve.wait_ge(sems[1], 2)
                dve.tensor_tensor(equal[:], equal[:], order, ALU.mult).then_inc(sems[1], 1)
                dve.wait_ge(sems[1], 3)
                dve.tensor_reduce(place[:], equal[:], AX.X, ALU.max).then_inc(sems[2], 1)
                dve.wait_ge(sems[2], 2)
                dve.tensor_tensor(chosen[:], equal[:], each(place[:]), ALU.is_equal).then_inc(sems[3], 1)
                dve.wait_ge(sems[3], 2)
                if values is b["lg"]:
                    dve.tensor_tensor(b["ex"][:], b["lg"][:], each(b["m1"][:]), ALU.subtract).then_inc(s["shifted"], 1)
                    dve.scalar_tensor_tensor(b["left"][:], b["o1"][:], -BIG, b["lg"][:], ALU.mult, ALU.add).then_inc(s["left"], 1)
                    dve.wait_ge(s["left"], 2)
            dve.tensor_tensor(b["o1"][:], b["o1"][:], b["o2"][:], ALU.add).then_inc(s["mask"], 1)
            dve.wait_ge(s["mask"], 2)
            dve.wait_ge(s["ex"], 2)
            dve.tensor_tensor(b["em"][:], b["ex"][:], b["o1"][:], ALU.mult).then_inc(s["em"], 1)
            dve.wait_ge(s["em"], 2)
            dve.tensor_reduce(b["sm"][:], b["em"][:], AX.X, ALU.add).then_inc(s["sm"], 1)
            dve.wait_ge(s["sm"], 2)
            dve.reciprocal(b["rs"][:], b["sm"][:]).then_inc(s["rs"], 1)
            dve.wait_ge(s["rs"], 2)
            dve.tensor_tensor(b["gates"][:], b["em"][:], each(b["rs"][:]), ALU.mult).then_inc(s["gates"], 1)
            dve.wait_ge(s["gates"], 1)
            dve.wait_ge(g["Y"], GROUPS + 1)

            def add_expert(i, u, q):
                dve.wait_ge(w[u], 48 * i)
                e = 2 * (i - 1) + u
                n0 = GROUP * (GROUPS * e + q - 1) + 2
                for r in range(GROUP):
                    turn = GROUP * (q - 1) + r
                    dve.wait_ge(s["out_ps"], n0 + r)
                    dve.tensor_tensor(b["ob"][:, r], outs[r % 2][0:PAIR, 0:WIDTH], b["b2"][:, u], ALU.add).then_inc(s["ob"], 1)
                    dve.wait_ge(s["ob"], n0 + r)
                    row = keep["Y"][:, bass.ds(turn, 1), :].rearrange("p o w -> p (o w)")
                    gate = b["gates"][:].rearrange("p t e -> p (t e)")[:, bass.ds(NE * turn + e, 1)]
                    dve.scalar_tensor_tensor(row, b["ob"][:, r], gate, row, ALU.mult, ALU.add).then_inc(s["Y"], 1)

            with dve.Fori(1, NE // 2) as i:
                for u in range(2):
                    with dve.Fori(1, GROUPS + 1) as q:
                        add_expert(i, u, q)
            with dve.Fori(1, GROUPS + 1) as q:
                add_expert(NE // 2, 0, q)
            with dve.Fori(1, GROUPS + 1) as q:
                add_expert(NE // 2, 1, q)
                norm_group(dve, b, f, q + 1, 1e-5, b["xn"], f["xn"], ((f["stored"], 16 * q),))

        @block.gpsimd
        def _(pool):
            pool.sem_inc(s["imm"], 1)
            with pool.Fori(2, GROUPS + 2) as n:
                pool_rstd_group(pool, b, g, n, keep)
            with pool.Fori(2, GROUPS + 2) as n:
                pool.wait_ge(f["xn"], GROUP * (n - 2) + 1)
                pool.wait_ge(s["Y"], TURNS * (NE - 1) + GROUP * (n - 1) + 1)
                pool.tensor_copy(b["y"][:], keep["Y"][:, bass.ds((n - 2) * GROUP, GROUP), :]).then_inc(f["y"], 1)
                pool_rstd_group(pool, b, f, n, keep)


def storage(nc, ctx, d):
    keep = buffers(ctx, nc, "keep", X=(PAIR, TURNS, WIDTH), XT=(HALF + 1, 2, TOKENS), Y=(PAIR, TURNS, WIDTH), w6=(PAIR, TURNS, TOPK),
                   ident=(128, 128), half=(PAIR, 1))
    keep["rows"] = ctx.enter_context(nc.sbuf_tensor("keep_rows", [PAIR, TURNS, 8], I32))
    d["x_rows"] = nc.dram_tensor("x_rows", (TURNS, PAIR, WIDTH), F32).ap()
    d["x_flat"] = d["x_rows"].rearrange("t p w -> (t p) w")
    d["slot_token"] = nc.dram_tensor("slot_token", (CAPH, 2 * EXPERTS), I32).ap()
    d["slot_token_rows"] = d["slot_token"].rearrange("p (e o) -> (p e) o", o=1)
    d["slot_out"] = nc.dram_tensor("slot_out", (CAPH, 2 * EXPERTS, WIDTH), F32).ap()
    d["slot_out_rows"] = d["slot_out"].rearrange("p e w -> (p e) w")
    return keep, d


def program(nc, d, out):
    d = dict(d, out=out)
    with ExitStack() as ctx:
        keep, d = storage(nc, ctx, d)
        block_embed_and_latent_attention(nc, d, keep)
        block_router_and_shared_expert(nc, d, keep)
        block_routed_experts(nc, d, keep)
        block_combine(nc, d, keep)
        block_bert(nc, d, keep)
        block_mixture(nc, d, keep)


def rope_tables():
    inv = (1.0 / 10000.0 ** (np.arange(0, HD0, 2, dtype=np.float32) / HD0)).astype(np.float32)
    ang = np.arange(PATCHES, dtype=np.float32)[:, None] * inv[None, :]
    ang = np.concatenate([ang, ang], axis=-1).T
    sign = np.where(np.arange(HD0) < HD0 // 2, -1.0, 1.0).astype(np.float32)[:, None]
    return np.tile(np.cos(ang), (2, 2)), np.tile(np.sin(ang) * sign, (2, 2))


def position_table():
    j = np.arange(WIDTH)
    expo = (2 * (j // 2)).astype(np.float32) / np.float32(WIDTH)
    angle = np.arange(PATCHES, dtype=np.float32)[:, None] / np.power(np.float32(10000.0), expo)
    angle = angle + np.where(j % 2 == 1, np.float32(np.pi / 2), np.float32(0.0)).astype(np.float32)
    return np.tile(np.sin(angle.astype(np.float32)), (2, 1))


def constants():
    cos, sin = rope_tables()
    row, col = np.arange(128)[:, None] % SLOT, np.arange(PATCHES)[None, :]
    e = np.arange(EXPERTS)
    token = np.arange(PAIR)[:, None] + PAIR * np.arange(TURNS)[None, :]
    return {
        "cos": cos, "sin": sin, "pos": position_table(),
        "mask": np.where((row >= PATCHES) | (col <= row), 0.0, -BIG),
        "eye": np.where(row == col, np.e, 1.0), "ident": np.eye(128), "half": np.full((PAIR, 1), -0.5),
        "before": np.triu(np.ones((PAIR, PAIR)), 1), "ones": np.ones((PAIR, PAIR)),
        "slot0": np.tile(2.0 * e, (PAIR, 1)), "token": token.astype(np.uint32),
        "order": np.tile(np.arange(8.0, 0.0, -1.0), (PAIR, 1)),
        "own": np.where(np.arange(HALF)[:, None] // 16 == np.arange(NI)[None, :], 1.0, 0.0),
        "block16": np.where(np.arange(HALF)[:, None] // 16 == np.arange(HALF)[None, :] // 16, 1.0, 0.0),
    }


def chunks(w, ones=None):
    out = w.reshape(2, HALF, -1).transpose(1, 0, 2)
    if ones is None:
        return out
    row = np.stack([np.zeros_like(ones), ones])[None]
    return np.concatenate([out, row], axis=0)


def rows_of(v):
    return np.broadcast_to(v, (PAIR, v.shape[-1]))


def layout(i):
    px = i["x"][:, :, 0:112, 0:112].reshape(TURNS, 2, 3, 7, 16, 7, 16)
    px = px.transpose(0, 2, 4, 6, 1, 3, 5).reshape(TURNS, 6, 128, PAIR).transpose(0, 2, 1, 3)
    wq, wup = i["L0_attn_Wq"], i["L0_attn_Wup"]
    turn = (np.arange(HD0) + HD0 // 2) % HD0
    swap = (np.arange(HEADS)[:, None] * HD0 + turn[None, :]).reshape(-1)
    wk = wup[:, 0:768]
    a = {
        "xp": px, "wtok": i["L0_tok_W"].reshape(WIDTH, 6, 128).transpose(2, 1, 0), "tok_b": rows_of(i["L0_tok_b"]),
        "bo0": rows_of(i["L0_attn_bo"]), "wdown": chunks(i["L0_attn_Wdown"]), "wq0": chunks(wq), "wq0r": chunks(wq[:, swap]),
        "wk0": wk, "wk0r": wk[:, swap], "wv0": wup[:, 768:].reshape(64, NI, 2, HD0).transpose(0, 2, 1, 3).reshape(64, 768),
        "wo0": i["L0_attn_Wo"].reshape(6, 128, WIDTH).transpose(1, 0, 2),
        "ln_g": i["L0_attn_ln_g"].reshape(64, 1), "ln_b": i["L0_attn_ln_b"].reshape(64, 1),
        "wg": chunks(i["L0_ffn_Wg"].T), "e_bias": rows_of(i["L0_ffn_e_bias"]),
        "wgu": i["L0_ffn_W_gate_up"].reshape(EXPERTS, 2, HALF, 2 * INTER).transpose(0, 2, 1, 3),
        "wdn": i["L0_ffn_W_down"].reshape(EXPERTS, NF, FC, WIDTH).transpose(0, 2, 1, 3),
        "wsg": chunks(i["L0_ffn_Wsg"]), "wsu": chunks(i["L0_ffn_Wsu"]),
        "wsd": i["L0_ffn_Wsd"].reshape(8, FC, WIDTH).transpose(1, 0, 2),
    }
    for n in "qkvc":
        w, bias = i[f"L1_attn_W{n}"], i[f"L1_attn_b{n}"]
        a[f"bw{n}"] = np.stack([chunks(w[l], bias[l]) for l in range(LAYERS)])
    a["bwo"] = np.stack([chunks(i["L1_attn_Wo"][l]) for l in range(LAYERS)])
    a["bwi"] = np.stack([chunks(i["L1_attn_Wi"][l], i["L1_attn_bi"][l]) for l in range(LAYERS)])
    a["bwo2"] = i["L1_attn_Wo2"].reshape(LAYERS, NFF, 128, WIDTH).transpose(0, 2, 1, 3)
    rows = [i[f"L1_attn_{n}"] for n in ("bo", "g1", "b1", "bo2", "g2", "b2")]
    a["brows"] = np.broadcast_to(np.stack(rows, axis=1)[:, None], (LAYERS, PAIR, 6, WIDTH))
    a["gwg"] = chunks(i["L1_ffn_Wg"], i["L1_ffn_bg"])
    a["w1"] = np.stack([chunks(i["L1_ffn_W1"][e], i["L1_ffn_b1"][e]) for e in range(8)])
    a["w2"] = i["L1_ffn_W2"].reshape(8, NFF, 128, WIDTH).transpose(0, 2, 1, 3)
    a["b2e"] = np.broadcast_to(i["L1_ffn_b2"][:, None], (8, PAIR, WIDTH))
    return a


def kernel(**inputs):
    import concourse.bacc as bacc
    from concourse.bass_utils import run_bass_kernel_spmd

    arrays = {n: np.ascontiguousarray(a) for n, a in layout({k: np.asarray(v) for k, v in inputs.items()}).items()}
    arrays |= {n: np.ascontiguousarray(a if a.dtype == np.uint32 else a.astype(np.float32)) for n, a in constants().items()}
    nc = bacc.Bacc("TRN2", target_bir_lowering=False, num_devices=1)
    d = {n: nc.dram_tensor(n, a.shape, mybir.dt.from_np(a.dtype), kind="ExternalInput").ap() for n, a in arrays.items()}
    out = nc.dram_tensor("out", (TOKENS, WIDTH), F32, kind="ExternalOutput").ap()
    program(nc, d, out)
    r = run_bass_kernel_spmd(nc, [arrays], core_ids=[0])
    return r.results[0]["out"].reshape(IMAGES, PATCHES, WIDTH)
```
